# Optimizing a Trainium2 kernel written in Bass

```python
import numpy as np
import jax
import jax.numpy as jnp

def _softmax(x, axis=-1):
    return jax.nn.softmax(x, axis=axis)

def _gelu(x):
    return jax.nn.gelu(x, approximate=True)

def _silu(x):
    return jax.nn.silu(x)

def _sigmoid(x):
    return jax.nn.sigmoid(x)

def _layernorm(x, axis=-1, eps=1e-05):
    m = jnp.mean(x, axis=axis, keepdims=True)
    v = jnp.var(x, axis=axis, keepdims=True)
    return (x - m) / jnp.sqrt(v + eps)

def _scatter_add(tgt, idx, src, axis=0):
    return tgt.at[idx].add(src)

def _segment_sum(src, seg, n):
    return jax.ops.segment_sum(src, seg, n)
kernel_name = 'mk_decoder_preln_d1_seqx_r4_391daa'

def setup_inputs(seed: int=0):
    np.random.seed(seed)
    _w = jnp.asarray

    def _rec_inputs():
        import jax
        import jax.numpy as jnp
        _rk = jax.random.key(seed)
        x = -0.0002928 + 1 * jax.random.normal(jax.random.fold_in(_rk, 1), (8, 256, 512), jnp.float32)
        _lenS = 256 - jax.random.randint(jax.random.fold_in(_rk, 7), (8,), 0, max(1, 256 // 4) + 1, jnp.int32)
        _lenS2 = 256 - jax.random.randint(jax.random.fold_in(_rk, 8), (8,), 0, max(1, 256 // 4) + 1, jnp.int32)
        fside_S2_0 = -0.00337071 + 1.01897 * jax.random.normal(jax.random.fold_in(_rk, 11), (256,), jnp.float32)
        _ctx_2048P = jax.random.normal(jax.random.fold_in(_rk, 12), (8, 16, 512), jnp.float32)
        _ctx_2048c = jax.random.dirichlet(jax.random.fold_in(_rk, 512), 0.3 * jnp.ones((16,), jnp.float32), (8, 256))
        _ctx_2048t = jnp.einsum('bsk,bkd->bsd', _ctx_2048c, _ctx_2048P)
        _ctx_2048t = _ctx_2048t * jax.lax.rsqrt(jnp.mean(jnp.square(_ctx_2048t)) + 1e-12) * 0.953939
        ctx_2048 = 0.000675642 + 1.00031 * (_ctx_2048t + 0.3 * jax.random.normal(jax.random.fold_in(_rk, 612), (8, 256, 512), jnp.float32))
        return (x, fside_S2_0, ctx_2048)
    x, fside_S2_0, ctx_2048 = _rec_inputs()

    def _L0_attn_setup():
        import jax, jax.numpy as jnp
        import numpy as np
        D_MODEL = 512
        NUM_HEADS = 16
        HEAD_DIM = D_MODEL // NUM_HEADS
        D_C = 128
        D_ROT = 64
        B, S = (4, 512)

        def _apply_rotary(c_rot, seq_len):
            half = D_ROT // 2
            inv_freq = 1.0 / 10000.0 ** (jnp.arange(0, D_ROT, 2, dtype=jnp.float32) / D_ROT)
            ang = jnp.arange(seq_len, dtype=jnp.float32)[:, None] * inv_freq[None, :]
            cos, sin = (jnp.cos(ang), jnp.sin(ang))
            x1, x2 = (c_rot[..., :half], c_rot[..., half:])
            return jnp.concatenate([x1 * cos - x2 * sin, x1 * sin + x2 * cos], axis=-1)
        key = jax.random.key(seed)
        ks = jax.random.split(key, 7)
        std = 0.02
        x = jax.random.normal(ks[0], (B, S, D_MODEL), dtype=jnp.float32)
        W_c = jax.random.normal(ks[1], (D_MODEL, D_C), dtype=jnp.float32) * std
        b_c = jnp.zeros((D_C,), dtype=jnp.float32)
        W_d = jax.random.normal(ks[2], (D_C, 3 * D_MODEL), dtype=jnp.float32) * std
        b_d = jnp.zeros((3 * D_MODEL,), dtype=jnp.float32)
        W_o = jax.random.normal(ks[3], (D_MODEL, D_MODEL), dtype=jnp.float32) * std
        b_o = jnp.zeros((D_MODEL,), dtype=jnp.float32)
        return {'x': x, 'W_c': W_c, 'b_c': b_c, 'W_d': W_d, 'b_d': b_d, 'W_o': W_o, 'b_o': b_o}
    _L0_attn_all = _L0_attn_setup()
    _L0_attn_in = {k: v for k, v in _L0_attn_all.items() if k in ('W_c', 'b_c', 'W_d', 'b_d', 'W_o', 'b_o')}
    del _L0_attn_all

    def _L0_xattn_setup():
        import jax, jax.numpy as jnp
        import numpy as np
        key = jax.random.key(seed)
        ks = jax.random.split(key, 5)
        B, D, L, NH = (2, 256, 512, 8)
        H = D // NH
        return {'v': jax.random.normal(ks[0], (B, D, L), jnp.float32), 'k': jax.random.normal(ks[1], (H, L), jnp.float32) * 0.1, 'bias': jax.random.normal(ks[2], (D,), jnp.float32), 'x1': jax.random.normal(ks[3], (B, D, L), jnp.float32), 'x2': jax.random.normal(ks[4], (B, D, L), jnp.float32), 'num_heads': NH}
    _L0_xattn_all = _L0_xattn_setup()
    _L0_xattn_in = {k: v for k, v in _L0_xattn_all.items() if k in ('k',)}
    del _L0_xattn_all

    def _L0_ffn_setup():
        import jax, jax.numpy as jnp
        import numpy as np
        BLOCK_SIZE = 32
        HIDDEN_SIZE = 512
        MLP_DIM = 4096
        NVFP4_LUT = jnp.array([0.0, 0.5, 1.0, 1.5, 2.0, 3.0, 4.0, 6.0, 0.0, -0.5, -1.0, -1.5, -2.0, -3.0, -4.0, -6.0], dtype=jnp.float32)

        def dequant_nvfp4(W_packed, scales, block=BLOCK_SIZE):
            N = W_packed.shape[0]
            low = W_packed & 15
            high = W_packed >> 4 & 15
            idx = jnp.stack([low, high], axis=-1).reshape(N, -1)
            vals = NVFP4_LUT[idx]
            K = vals.shape[1]
            vals = vals.reshape(N, K // block, block) * scales[:, :, None]
            return vals.reshape(N, K)
        key = jax.random.key(seed)
        ks = jax.random.split(key, 7)
        x = jax.random.normal(ks[0], (4, 32, HIDDEN_SIZE), dtype=jnp.float32)
        gate_W_packed = jax.random.randint(ks[1], (MLP_DIM, HIDDEN_SIZE // 2), 0, 64, dtype=jnp.int32)
        gate_scales = jax.random.uniform(ks[2], (MLP_DIM, HIDDEN_SIZE // BLOCK_SIZE), dtype=jnp.float32) * 0.1 + 0.001
        up_W_packed = jax.random.randint(ks[3], (MLP_DIM, HIDDEN_SIZE // 2), 0, 64, dtype=jnp.int32)
        up_scales = jax.random.uniform(ks[4], (MLP_DIM, HIDDEN_SIZE // BLOCK_SIZE), dtype=jnp.float32) * 0.1 + 0.001
        down_W_packed = jax.random.randint(ks[5], (HIDDEN_SIZE, MLP_DIM // 2), 0, 64, dtype=jnp.int32)
        down_scales = jax.random.uniform(ks[6], (HIDDEN_SIZE, MLP_DIM // BLOCK_SIZE), dtype=jnp.float32) * 0.1 + 0.001
        return {'x': x, 'gate_W_packed': gate_W_packed, 'gate_scales': gate_scales, 'up_W_packed': up_W_packed, 'up_scales': up_scales, 'down_W_packed': down_W_packed, 'down_scales': down_scales}
    _L0_ffn_all = _L0_ffn_setup()
    _L0_ffn_in = {k: v for k, v in _L0_ffn_all.items() if k in ('gate_W_packed', 'gate_scales', 'up_W_packed', 'up_scales', 'down_W_packed', 'down_scales')}
    del _L0_ffn_all
    return {'x': x, 'fside_S2_0': fside_S2_0, 'ctx_2048': ctx_2048, 'L0_attn_W_c': _L0_attn_in['W_c'], 'L0_attn_b_c': _L0_attn_in['b_c'], 'L0_attn_W_d': _L0_attn_in['W_d'], 'L0_attn_b_d': _L0_attn_in['b_d'], 'L0_attn_W_o': _L0_attn_in['W_o'], 'L0_attn_b_o': _L0_attn_in['b_o'], 'L0_xattn_k': _L0_xattn_in['k'], 'L0_ffn_gate_W_packed': _L0_ffn_in['gate_W_packed'], 'L0_ffn_gate_scales': _L0_ffn_in['gate_scales'], 'L0_ffn_up_W_packed': _L0_ffn_in['up_W_packed'], 'L0_ffn_up_scales': _L0_ffn_in['up_scales'], 'L0_ffn_down_W_packed': _L0_ffn_in['down_W_packed'], 'L0_ffn_down_scales': _L0_ffn_in['down_scales']}

def reference(x, fside_S2_0, ctx_2048, L0_attn_W_c, L0_attn_b_c, L0_attn_W_d, L0_attn_b_d, L0_attn_W_o, L0_attn_b_o, L0_xattn_k, L0_ffn_gate_W_packed, L0_ffn_gate_scales, L0_ffn_up_W_packed, L0_ffn_up_scales, L0_ffn_down_W_packed, L0_ffn_down_scales):
    import jax
    import jax.numpy as jnp

    def _L0_attn_ref(x, W_c, b_c, W_d, b_d, W_o, b_o):
        import jax, jax.numpy as jnp
        import numpy as np
        D_MODEL = 512
        NUM_HEADS = 16
        HEAD_DIM = D_MODEL // NUM_HEADS
        D_C = 128
        D_ROT = 64
        B, S = (4, 512)

        def _apply_rotary(c_rot, seq_len):
            half = D_ROT // 2
            inv_freq = 1.0 / 10000.0 ** (jnp.arange(0, D_ROT, 2, dtype=jnp.float32) / D_ROT)
            ang = jnp.arange(seq_len, dtype=jnp.float32)[:, None] * inv_freq[None, :]
            cos, sin = (jnp.cos(ang), jnp.sin(ang))
            x1, x2 = (c_rot[..., :half], c_rot[..., half:])
            return jnp.concatenate([x1 * cos - x2 * sin, x1 * sin + x2 * cos], axis=-1)
        b, s, _ = x.shape
        C = x @ W_c + b_c
        C_rot = _apply_rotary(C[..., :D_ROT], s)
        C = jnp.concatenate([C_rot, C[..., D_ROT:]], axis=-1)
        H = C @ W_d + b_d
        q, k, v = jnp.split(H, 3, axis=-1)
        q = q.reshape(b, s, NUM_HEADS, HEAD_DIM)
        k = k.reshape(b, s, NUM_HEADS, HEAD_DIM)
        v = v.reshape(b, s, NUM_HEADS, HEAD_DIM)
        scale = 1.0 / jnp.sqrt(jnp.asarray(HEAD_DIM, dtype=x.dtype))
        scores = jnp.einsum('bqhd,bkhd->bhqk', q, k) * scale
        attn = jax.nn.softmax(scores, axis=-1)
        out = jnp.einsum('bhqk,bkhd->bqhd', attn, v).reshape(b, s, D_MODEL)
        return out @ W_o + b_o

    def _L0_xattn_ref(v, k, bias, x1, x2, num_heads):
        import jax, jax.numpy as jnp
        import numpy as np
        B, D, L = v.shape
        H = D // num_heads
        fft_size = 2 * L
        vr = v.reshape(B, H, num_heads, L)
        x1r = x1.reshape(B, H, num_heads, L)
        x2r = x2.reshape(B, H, num_heads, L)
        kv = vr[:, :, :, None, :] * x2r[:, :, None, :, :]
        k_f = jnp.fft.rfft(k.astype(jnp.float32), n=fft_size)
        y = jnp.fft.irfft(jnp.fft.rfft(kv, n=fft_size) * k_f[None, :, None, None, :], n=fft_size)[..., :L]
        skip = bias.astype(jnp.float32).reshape(H, num_heads)[None, :, :, None, None]
        y = y + kv * skip
        out = jnp.einsum('bhijl,bhil->bhjl', y, x1r)
        return out.reshape(B, D, L)

    def _L0_ffn_ref(x, gate_W_packed, gate_scales, up_W_packed, up_scales, down_W_packed, down_scales):
        import jax, jax.numpy as jnp
        import numpy as np
        BLOCK_SIZE = 32
        HIDDEN_SIZE = 512
        MLP_DIM = 4096
        NVFP4_LUT = jnp.array([0.0, 0.5, 1.0, 1.5, 2.0, 3.0, 4.0, 6.0, 0.0, -0.5, -1.0, -1.5, -2.0, -3.0, -4.0, -6.0], dtype=jnp.float32)

        def dequant_nvfp4(W_packed, scales, block=BLOCK_SIZE):
            N = W_packed.shape[0]
            low = W_packed & 15
            high = W_packed >> 4 & 15
            idx = jnp.stack([low, high], axis=-1).reshape(N, -1)
            vals = NVFP4_LUT[idx]
            K = vals.shape[1]
            vals = vals.reshape(N, K // block, block) * scales[:, :, None]
            return vals.reshape(N, K)
        B, S, H = x.shape
        xt = x.reshape(B * S, H)
        Wg = dequant_nvfp4(gate_W_packed, gate_scales)
        Wu = dequant_nvfp4(up_W_packed, up_scales)
        Wd = dequant_nvfp4(down_W_packed, down_scales)
        gate = jnp.einsum('th,nh->tn', xt, Wg)
        up = jnp.einsum('th,nh->tn', xt, Wu)
        gelu = jnp.tanh(0.7978845608028654 * (gate + 0.044715 * gate ** 3)) * gate * 0.5 + gate * 0.5
        inter = gelu * up
        out = jnp.einsum('tn,hn->th', inter, Wd)
        return out.reshape(B, S, H)
    x = x + _L0_attn_ref(_layernorm(x, axis=-1), L0_attn_W_c, L0_attn_b_c, L0_attn_W_d, L0_attn_b_d, L0_attn_W_o, L0_attn_b_o)
    x = x + _L0_xattn_ref(_layernorm(x, axis=-1), L0_xattn_k, fside_S2_0, ctx_2048, ctx_2048, 8)
    x = x + _L0_ffn_ref(_layernorm(x, axis=-1), L0_ffn_gate_W_packed, L0_ffn_gate_scales, L0_ffn_up_W_packed, L0_ffn_up_scales, L0_ffn_down_W_packed, L0_ffn_down_scales)
    return x

_drawn_inputs = setup_inputs


def setup_inputs(seed=0):
    import zlib

    import numpy as np

    out = dict(_drawn_inputs(seed))
    spreads = {'L0_attn_b_c': (0.0, 0.541), 'L0_attn_b_d': (0.0, 0.1), 'L0_attn_b_o': (0.0, 0.1)}
    factors = {'L0_attn_W_c': 8.0, 'L0_attn_W_d': 3.487}
    for name, (base, spread) in spreads.items():
        noise = np.random.default_rng([zlib.crc32(name.encode()), seed]).standard_normal(out[name].shape)
        drawn = base * np.exp(spread * noise) if base else spread * noise
        out[name] = jnp.asarray(drawn.astype(out[name].dtype))
    for name, factor in factors.items():
        out[name] = (out[name] * factor).astype(out[name].dtype)
    return out
```

```python
from contextlib import ExitStack

import concourse.bass as bass
from concourse import mybir

P = 128
F32 = mybir.dt.float32
F16 = mybir.dt.float16
BF16 = mybir.dt.bfloat16
I32 = mybir.dt.int32
U16 = mybir.dt.uint16
ALU = mybir.AluOpType
ACT = mybir.ActivationFunctionType
AX_X = mybir.AxisListType.X

B, S, D = 8, 256, 512
DC = 128
NH, DH = 16, 32
KC = D // P
TT = S // P
XH = 8
XG = S // XH
MLP = 4096
EPS = 1e-5

X_SCALE = 2.0 ** 11
WC_SCALE = 2.0 ** 8
C_SCALE = 2.0 ** 4
WD_SCALE = 2.0 ** 8
QK_SCALE = 2.0 ** 2
V_SCALE = 2.0 ** 4
P_SCALE_LOG = 8 * 0.6931471805599453
O_SCALE = 2.0 ** 4
WO_SCALE = 2.0 ** 10
T_SCALE = 2.0 ** 10
KV_SCALE = 2.0 ** 4
W_SCALE = 2.0 ** 8
HIDDEN_SCALE = 2.0 ** -2
SOFTMAX_SCALE = float(DH) ** -0.5

T_COS, T_SIN, T_ID, T_GROUP, T_QMASK, T_KMASK = 0, S, 2 * S, 2 * S + P, 2 * S + 2 * P, 2 * S + 2 * P + 1
T_COLS = T_KMASK + 1


def program(nc, x, ctx_in, ctx_t, tables, wc, bc, wd, bqk, bv, wo, bo, skip, toeplitz,
            packed, scales, out):
    with ExitStack() as top:
        def sb(name, shape, dt, stack=top):
            return stack.enter_context(nc.sbuf_tensor(name, shape, dt))

        X = sb("residual", [P, B * TT, D], F32)
        vT = sb("norm_t", [P, KC, B, S], F32)
        tab = sb("tables_sb", [P, T_COLS], F32)
        attention(nc, X, vT, tab, x, ctx_in, tables, wc, bc, wd, bqk, bv, wo, bo, skip)
        mixing(nc, X, vT, ctx_t, toeplitz)
        feed_forward(nc, X, tab, packed, scales, out)


def attention(nc, X, vT, tab, x, ctx_in, tables, wc, bc, wd, bqk, bv, wo, bo, skip):
    with ExitStack() as st:
        def sb(name, shape, dt):
            return st.enter_context(nc.sbuf_tensor(name, shape, dt))

        def ps(name):
            return st.enter_context(nc.psum_tensor(name, [P, D], F32))

        def sem(name):
            return st.enter_context(nc.semaphore(name))

        ident = tab[:, T_ID:T_ID + P]
        group = tab[:, T_GROUP:T_GROUP + P]
        qmask = tab[:, T_QMASK:T_QMASK + 1]
        kmask = tab[:, T_KMASK:T_KMASK + 1]

        ctxn = sb("ctx_natural", [P, B * TT, D], F32)
        wc_hi, wc_lo = (sb(f"wc_{s}", [P, KC, DC], F16) for s in ("hi", "lo"))
        wd_hi, wd_lo = (sb(f"wd_{s}", [P, 3 * D], F16) for s in ("hi", "lo"))
        w4_hi, w4_lo = (sb(f"w4_{s}", [P, 2 * NH, 4, DH], F16) for s in ("hi", "lo"))
        wo_hi, wo_lo = (sb(f"wo_{s}", [P, KC, D], F16) for s in ("hi", "lo"))
        stage = sb("weights_stage", [P, 4 * D], F32)
        bc_sb = sb("bc_sb", [P, 1], F32)
        bqk_sb = sb("bqk_sb", [P, 2 * NH], F32)
        bv_sb = sb("bv_sb", [P, D], F32)
        bo_sb = sb("bo_sb", [P, D], F32)
        skip_sb = sb("skip_sb", [P, TT], F32)
        half = sb("minus_half", [P, 2 * TT], F32)
        ident_bf = sb("ident_bf", [P, P], BF16)
        ones_bf = sb("ones_bf", [P, P], BF16)

        stats = sb("stats", [P, TT, 6], F32)
        mv = sb("mean_var", [P, TT, 2], F32)
        ve = sb("var_plus_eps", [P, TT], F32)
        rstd = sb("rstd", [P, TT], F32)
        xn = sb("xn", [P, TT, D], F32)
        xT_hi, xT_lo = (sb(f"xT_{s}", [P, KC, S], F16) for s in ("hi", "lo"))
        c32 = sb("c32", [P, S], F32)
        csw = sb("c_swapped", [P, S], F32)
        c_hi, c_lo = (sb(f"c_{s}", [P, S], F16) for s in ("hi", "lo"))
        v32 = sb("v32", [P, TT, D], F32)
        v_hi, v_lo = (sb(f"v_{s}", [P, TT, D], F16) for s in ("hi", "lo"))
        den_col = sb("den_col", [P, 1], F16)
        log_scale = sb("log_scale", [P, 1], F32)
        QR = 4
        qk_hi = sb("qk_hi", [P, 2, 2, S], F16)
        qk32 = sb("qk32", [P, 2, 2, S], F32)
        qk = sb("qk", [P, QR, 2, S], F16)
        nmax = sb("minus_max", [P, 2, TT], F32)
        diag = sb("minus_max_diag", [P, 2, TT, P], BF16)
        p32 = sb("p32", [P, 2, TT, S], F32)
        p_hi, p_lo = (sb(f"p_{s}", [P, 2, TT, S], F16) for s in ("hi", "lo"))
        rden = sb("rden", [P, TT * NH], F32)
        o_n = sb("o_n", [P, TT, D], F32)
        oT_hi, oT_lo = (sb(f"oT_{s}", [P, KC, P], F16) for s in ("hi", "lo"))
        wskip = sb("w_skip", [P, TT, D], F32)
        skt = sb("skip_term", [P, D], F32)
        xbo = sb("x_plus_bo", [P, TT, D], F32)

        pS, pST0, pST1, pO0, pO1, pH, pDen, pM = (
            ps(n) for n in ("p_scores", "p_scores_t0", "p_scores_t1", "p_o0", "p_o1", "p_qk", "p_den", "p_misc"))
        pST, pO = (pST0, pST1), (pO0, pO1)
        pSv = pS[:].rearrange("p (t k) -> p t k", t=TT)
        pSTv = [a[:].rearrange("p (t q) -> p t q", t=TT) for a in pST]
        pHv = pH[:].rearrange("p (a t) -> p a t", a=2)
        pMv = pM[:].rearrange("p (c t) -> p c t", c=KC)
        pDenv = pDen[:, 0:TT * NH].rearrange("p (t h) -> p t h", t=TT)

        s_load = [sem(f"loaded_{i}") for i in range(5)]
        s_x = sem("x_loaded")
        s_small = sem("small_loaded")
        s_ctx = sem("ctx_loaded")
        s_whi = sem("weight_hi")
        s_wlo = sem("weight_lo")
        with nc.Block() as block:
            jobs = [(wc.rearrange("(c p) n -> p c n", p=P), wc_hi, wc_lo, KC * DC, WC_SCALE, DC),
                    (wd, wd_hi, wd_lo, 3 * D, WD_SCALE, None),
                    (wo.rearrange("(c p) n -> p c n", p=P), wo_hi, wo_lo, KC * D, WO_SCALE, D)]

            def staged(n, width):
                a = stage[:, 0:n]
                return a if width is None else a.rearrange("p (c n) -> p c n", n=width)

            @block.sync
            def _(sp):
                sp.dma_start(tab[:], tables).then_inc(s_small, 16)
                for j, (src, hi, lo, n, scale, width) in enumerate(jobs):
                    if j:
                        sp.wait_ge(s_wlo, j)
                    sp.dma_start(staged(n, width), src).then_inc(s_load[j], 16)
                    if j == 0:
                        sp.dma_start(X[:], x.rearrange("b (t p) d -> p (b t) d", p=P)).then_inc(s_x, 16)

            @block.gpsimd
            def _(pool):
                pool.memset(half[:], -0.5)
                pool.memset(log_scale[:], P_SCALE_LOG)
                pool.memset(ones_bf[:], 1.0)
                pool.memset(den_col[:], V_SCALE).then_inc(s_ctx, 16)

            @block.scalar
            def _(act):
                act.dma_start(bc_sb[:], bc.rearrange("(p a) -> p a", a=1)).then_inc(s_small, 16)
                for r in range(4):
                    act.dma_start(bqk_sb[r * DH:(r + 1) * DH, :], bqk).then_inc(s_small, 16)
                act.dma_start(bv_sb[:], bv.rearrange("(a n) -> a n", a=1).to_broadcast([P, D])).then_inc(s_small, 16)
                act.dma_start(bo_sb[:], bo.rearrange("(a n) -> a n", a=1).to_broadcast([P, D])).then_inc(s_small, 16)
                act.dma_start(skip_sb[:], skip).then_inc(s_small, 16)
                act.dma_start(ctxn[:], ctx_in.rearrange("b (t p) d -> p (b t) d", p=P)).then_inc(s_ctx, 16)
                for j, (src, hi, lo, n, scale, width) in enumerate(jobs):
                    act.wait_ge(s_load[j], 16)
                    nc.scalar.activation(hi[:], staged(n, width), ACT.Copy, scale=scale).then_inc(s_whi, 1)

            @block.vector
            def _(dve):
                for j, (src, hi, lo, n, scale, width) in enumerate(jobs):
                    dve.wait_ge(s_whi, j + 1)
                    nc.vector.scalar_tensor_tensor(out=lo[:], in0=staged(n, width), scalar=scale, in1=hi[:],
                                                   op0=ALU.mult, op1=ALU.subtract).then_inc(s_wlo, 1)
                dve.wait_ge(s_wlo, 3)
                for r in range(4):
                    for one, four in ((wd_hi, w4_hi), (wd_lo, w4_lo)):
                        nc.vector.tensor_copy(four[:, :, r, :], one[:, 0:2 * D].rearrange("p (n d) -> p n d", d=DH))
                dve.wait_ge(s_small, 16 * 9)
                nc.vector.tensor_copy(ident_bf[:], ident)
                nc.vector.tensor_scalar(bqk_sb[:], bqk_sb[:], QK_SCALE, None, ALU.mult)
                nc.vector.tensor_scalar(bv_sb[:], bv_sb[:], V_SCALE, None, ALU.mult)
                nc.vector.memset(csw[:], 0.0)
                dve.wait_ge(s_x, 16)
                dve.wait_ge(s_ctx, 32)

        s_stat = sem("mean_and_variance")
        s_rstd = sem("rstd_ready")
        s_xn = sem("normed")
        s_misc = sem("misc_product")
        s_hi = sem("hi_half")
        s_xT = sem("xT_ready")
        s_rot = sem("c_rotated")
        s_c = sem("c_ready")
        s_v32 = sem("v32_ready")
        s_v = sem("v_ready")
        s_qk_mm = sem("qk_product")
        s_qk_act = sem("qk_read")
        s_qk = sem("qk_ready")
        s_s = sem("scores")
        s_dg = sem("maxima_ready")
        s_st = sem("scores_t")
        s_e = sem("exp_done")
        s_ph = sem("p_hi_ready")
        s_pl = sem("p_lo_ready")
        s_pv = sem("weighted_done")
        s_on = sem("o_normed")
        s_oT = sem("oT_ready")
        s_xbo = sem("bias_added")
        s_x1 = sem("x1_ready")
        s_vn = sem("v_normed")
        s_vT = sem("vT_written")
        s_x2 = sem("skip_added")
        s_step = sem("dve_step")
        s_passed = sem("dve_wait_passed")
        STEPS = 12 + NH

        uses = [("xT", 0), ("xT", 1), ("c", 0), ("v", 0), ("v", 1), ("oT", 0), ("wo", 0), ("oT", 1), ("wo", 1),
                ("vT", 0), ("sk", 0), ("vT", 1), ("sk", 1)]
        halves = [("xT", 0), ("xT", 1), ("c", 0), ("v", 0), ("v", 1), ("oT", 0), ("oT", 1)]

        def product(b, key):
            return b * len(uses) + uses.index(key) + 1

        def hi_half(b, key):
            return b * len(halves) + halves.index(key) + 1

        QK0, QKA0, DG0, ST0, E0, PL0, PV0, ON0, X20 = 4, 2, 1, 4, 2, 2, 2, 1, 1

        with nc.Block() as block:
            @block.gpsimd
            def _(pool):
                with pool.Fori(0, B) as b:
                    pool.wait_ge(s_stat, b * 2 + 1)
                    nc.gpsimd.tensor_tensor(rstd[:], ve[:], half[:, 0:TT], ALU.pow).then_inc(s_rstd, 1)
                    for t in range(TT):
                        last = nc.gpsimd.tensor_tensor(xbo[:, t, :], X[:, bass.ds(b * TT + t, 1), :].rearrange("p a d -> p (a d)"),
                                                       bo_sb[:], ALU.add)
                    last.then_inc(s_xbo, 1)
                    pool.wait_ge(s_stat, b * 2 + 2)
                    nc.gpsimd.tensor_tensor(rstd[:], ve[:], half[:, 0:TT], ALU.pow).then_inc(s_rstd, 1)

            @block.tensor
            def _(pe):
                pe.sem_inc(s_st, ST0)
                pe.sem_inc(s_pv, PV0)
                with pe.Fori(0, B) as b:
                    def transposes(src):
                        for c in range(KC):
                            last = nc.tensor.transpose(pMv[:, c, :], src[:, c * P:(c + 1) * P], ident)
                        last.then_inc(s_misc, 1)

                    pe.wait_ge(s_x2, b * TT + X20)
                    for t in range(TT):
                        pe.wait_ge(s_xn, b * TT + t + 1)
                        if t:
                            pe.wait_ge(s_xT, b * TT + t)
                        transposes(xn[:, t, :])
                    pe.wait_ge(s_xT, b * TT + TT)
                    n = 0
                    for c in range(KC):
                        for w, m in ((wc_hi, xT_hi), (wc_hi, xT_lo), (wc_lo, xT_hi)):
                            last = nc.tensor.matmul(pM[:, 0:S], w[:, c, :], m[:, c, :], start=(n == 0), stop=(n == 3 * KC - 1))
                            n += 1
                    last.then_inc(s_misc, 1)
                    pe.wait_ge(s_c, b + 1)
                    for t in range(TT):
                        if t:
                            pe.wait_ge(s_v32, b * TT + t)
                        for k, (w, m) in enumerate(((c_hi, wd_hi), (c_lo, wd_hi), (c_hi, wd_lo))):
                            last = nc.tensor.matmul(pM[:], w[:, t * P:(t + 1) * P], m[:, 2 * D:3 * D],
                                                    start=(k == 0), stop=(k == 2))
                        last.then_inc(s_misc, 1)

                    def project(h):
                        pe.wait_ge(s_qk_act, (b * NH + h) * 2 + QKA0)
                        for a in range(2):
                            for k, (w, m) in enumerate(((w4_hi, c_hi), (w4_lo, c_hi), (w4_hi, c_lo))):
                                last = nc.tensor.matmul(pHv[:, a, :], w[:, a * NH + h].rearrange("p r d -> p (r d)"), m[:],
                                                        start=(k == 0), stop=(k == 2))
                        last.then_inc(s_qk_mm, 1)

                    def scores(h):
                        pe.wait_ge(s_qk, (b * NH + h) * 2 + 2 + QK0)
                        pe.wait_ge(s_dg, b * NH + h + DG0)
                        r = h % QR
                        for t in range(TT):
                            last = nc.tensor.matmul(pSv[:, t, :], qk[:, r, 0, t * P:(t + 1) * P], qk[:, r, 1, :],
                                                    start=True, stop=True)
                        last.then_inc(s_s, 1)

                    def scores_t(h):
                        pe.wait_ge(s_dg, b * NH + h + 1 + DG0)
                        pe.wait_ge(s_e, b * NH + h - 1 + E0)
                        r = h % QR
                        for t in range(TT):
                            part = pSTv[h % 2][:, t, :]
                            nc.tensor.matmul(part, qk[:, r, 1, t * P:(t + 1) * P], qk[:, r, 0, :], start=True, stop=False)
                            last = nc.tensor.matmul(part, ones_bf[:], diag[:, h % 2].rearrange("p t q -> p (t q)"),
                                                    start=False, stop=True)
                        last.then_inc(s_st, 1)

                    def weighted(h):
                        pe.wait_ge(s_pl, b * NH + h + 1 + PL0)
                        r = h % 2
                        for t in range(TT):
                            n = 0
                            for c in range(TT):
                                ph, pl = (a[:, r, c, t * P:(t + 1) * P] for a in (p_hi, p_lo))
                                vh, vl = (a[:, c, h * DH:(h + 1) * DH] for a in (v_hi, v_lo))
                                for w, v_ in ((ph, vh), (ph, vl), (pl, vh)):
                                    nc.tensor.matmul(pO[t][:, h * DH:(h + 1) * DH], w, v_,
                                                     start=(n == 0), stop=(n == 3 * TT - 1))
                                    n += 1
                            n = 0
                            for c in range(TT):
                                for a in (p_hi, p_lo):
                                    last = nc.tensor.matmul(pDenv[:, t, h:h + 1], a[:, r, c, t * P:(t + 1) * P], den_col[:],
                                                            start=(n == 0), stop=(n == 2 * TT - 1))
                                    n += 1
                        last.then_inc(s_pv, 1)

                    project(0)
                    project(1)
                    scores(0)
                    pe.wait_ge(s_v, b * TT + TT)
                    pe.wait_ge(s_on, b * TT + ON0)
                    for h in range(NH):
                        scores_t(h)
                        if h + 1 < NH:
                            scores(h + 1)
                        if h + 2 < NH:
                            project(h + 2)
                        if h:
                            weighted(h - 1)
                    weighted(NH - 1)

                    for t in range(TT):
                        pe.wait_ge(s_on, b * TT + t + 1 + ON0)
                        if t:
                            pe.wait_ge(s_x1, b * TT + t)
                        transposes(o_n[:, t, :])
                        pe.wait_ge(s_oT, b * TT + t + 1)
                        n = 0
                        for c in range(KC):
                            for w, m in ((oT_hi, wo_hi), (oT_lo, wo_hi), (oT_hi, wo_lo)):
                                last = nc.tensor.matmul(pM[:], w[:, c, :], m[:, c, :], start=(n == 0), stop=(n == 3 * KC - 1))
                                n += 1
                        last.then_inc(s_misc, 1)
                    for t in range(TT):
                        pe.wait_ge(s_vn, b * TT + t + 1)
                        if t:
                            pe.wait_ge(s_x2, b * TT + t + X20)
                        transposes(xn[:, t, :])
                        pe.wait_ge(s_vT, b * TT + t + 1)
                        nc.tensor.matmul(pM[:], group, wskip[:, t, :], start=True, stop=True).then_inc(s_misc, 1)

            @block.scalar
            def _(act):
                act.sem_inc(s_qk_act, QKA0)
                act.sem_inc(s_e, E0)
                with act.Fori(0, B) as b:
                    for t in range(TT):
                        act.wait_ge(s_misc, product(b, ("xT", t)))
                        nc.scalar.activation(xT_hi[:, :, t * P:(t + 1) * P], pMv, ACT.Copy,
                                             scale=X_SCALE).then_inc(s_hi, 1)
                    act.wait_ge(s_rot, b + 1)
                    act.wait_ge(s_pv, b * NH + PV0)
                    nc.scalar.activation(c_hi[:], c32[:], ACT.Copy, scale=C_SCALE).then_inc(s_hi, 1)
                    for t in range(TT):
                        act.wait_ge(s_v32, b * TT + t + 1)
                        nc.scalar.activation(v_hi[:, t, :], v32[:, t, :], ACT.Copy).then_inc(s_hi, 1)

                    def evacuate(h):
                        for a in range(2):
                            n = (b * NH + h) * 2 + a
                            if a == 0:
                                act.wait_ge(s_qk_mm, b * NH + h + 1)
                            act.wait_ge(s_qk, n - 3 + QK0)
                            bias = bqk_sb[:, a * NH + h:a * NH + h + 1]
                            scale = QK_SCALE / (C_SCALE * WD_SCALE)
                            nc.scalar.activation(qk_hi[:, h % 2, a, :], pHv[:, a, :], ACT.Identity, bias=bias, scale=scale)
                            nc.scalar.activation(qk32[:, h % 2, a, :], pHv[:, a, :], ACT.Identity, bias=bias,
                                                 scale=scale).then_inc(s_qk_act, 1)

                    evacuate(0)
                    evacuate(1)
                    for h in range(NH):
                        n = b * NH + h
                        act.wait_ge(s_st, n + 1 + ST0)
                        act.wait_ge(s_pl, n - 1 + PL0)
                        nc.scalar.activation(p32[:, h % 2].rearrange("p t q -> p (t q)"), pST[h % 2][:], ACT.Exp,
                                             bias=log_scale[:, 0:1], scale=SOFTMAX_SCALE / QK_SCALE ** 2).then_inc(s_e, 1)
                        act.wait_ge(s_pv, n - 1 + PV0)
                        act.wait_ge(s_e, n + 1 + E0)
                        nc.scalar.activation(p_hi[:, h % 2], p32[:, h % 2], ACT.Copy).then_inc(s_ph, 1)
                        if h + 2 < NH:
                            evacuate(h + 2)
                    for t in range(TT):
                        act.wait_ge(s_misc, product(b, ("oT", t)))
                        nc.scalar.activation(oT_hi[:], pMv, ACT.Copy, scale=O_SCALE).then_inc(s_hi, 1)
                    for t in range(TT):
                        act.wait_ge(s_misc, product(b, ("vT", t)))
                        nc.scalar.activation(vT[:, :, bass.ds(b, 1), t * P:(t + 1) * P].rearrange("p c a s -> p c (a s)"), pMv,
                                             ACT.Copy).then_inc(s_vT, 1)

            @block.vector
            def _(dve):
                for s_, n in ((s_qk, QK0), (s_dg, DG0), (s_pl, PL0), (s_on, ON0), (s_x2, X20)):
                    dve.sem_inc(s_, n)
                with dve.Fori(0, B) as b:
                    steps = [0]

                    def written(instruction):
                        steps[0] += 1
                        instruction.then_inc(s_step, 1)
                        dve.wait_ge(s_step, b * STEPS + steps[0])

                    def tile_of(a, t):
                        return a[:, bass.ds(b * TT + t, 1), :].rearrange("p a d -> p (a d)")

                    def moments():
                        for t in range(TT):
                            last = nc.vector.bn_stats(stats[:, t, :], tile_of(X, t))
                        written(last)
                        dve.sem_inc(s_passed, 1)
                        for t in range(TT):
                            last = nc.vector.bn_aggr(mv[:, t, :], stats[:, t, :])
                        written(last)
                        nc.vector.tensor_scalar(ve[:], mv[:, :, 1], EPS, None, ALU.add).then_inc(s_stat, 1)

                    def normed(t):
                        return nc.vector.tensor_scalar(xn[:, t, :], tile_of(X, t), mv[:, t, 0:1], rstd[:, t:t + 1],
                                                       ALU.subtract, ALU.mult)

                    moments()
                    dve.wait_ge(s_rstd, b * 2 + 1)
                    for t in range(TT):
                        normed(t).then_inc(s_xn, 1)
                    for t in range(TT):
                        dve.wait_ge(s_hi, hi_half(b, ("xT", t)))
                        nc.vector.scalar_tensor_tensor(out=xT_lo[:, :, t * P:(t + 1) * P], in0=pMv,
                                                       scalar=X_SCALE, in1=xT_hi[:, :, t * P:(t + 1) * P],
                                                       op0=ALU.mult, op1=ALU.subtract).then_inc(s_xT, 1)
                    dve.wait_ge(s_misc, product(b, ("c", 0)))
                    written(nc.vector.tensor_scalar(c32[:], pM[:, 0:S], 1.0 / (X_SCALE * WC_SCALE), bc_sb[:, 0:1],
                                                    ALU.mult, ALU.add))
                    nc.vector.tensor_copy(csw[0:DH, :], c32[DH:2 * DH, :])
                    written(nc.vector.tensor_copy(csw[DH:2 * DH, :], c32[0:DH, :]))
                    nc.vector.tensor_tensor(c32[:], c32[:], tab[:, T_COS:T_COS + S], ALU.mult)
                    written(nc.vector.tensor_tensor(csw[:], csw[:], tab[:, T_SIN:T_SIN + S], ALU.mult))
                    nc.vector.tensor_tensor(c32[:], c32[:], csw[:], ALU.add).then_inc(s_rot, 1)
                    dve.wait_ge(s_hi, hi_half(b, ("c", 0)))
                    nc.vector.scalar_tensor_tensor(out=c_lo[:], in0=c32[:], scalar=C_SCALE, in1=c_hi[:],
                                                   op0=ALU.mult, op1=ALU.subtract).then_inc(s_c, 1)
                    for t in range(TT):
                        dve.wait_ge(s_misc, product(b, ("v", t)))
                        nc.vector.scalar_tensor_tensor(out=v32[:, t, :], in0=pM[:], scalar=V_SCALE / (C_SCALE * WD_SCALE),
                                                       in1=bv_sb[:], op0=ALU.mult, op1=ALU.add).then_inc(s_v32, 1)
                    for t in range(TT):
                        dve.wait_ge(s_hi, hi_half(b, ("v", t)))
                        nc.vector.tensor_tensor(v_lo[:, t, :], v32[:, t, :], v_hi[:, t, :], ALU.subtract).then_inc(s_v, 1)

                    def halves_of(h):
                        for a, mask in ((0, qmask), (1, kmask)):
                            n = (b * NH + h) * 2 + a
                            dve.wait_ge(s_qk_act, n + 1 + QKA0)
                            if a == 0:
                                dve.wait_ge(s_st, b * NH + h - 3 + ST0)
                            nc.vector.scalar_tensor_tensor(out=qk[:, h % QR, a, :], in0=qk_hi[:, h % 2, a, :], scalar=mask,
                                                           in1=qk32[:, h % 2, a, :], op0=ALU.mult,
                                                           op1=ALU.add).then_inc(s_qk, 1)

                    def maxima(h):
                        n = b * NH + h
                        dve.wait_ge(s_s, n + 1)
                        written(nc.vector.tensor_reduce(nmax[:, h % 2, :], pSv, AX_X, ALU.max, negate=True))
                        dve.wait_ge(s_st, n - 1 + ST0)
                        for t in range(TT):
                            last = nc.vector.tensor_scalar(diag[:, h % 2, t, :], ident_bf[:], nmax[:, h % 2, t:t + 1], None,
                                                           ALU.mult)
                        last.then_inc(s_dg, 1)

                    halves_of(0)
                    halves_of(1)
                    maxima(0)
                    for h in range(NH):
                        if h + 1 < NH:
                            maxima(h + 1)
                        if h + 2 < NH:
                            halves_of(h + 2)
                        dve.wait_ge(s_ph, b * NH + h + 1)
                        nc.vector.tensor_tensor(p_lo[:, h % 2], p32[:, h % 2], p_hi[:, h % 2],
                                                ALU.subtract).then_inc(s_pl, 1)
                    dve.wait_ge(s_pv, b * NH + NH + PV0)
                    written(nc.vector.reciprocal(rden[:], pDen[:, 0:TT * NH]))
                    for t in range(TT):
                        nc.vector.tensor_tensor(
                            o_n[:, t, :].rearrange("p (h d) -> p h d", d=DH), pO[t][:].rearrange("p (h d) -> p h d", d=DH),
                            rden[:, t * NH:(t + 1) * NH].unsqueeze(2).to_broadcast([P, NH, DH]), ALU.mult).then_inc(s_on, 1)
                    dve.wait_ge(s_xbo, b + 1)
                    for t in range(TT):
                        dve.wait_ge(s_hi, hi_half(b, ("oT", t)))
                        nc.vector.scalar_tensor_tensor(out=oT_lo[:], in0=pMv, scalar=O_SCALE, in1=oT_hi[:],
                                                       op0=ALU.mult, op1=ALU.subtract).then_inc(s_oT, 1)
                        dve.wait_ge(s_misc, product(b, ("wo", t)))
                        nc.vector.scalar_tensor_tensor(out=tile_of(X, t), in0=pM[:], scalar=1.0 / (O_SCALE * WO_SCALE),
                                                       in1=xbo[:, t, :], op0=ALU.mult, op1=ALU.add).then_inc(s_x1, 1)
                    dve.wait_ge(s_x1, b * TT + TT)
                    dve.sem_inc(s_passed, 1)
                    moments()
                    dve.wait_ge(s_rstd, b * 2 + 2)
                    for t in range(TT):
                        written(normed(t))
                        nc.vector.scalar_tensor_tensor(out=wskip[:, t, :], in0=xn[:, t, :], scalar=skip_sb[:, t:t + 1],
                                                       in1=tile_of(ctxn, t), op0=ALU.mult, op1=ALU.mult).then_inc(s_vn, 1)
                    for t in range(TT):
                        dve.wait_ge(s_misc, product(b, ("sk", t)))
                        written(nc.vector.tensor_tensor(skt[:], pM[:], tile_of(ctxn, t), ALU.mult))
                        nc.vector.tensor_tensor(tile_of(X, t), tile_of(X, t), skt[:], ALU.add).then_inc(s_x2, 1)
                    assert steps[0] == STEPS


def mixing(nc, X, vT, ctx_t, toeplitz):
    PAIRS = B * XH * XH
    CB = KC * B
    with ExitStack() as st:
        def sb(name, shape, dt):
            return st.enter_context(nc.sbuf_tensor(name, shape, dt))

        def sem(name):
            return st.enter_context(nc.semaphore(name))

        cT = sb("ctx_transposed", [P, KC, B, S], F32)
        t32 = sb("toeplitz32", [P, 2, D], F32)
        t_hi, t_lo = (sb(f"toeplitz_{s}", [P, 2, D], F16) for s in ("hi", "lo"))
        kv32 = sb("pairs32", [P, 2, KC, PAIRS], F32)
        kv_hi, kv_lo = (sb(f"pairs_{s}", [P, 2, KC, PAIRS], F16) for s in ("hi", "lo"))
        z = sb("weighted_pairs", [P, 2, KC, PAIRS], F32)
        half1 = sb("sum_of_2", [P, CB, 4 * XH], F32)
        half2 = sb("sum_of_4", [P, CB, 2 * XH], F32)
        vT_cb = vT[:].rearrange("p c b s -> p (c b) s")
        cT_cb = cT[:].rearrange("p c b s -> p (c b) s")

        s_ctx = sem("ctx_t_loaded")
        s_t32 = [sem(f"toeplitz_loaded_{r}") for r in range(2)]
        s_thi = sem("toeplitz_hi_ready")
        s_tlo = sem("toeplitz_lo_ready")
        s_kv = sem("pairs_ready")
        s_kvhi = sem("pairs_hi_ready")
        s_kvlo = sem("pairs_lo_ready")
        s_y = sem("convolved")
        s_z = sem("weighted_pairs_ready")
        s_sum = sem("summed")
        s_pool = sem("partial_sum")
        TLO0, KVLO0, Y0, Z0, SUM0 = 2, 2, 2 * KC, 2 * KC, 2

        with ExitStack() as banks:
            pY = [[banks.enter_context(nc.psum_tensor(f"p_conv{r}{c}", [P, PAIRS], F32)) for c in range(KC)]
                  for r in range(2)]
            with nc.Block() as block:
                @block.sync
                def _(sp):
                    sp.dma_start(cT[:], ctx_t.rearrange("(c p) b s -> p c b s", p=P)).then_inc(s_ctx, 16)
                    with sp.Fori(0, XG // 2) as i:
                        for r in range(2):
                            g = i * 2 + r
                            sp.wait_ge(s_tlo, g - 1 + TLO0)
                            sp.dma_start(t32[:, r, :], toeplitz[bass.ds(g, 1)].rearrange("a p n -> p (a n)")
                                         ).then_inc(s_t32[r], 16)

                @block.tensor
                def _(pe):
                    pe.sem_inc(s_y, Y0)
                    with pe.Fori(0, XG // 2) as i:
                        for r in range(2):
                            g = i * 2 + r
                            pe.wait_ge(s_kvlo, g + 1 + KVLO0)
                            for c in range(KC):
                                pe.wait_ge(s_z, (g - 2) * KC + c + 1 + Z0)
                                n = 0
                                for m in range(c + 1):
                                    block_ = slice((c - m) * P, (c - m + 1) * P)
                                    for w, v_ in ((t_hi, kv_hi), (t_hi, kv_lo), (t_lo, kv_hi)):
                                        last = nc.tensor.matmul(pY[r][c][:], w[:, r, block_], v_[:, r, m, :],
                                                                start=(n == 0), stop=(n == 3 * c + 2))
                                        n += 1
                                last.then_inc(s_y, 1)

                @block.scalar
                def _(act):
                    with act.Fori(0, XG // 2) as i:
                        for r in range(2):
                            g = i * 2 + r
                            act.wait_ge(s_t32[r], (i + 1) * 16)
                            act.wait_ge(s_y, (g - 1) * KC + Y0)
                            nc.scalar.activation(t_hi[:, r, :], t32[:, r, :], ACT.Copy, scale=T_SCALE).then_inc(s_thi, 1)
                            act.wait_ge(s_kv, g + 1)
                            nc.scalar.activation(kv_hi[:, r], kv32[:, r], ACT.Copy, scale=KV_SCALE).then_inc(s_kvhi, 1)

                @block.gpsimd
                def _(pool):
                    pool.sem_inc(s_sum, SUM0)
                    with pool.Fori(0, XG // 2) as i:
                        for r in range(2):
                            g = i * 2 + r
                            zz = z[:, r].rearrange("p c (b n) -> p (c b) n", b=B)
                            pool.wait_ge(s_z, (g + 1) * KC + Z0)
                            nc.gpsimd.tensor_tensor(half1[:], zz[:, :, 0:4 * XH], zz[:, :, 4 * XH:8 * XH],
                                                    ALU.add).then_inc(s_pool, 1)
                            pool.wait_ge(s_pool, g * 2 + 1)
                            nc.gpsimd.tensor_tensor(half2[:], half1[:, :, 0:2 * XH], half1[:, :, 2 * XH:4 * XH],
                                                    ALU.add).then_inc(s_pool, 1)
                            pool.wait_ge(s_pool, g * 2 + 2)
                            nc.gpsimd.tensor_tensor(vT_cb[:, :, bass.ds(g * XH, XH)], half2[:, :, 0:XH],
                                                    half2[:, :, XH:2 * XH], ALU.add).then_inc(s_sum, 1)

                @block.vector
                def _(dve):
                    dve.sem_inc(s_tlo, TLO0)
                    dve.sem_inc(s_kvlo, KVLO0)
                    dve.sem_inc(s_z, Z0)

                    def pairs(g, r):
                        dve.wait_ge(s_kvlo, g - 1 + KVLO0)
                        v_, c_ = (a[:, :, bass.ds(g * XH, XH)] for a in (vT_cb, cT_cb))
                        nc.vector.tensor_tensor(kv32[:, r].rearrange("p c (b i j) -> p (c b) i j", i=XH, j=XH),
                                                v_.unsqueeze(3).to_broadcast([P, CB, XH, XH]),
                                                c_.unsqueeze(2).to_broadcast([P, CB, XH, XH]), ALU.mult).then_inc(s_kv, 1)

                    def low_halves(g, r):
                        dve.wait_ge(s_thi, g + 1)
                        nc.vector.scalar_tensor_tensor(out=t_lo[:, r, :], in0=t32[:, r, :], scalar=T_SCALE, in1=t_hi[:, r, :],
                                                       op0=ALU.mult, op1=ALU.subtract).then_inc(s_tlo, 1)
                        dve.wait_ge(s_kvhi, g + 1)
                        nc.vector.scalar_tensor_tensor(out=kv_lo[:, r], in0=kv32[:, r], scalar=KV_SCALE, in1=kv_hi[:, r],
                                                       op0=ALU.mult, op1=ALU.subtract).then_inc(s_kvlo, 1)

                    def weigh(g, r):
                        dve.wait_ge(s_sum, g - 1 + SUM0)
                        for c in range(KC):
                            dve.wait_ge(s_y, g * KC + c + 1 + Y0)
                            nc.vector.tensor_tensor(
                                z[:, r, c].rearrange("p (b i j) -> p b i j", i=XH, j=XH),
                                pY[r][c][:].rearrange("p (b i j) -> p b i j", i=XH, j=XH),
                                cT[:, c, :, bass.ds(g * XH, XH)].unsqueeze(3).to_broadcast([P, B, XH, XH]),
                                ALU.mult).then_inc(s_z, 1)

                    dve.wait_ge(s_ctx, 16)
                    pairs(0, 0)
                    pairs(1, 1)
                    low_halves(0, 0)
                    with dve.Fori(0, XG // 2 - 1) as i:
                        for r in range(2):
                            pairs(i * 2 + r + 2, r)
                            low_halves(i * 2 + r + 1, (r + 1) % 2)
                            weigh(i * 2 + r, r)
                    low_halves(XG - 1, 1)
                    weigh(XG - 2, 0)
                    weigh(XG - 1, 1)

        s_back = sem("transposed_back")
        s_added = sem("mixing_added")
        with ExitStack() as banks:
            pT = [banks.enter_context(nc.psum_tensor(f"p_back{r}", [P, KC, P], F32)) for r in range(4)]
            ident = sb("ident_back", [P, P], F32)
            with nc.Block() as block:
                tiles = [(b, t) for b in range(B) for t in range(TT)]

                @block.sync
                def _(sp):
                    pass

                @block.gpsimd
                def _(pool):
                    pool.memset(ident[:], 0.0).then_inc(s_pool, 1)
                    pool.wait_ge(s_pool, 2 * XG + 1)
                    nc.gpsimd.affine_select(out=ident[:], in_=ident[:], compare_op=ALU.not_equal, fill=1.0, base=0,
                                            pattern=[[-1, P]], channel_multiplier=1).then_inc(s_pool, 1)

                @block.tensor
                def _(pe):
                    pe.wait_ge(s_pool, 2 * XG + 2)
                    for n, (b, t) in enumerate(tiles):
                        if n >= len(pT):
                            pe.wait_ge(s_added, n - len(pT) + 1)
                        for c in range(KC):
                            last = nc.tensor.transpose(pT[n % len(pT)][:, c, :], vT[:, c, b, t * P:(t + 1) * P], ident[:])
                        last.then_inc(s_back, 1)

                @block.vector
                def _(dve):
                    for n in range(len(tiles)):
                        dve.wait_ge(s_back, n + 1)
                        row = X[:, n, :]
                        nc.vector.scalar_tensor_tensor(out=row, in0=pT[n % len(pT)][:].rearrange("p c l -> p (c l)"),
                                                       scalar=1.0 / (T_SCALE * KV_SCALE), in1=row,
                                                       op0=ALU.mult, op1=ALU.add).then_inc(s_added, 1)


def feed_forward(nc, X, tab, packed, scales, out):
    UNITS = MLP // (2 * P)
    GU = 2
    GROUPS = UNITS // GU
    THIRDS = 3 * GU
    HC = 2 * GU
    TB = 4
    TW = B * S // TB
    BT = TW // P
    TILES = B * TT
    SLOTS = TB * HC
    KS = P // 16
    W_FACTOR = 2.0 ** 14 * W_SCALE
    GU_OUT = 1.0 / (X_SCALE * W_SCALE)
    ROOT, CUBIC = 0.7978845608028654, 0.044715
    with ExitStack() as st:
        def sb(name, shape, dt):
            return st.enter_context(nc.sbuf_tensor(name, shape, dt))

        def sem(name):
            return st.enter_context(nc.semaphore(name))

        ident = tab[:, T_ID:T_ID + P]
        xT_hi, xT_lo = (sb(f"ff_xT_{s}", [P, 2, 2, B * S], F16) for s in ("hi", "lo"))
        w_hi, w_lo = (sb(f"ff_w_{s}", [P, 2, GU, 3, 2, D], F16) for s in ("hi", "lo"))
        codes = sb("codes", [P, GU, 3, D], I32)
        scale = sb("code_scales", [P, GU, 3, D], F32)
        mag = sb("magnitude_bits", [P, 2, D], U16)
        sign = sb("sign_bits", [P, 2, D], U16)
        w32 = sb("weights32", [P, 2, 2, D], F32)
        s_load = [sem(f"unit_loaded_{r}") for r in range(GU)]
        s_w32 = sem("weights32_ready")
        s_whi = sem("w_hi_ready")
        s_wlo = sem("w_lo_ready")
        s_down = sem("down_done")
        s_step = sem("ff_dve_step")
        W320, DOWN0 = THIRDS, SLOTS

        def load(sp, g):
            for c in range(GU):
                sp.wait_ge(s_w32, (g - 1) * THIRDS + (c + 1) * 3 + W320)
                unit = bass.ds(g * GU + c, 1)
                sp.dma_start(codes[:, c].rearrange("p c n -> p (c n)"),
                             packed[unit].rearrange("a p c n -> p (a c n)")).then_inc(s_load[c], 16)
                sp.dma_start(scale[:, c].rearrange("p c n -> p (c n)"),
                             scales[unit].rearrange("a k c n -> k (a c n)").unsqueeze(1).to_broadcast([KS, P // KS, 3 * D])
                             ).then_inc(s_load[c], 16)

        def decode(dve, written, g, c):
            unit, third = c // 3, c % 3
            if third == 0:
                dve.wait_ge(s_load[unit], (g + 1) * 32)
            code = codes[:, unit, third].bitcast(U16).rearrange("p (n w) -> p n w", w=2)[:, :, 0]
            for e, nibble in enumerate((0, 4)):
                nc.vector.tensor_scalar(mag[:, e], code, 9 - nibble, 0x0E00, ALU.logical_shift_left, ALU.bitwise_and)
                last = nc.vector.tensor_scalar(sign[:, e], code, 12 - nibble, 0x8000, ALU.logical_shift_left, ALU.bitwise_and)
            written(last)
            written(nc.vector.tensor_tensor(mag[:], mag[:], sign[:], ALU.bitwise_or))
            nc.vector.tensor_tensor(w32[:, c % 2], mag[:].bitcast(F16), scale[:, unit, third].unsqueeze(1).to_broadcast([P, 2, D]),
                                    ALU.mult).then_inc(s_w32, 1)

        def decoded_hi(act, g, r, c):
            act.wait_ge(s_w32, g * THIRDS + c + 1 + W320)
            act.wait_ge(s_down, (g - 1) * SLOTS + DOWN0)
            nc.scalar.activation(w_hi[:, r, c // 3, c % 3], w32[:, c % 2], ACT.Copy, scale=W_FACTOR).then_inc(s_whi, 1)

        def decoded_lo(dve, g, r, c):
            dve.wait_ge(s_whi, g * THIRDS + c + 1)
            nc.vector.scalar_tensor_tensor(out=w_lo[:, r, c // 3, c % 3], in0=w32[:, c % 2], scalar=W_FACTOR,
                                           in1=w_hi[:, r, c // 3, c % 3], op0=ALU.mult, op1=ALU.subtract).then_inc(s_wlo, 1)

        with ExitStack() as pre:
            stats = pre.enter_context(nc.sbuf_tensor("ff_stats", [P, TILES, 6], F32))
            mv = pre.enter_context(nc.sbuf_tensor("ff_mean_var", [P, TILES, 2], F32))
            ve = pre.enter_context(nc.sbuf_tensor("ff_var_plus_eps", [P, TILES], F32))
            rstd = pre.enter_context(nc.sbuf_tensor("ff_rstd", [P, TILES], F32))
            half = pre.enter_context(nc.sbuf_tensor("ff_minus_half", [P, TILES], F32))
            RX = 4
            xn = pre.enter_context(nc.sbuf_tensor("ff_xn", [P, RX, D], F32))
            pT = [pre.enter_context(nc.psum_tensor(f"ff_p_xT{r}", [P, 2, 2, P], F32)) for r in range(RX)]
            s_stat = pre.enter_context(nc.semaphore("ff_variance"))
            s_rstd = pre.enter_context(nc.semaphore("ff_rstd_ready"))
            s_xn = pre.enter_context(nc.semaphore("ff_normed"))
            s_tr = pre.enter_context(nc.semaphore("ff_transposed"))
            s_xhi = pre.enter_context(nc.semaphore("ff_xT_hi_ready"))
            s_xlo = pre.enter_context(nc.semaphore("ff_xT_lo_ready"))
            s_first = pre.enter_context(nc.semaphore("ff_dve_first_steps"))
            with nc.Block() as block:
                @block.sync
                def _(sp):
                    load(sp, 0)

                @block.gpsimd
                def _(pool):
                    pool.memset(half[:], -0.5).then_inc(s_rstd, 1)
                    pool.wait_ge(s_rstd, 1)
                    pool.wait_ge(s_stat, 1)
                    nc.gpsimd.tensor_tensor(rstd[:], ve[:], half[:], ALU.pow).then_inc(s_rstd, 1)

                @block.tensor
                def _(pe):
                    pe.sem_inc(s_down, DOWN0)
                    for n in range(TILES):
                        pe.wait_ge(s_xn, n + 1)
                        if n >= RX:
                            pe.wait_ge(s_xlo, n - RX + 1)
                        for q in range(2):
                            for e in range(2):
                                last = nc.tensor.transpose(pT[n % RX][:, q, e, :],
                                                           xn[:, n % RX, q * 2 * P:(q + 1) * 2 * P].rearrange(
                                                               "p (j e) -> p j e", e=2)[:, :, e], ident)
                        last.then_inc(s_tr, 1)

                @block.scalar
                def _(act):
                    for n in range(TILES):
                        act.wait_ge(s_tr, n + 1)
                        nc.scalar.activation(xT_hi[:, :, :, n * P:(n + 1) * P].rearrange("p q e t -> p (q e) t"),
                                             pT[n % RX][:].rearrange("p q e t -> p (q e) t"), ACT.Copy,
                                             scale=X_SCALE).then_inc(s_xhi, 1)
                    for c in range(THIRDS):
                        decoded_hi(act, 0, 0, c)

                @block.vector
                def _(dve):
                    dve.sem_inc(s_w32, W320)
                    firsts = [0]

                    def written(instruction):
                        firsts[0] += 1
                        instruction.then_inc(s_first, 1)
                        dve.wait_ge(s_first, firsts[0])

                    for n in range(TILES):
                        last = nc.vector.bn_stats(stats[:, n, :], X[:, n, :])
                    written(last)
                    for n in range(TILES):
                        last = nc.vector.bn_aggr(mv[:, n, :], stats[:, n, :])
                    written(last)
                    nc.vector.tensor_scalar(ve[:], mv[:, :, 1], EPS, None, ALU.add).then_inc(s_stat, 1)
                    dve.wait_ge(s_rstd, 2)

                    def normed(n):
                        if n >= RX:
                            dve.wait_ge(s_tr, n - RX + 1)
                        nc.vector.tensor_scalar(xn[:, n % RX, :], X[:, n, :], mv[:, n, 0:1], rstd[:, n:n + 1],
                                                ALU.subtract, ALU.mult).then_inc(s_xn, 1)

                    def low(n):
                        dve.wait_ge(s_xhi, n + 1)
                        tiles_ = (slice(None), slice(None), slice(None), slice(n * P, (n + 1) * P))
                        nc.vector.scalar_tensor_tensor(out=xT_lo[tiles_].rearrange("p q e t -> p (q e) t"),
                                                       in0=pT[n % RX][:].rearrange("p q e t -> p (q e) t"), scalar=X_SCALE,
                                                       in1=xT_hi[tiles_].rearrange("p q e t -> p (q e) t"),
                                                       op0=ALU.mult, op1=ALU.subtract).then_inc(s_xlo, 1)

                    for n in range(RX - 1):
                        normed(n)
                    for n in range(TILES):
                        if n + RX - 1 < TILES:
                            normed(n + RX - 1)
                        low(n)
                    for c in range(THIRDS):
                        decode(dve, written, 0, c)
                        decoded_lo(dve, 0, 0, c)

        cube = sb("ff_cubic", [P, 2, TW], F32)
        arg = sb("ff_tanh_arg", [P, 2, TW], F32)
        th = sb("ff_tanh", [P, 2, TW], F32)
        gated = sb("ff_gated", [P, 2, TW], F32)
        hidden = sb("ff_hidden", [P, 2, TW], F32)
        h_hi, h_lo = (sb(f"ff_hidden_{s}", [P, 2, TW], F16) for s in ("hi", "lo"))
        pG = [st.enter_context(nc.psum_tensor(f"ff_p_gate{r}", [P, TW], F32)) for r in range(2)]
        pU = [st.enter_context(nc.psum_tensor(f"ff_p_up{r}", [P, TW], F32)) for r in range(2)]
        pD = [st.enter_context(nc.psum_tensor(f"ff_p_down{r}", [P, D], F32)) for r in range(BT)]
        s_gate = sem("gate_done")
        s_up = sem("up_done")
        s_sq = sem("square_ready")
        s_arg = sem("tanh_arg_ready")
        s_th = sem("tanh_ready")
        s_h = sem("hidden_ready")
        s_hhi = sem("hidden_hi_ready")
        s_hlo = sem("hidden_lo_ready")
        s_acc = sem("down_added")
        s_out = sem("stored")
        H0, ARG0, ACC0 = 2, 2, 1
        DECODE_AT = {k: c for c, k in enumerate([k for k in range(SLOTS) if k % HC != 0][:THIRDS])}
        STEPS = 2 * SLOTS + 2 * THIRDS

        def over_groups(engine, body):
            with engine.Fori(0, GROUPS // 2 - 1) as i:
                for r in range(2):
                    body(i * 2 + r, r, False)
            for r in range(2):
                body(GROUPS - 2 + r, r, r == 1)

        with nc.Block() as block:
            @block.sync
            def _(sp):
                def body(g, r, last):
                    if not last:
                        load(sp, g + 1)

                over_groups(sp, body)
                for tb in range(TB):
                    sp.wait_ge(s_acc, ((GROUPS - 1) * TB + tb + 1) * BT + ACC0)
                    sp.dma_start(out.rearrange("b (t p) d -> p (b t) d", p=P)[:, tb * BT:(tb + 1) * BT, :],
                                 X[:, tb * BT:(tb + 1) * BT, :]).then_inc(s_out, 16)
                sp.wait_ge(s_out, 16 * TB)

            @block.tensor
            def _(pe):
                def gate_up(g, r, k):
                    n = g * SLOTS + k
                    tb, hc = k // HC, k % HC
                    tokens = slice(tb * TW, (tb + 1) * TW)
                    pe.wait_ge(s_h, n - 1 + H0)
                    if k == 0:
                        pe.wait_ge(s_wlo, (g + 1) * THIRDS)
                    for third, bank, done in ((0, pG, s_gate), (1, pU, s_up)):
                        m = 0
                        for q in range(2):
                            for e in range(2):
                                cols = slice(q * 2 * P + hc % 2 * P, q * 2 * P + hc % 2 * P + P)
                                for w, x_ in ((w_hi, xT_hi), (w_hi, xT_lo), (w_lo, xT_hi)):
                                    last = nc.tensor.matmul(bank[k % 2][:], w[:, r, hc // 2, third, e, cols], x_[:, q, e, tokens],
                                                            start=(m == 0), stop=(m == 11))
                                    m += 1
                        last.then_inc(done, 1)

                def down(g, r, k):
                    n = g * SLOTS + k
                    tb, hc = k // HC, k % HC
                    pe.wait_ge(s_hlo, n + 1)
                    if hc == 0:
                        pe.wait_ge(s_acc, (g * TB + tb) * BT + ACC0)
                    for t in range(BT):
                        tile = slice(t * P, (t + 1) * P)
                        for m, (h_, w) in enumerate(((h_hi, w_hi), (h_hi, w_lo), (h_lo, w_hi))):
                            last = nc.tensor.matmul(pD[t][:], h_[:, k % 2, tile], w[:, r, hc // 2, 2, hc % 2, :],
                                                    start=(hc == 0 and m == 0), stop=(hc == HC - 1 and m == 2))
                    last.then_inc(s_down, 1)

                gate_up(0, 0, 0)

                def body(g, r, last):
                    for k in range(SLOTS):
                        if k + 1 < SLOTS:
                            gate_up(g, r, k + 1)
                        elif not last:
                            gate_up(g + 1, 1 - r, 0)
                        down(g, r, k)

                over_groups(pe, body)

            @block.scalar
            def _(act):
                def body(g, r, last):
                    for k in range(SLOTS):
                        n = g * SLOTS + k
                        s_ = k % 2
                        act.wait_ge(s_gate, n + 1)
                        act.wait_ge(s_arg, n - 1 + ARG0)
                        nc.scalar.activation(cube[:, s_], pG[s_][:], ACT.Square, scale=GU_OUT).then_inc(s_sq, 1)
                        if k in DECODE_AT and not last:
                            decoded_hi(act, g + 1, 1 - r, DECODE_AT[k])
                        act.wait_ge(s_arg, n + 1 + ARG0)
                        act.wait_ge(s_h, n - 1 + H0)
                        nc.scalar.activation(th[:, s_], arg[:, s_], ACT.Tanh).then_inc(s_th, 1)
                        act.wait_ge(s_h, n + 1 + H0)
                        act.wait_ge(s_down, n - 1 + DOWN0)
                        nc.scalar.activation(h_hi[:, s_], hidden[:, s_], ACT.Copy).then_inc(s_hhi, 1)

                over_groups(act, body)

            @block.vector
            def _(dve):
                for s_, n in ((s_h, H0), (s_arg, ARG0), (s_acc, ACC0)):
                    dve.sem_inc(s_, n)

                def add_block(g, tb):
                    dve.wait_ge(s_down, g * SLOTS + (tb + 1) * HC + DOWN0)
                    for t in range(BT):
                        row = X[:, tb * BT + t, :]
                        nc.vector.scalar_tensor_tensor(out=row, in0=pD[t][:], scalar=1.0 / (W_SCALE * HIDDEN_SCALE), in1=row,
                                                       op0=ALU.mult, op1=ALU.add).then_inc(s_acc, 1)

                def body(g, r, last):
                    steps = [0]

                    def written(instruction):
                        steps[0] += 1
                        instruction.then_inc(s_step, 1)
                        dve.wait_ge(s_step, g * STEPS + steps[0])

                    for k in range(SLOTS):
                        n = g * SLOTS + k
                        s_ = k % 2
                        dve.wait_ge(s_sq, n + 1)
                        written(nc.vector.tensor_scalar(cube[:, s_], cube[:, s_], CUBIC * ROOT, ROOT, ALU.mult, ALU.add))
                        nc.vector.scalar_tensor_tensor(out=arg[:, s_], in0=pG[s_][:], scalar=GU_OUT, in1=cube[:, s_],
                                                       op0=ALU.mult, op1=ALU.mult).then_inc(s_arg, 1)
                        if k in DECODE_AT and not last:
                            decode(dve, written, g + 1, DECODE_AT[k])
                        dve.wait_ge(s_th, n + 1)
                        written(nc.vector.scalar_tensor_tensor(out=gated[:, s_], in0=th[:, s_], scalar=1.0, in1=pG[s_][:],
                                                               op0=ALU.add, op1=ALU.mult))
                        dve.wait_ge(s_up, n + 1)
                        nc.vector.scalar_tensor_tensor(out=hidden[:, s_], in0=pU[s_][:], scalar=0.5 * GU_OUT ** 2 * HIDDEN_SCALE,
                                                       in1=gated[:, s_], op0=ALU.mult, op1=ALU.mult).then_inc(s_h, 1)
                        if k in DECODE_AT and not last:
                            decoded_lo(dve, g + 1, 1 - r, DECODE_AT[k])
                        dve.wait_ge(s_hhi, n + 1)
                        nc.vector.tensor_tensor(h_lo[:, s_], hidden[:, s_], h_hi[:, s_], ALU.subtract).then_inc(s_hlo, 1)
                        if k and k % HC == 0:
                            add_block(g, k // HC - 1)
                    add_block(g, TB - 1)

                over_groups(dve, body)


def kernel(x, fside_S2_0, ctx_2048, L0_attn_W_c, L0_attn_b_c, L0_attn_W_d, L0_attn_b_d, L0_attn_W_o, L0_attn_b_o,
           L0_xattn_k, L0_ffn_gate_W_packed, L0_ffn_gate_scales, L0_ffn_up_W_packed, L0_ffn_up_scales,
           L0_ffn_down_W_packed, L0_ffn_down_scales):
    import numpy as np
    import concourse.bacc as bacc
    from concourse.bass_utils import run_bass_kernel_spmd

    rot = 2 * DH
    freq = (1.0 / 10000.0 ** (np.arange(0, rot, 2, dtype=np.float32) / np.float32(rot))).astype(np.float32)
    ang = (np.arange(S, dtype=np.float32)[None, :] * freq[:, None]).astype(np.float32)
    tables = np.zeros((P, T_COLS), np.float32)
    tables[:, T_COS:T_COS + S] = 1.0
    tables[0:DH, T_COS:T_COS + S] = np.cos(ang)
    tables[DH:rot, T_COS:T_COS + S] = np.cos(ang)
    tables[0:DH, T_SIN:T_SIN + S] = -np.sin(ang)
    tables[DH:rot, T_SIN:T_SIN + S] = np.sin(ang)
    tables[:, T_ID:T_ID + P] = np.eye(P)
    tables[:, T_GROUP:T_GROUP + P] = np.kron(np.eye(P // XH), np.ones((XH, XH)))
    tables[:, T_QMASK] = -(np.arange(P) // DH // 2)
    tables[:, T_KMASK] = -(np.arange(P) // DH % 2)

    def units(gate, up, down, per):
        g, u = (np.asarray(a).reshape(MLP // (2 * P), P, 2, 2, per).transpose(0, 4, 3, 2, 1) for a in (gate, up))
        d = np.asarray(down).T.reshape(MLP // (2 * P), per, D)
        g, u = (a.reshape(MLP // (2 * P), per, 2 * 2 * P) for a in (g, u))
        return np.ascontiguousarray(np.stack([g, u, d], axis=2))

    k = np.asarray(L0_xattn_k)
    padded = np.concatenate([np.zeros((XG, P - 1), k.dtype), k], axis=1)
    at = np.arange(D)[None, :] - np.arange(P)[:, None] + P - 1
    arrays = {
        "x": x, "ctx_natural_in": ctx_2048,
        "ctx_t": np.ascontiguousarray(np.asarray(ctx_2048).transpose(2, 0, 1)),
        "tables": tables,
        "wc": L0_attn_W_c, "bc": L0_attn_b_c, "wd": L0_attn_W_d,
        "bqk": np.ascontiguousarray(np.asarray(L0_attn_b_d)[:2 * D].reshape(2 * NH, DH).T),
        "bv": np.asarray(L0_attn_b_d)[2 * D:], "wo": L0_attn_W_o, "bo": L0_attn_b_o,
        "skip": np.asarray(fside_S2_0).reshape(TT, P).T,
        "toeplitz": np.ascontiguousarray(padded[:, at]),
        "packed": units(L0_ffn_gate_W_packed, L0_ffn_up_W_packed, L0_ffn_down_W_packed, P),
        "scales": units(L0_ffn_gate_scales, L0_ffn_up_scales, L0_ffn_down_scales, XH),
    }
    nc = bacc.Bacc("TRN2", target_bir_lowering=False, num_devices=1)
    arrays = {n: np.ascontiguousarray(a) for n, a in arrays.items()}
    args = [nc.dram_tensor(n, a.shape, mybir.dt.from_np(a.dtype), kind="ExternalInput").ap() for n, a in arrays.items()]
    out = nc.dram_tensor("out", (B, S, D), F32, kind="ExternalOutput").ap()
    program(nc, *args, out)
    r = run_bass_kernel_spmd(nc, [arrays], core_ids=[0])
    return r.results[0]["out"]
```

```python
from contextlib import ExitStack

import concourse.bass as bass
from concourse import mybir

P = 128
F32 = mybir.dt.float32
F16 = mybir.dt.float16
BF16 = mybir.dt.bfloat16
I32 = mybir.dt.int32
U16 = mybir.dt.uint16
ALU = mybir.AluOpType
ACT = mybir.ActivationFunctionType
AX_X = mybir.AxisListType.X

B, S, D = 8, 256, 512
DC = 128
NH, DH = 16, 32
KC = D // P
TT = S // P
XH = 8
XG = S // XH
MLP = 4096
EPS = 1e-5

X_SCALE = 2.0 ** 11
WC_SCALE = 2.0 ** 8
C_SCALE = 2.0 ** 4
WD_SCALE = 2.0 ** 8
QK_SCALE = 2.0 ** 2
V_SCALE = 2.0 ** 4
P_SCALE_LOG = 8 * 0.6931471805599453
O_SCALE = 2.0 ** 4
WO_SCALE = 2.0 ** 10
T_SCALE = 2.0 ** 10
KV_SCALE = 2.0 ** 4
W_SCALE = 2.0 ** 8
HIDDEN_SCALE = 2.0 ** -2
SOFTMAX_SCALE = float(DH) ** -0.5

T_COS, T_SIN, T_ID, T_GROUP, T_QMASK, T_KMASK = 0, S, 2 * S, 2 * S + P, 2 * S + 2 * P, 2 * S + 2 * P + 1
T_COLS = T_KMASK + 1


def program(nc, x, ctx_in, ctx_t, tables, wc, bc, wd, bqk, bv, wo, bo, skip, toeplitz,
            packed, scales, out):
    with ExitStack() as top:
        def sb(name, shape, dt, stack=top):
            return stack.enter_context(nc.sbuf_tensor(name, shape, dt))

        X = sb("residual", [P, B * TT, D], F32)
        tab = sb("tables_sb", [P, T_COLS], F32)
        with ExitStack() as mid:
            vT = sb("norm_t", [P, KC, B, S], F32, mid)
            cT = sb("ctx_transposed", [P, KC, B, S], F32, mid)
            attention(nc, X, vT, cT, tab, x, ctx_in, ctx_t, tables, wc, bc, wd, bqk, bv, wo, bo, skip)
            mixing(nc, X, vT, cT, toeplitz)
        feed_forward(nc, X, tab, packed, scales, out)


def attention(nc, X, vT, cT, tab, x, ctx_in, ctx_t, tables, wc, bc, wd, bqk, bv, wo, bo, skip):
    with ExitStack() as st:
        def sb(name, shape, dt):
            return st.enter_context(nc.sbuf_tensor(name, shape, dt))

        def ps(name):
            return st.enter_context(nc.psum_tensor(name, [P, D], F32))

        def sem(name):
            return st.enter_context(nc.semaphore(name))

        ident = tab[:, T_ID:T_ID + P]
        group = tab[:, T_GROUP:T_GROUP + P]
        qmask = tab[:, T_QMASK:T_QMASK + 1]
        kmask = tab[:, T_KMASK:T_KMASK + 1]

        wc_hi, wc_lo = (sb(f"wc_{s}", [P, KC, DC], F16) for s in ("hi", "lo"))
        wv_hi, wv_lo = (sb(f"wv_{s}", [P, D], F16) for s in ("hi", "lo"))
        w4_hi, w4_lo = (sb(f"w4_{s}", [P, 2 * NH, 4, DH], F16) for s in ("hi", "lo"))
        wo_hi, wo_lo = (sb(f"wo_{s}", [P, KC, D], F16) for s in ("hi", "lo"))
        bc_sb = sb("bc_sb", [P, 1], F32)
        bqk_sb = sb("bqk_sb", [P, 2 * NH], F32)
        bv_sb = sb("bv_sb", [P, D], F32)
        bo_sb = sb("bo_sb", [P, D], F32)
        skip_sb = sb("skip_sb", [P, TT], F32)
        half = sb("minus_half", [P, TT], F32)
        ident_bf = sb("ident_bf", [P, P], BF16)
        ones_bf = sb("ones_bf", [P, P], BF16)
        den_col = sb("den_col", [P, 1], F16)
        log_scale = sb("log_scale", [P, 1], F32)
        csw = sb("c_swapped", [P, S], F32)
        s_ctxn = [sem(f"ctx_loaded_{r}") for r in range(2)]

        s_x = [sem("x_first_loaded"), sem("x_rest_loaded")]
        with ExitStack() as setup:
            stage = setup.enter_context(nc.sbuf_tensor("weights_stage", [P, 4 * D], F32))
            wqk_hi, wqk_lo = (setup.enter_context(nc.sbuf_tensor(f"wqk_{s}", [P, 2 * D], F16)) for s in ("hi", "lo"))
            jobs = [(wc.rearrange("(c p) n -> p c n", p=P), wc_hi, wc_lo, KC * DC, WC_SCALE, DC),
                    (wd[:, 0:2 * D], wqk_hi, wqk_lo, 2 * D, WD_SCALE, None),
                    (wd[:, 2 * D:3 * D], wv_hi, wv_lo, D, WD_SCALE, None),
                    (wo.rearrange("(c p) n -> p c n", p=P), wo_hi, wo_lo, KC * D, WO_SCALE, D)]
            s_load = [setup.enter_context(nc.semaphore(f"weight_loaded_{i}")) for i in range(len(jobs))]
            s_small = setup.enter_context(nc.semaphore("small_loaded"))
            s_whi = setup.enter_context(nc.semaphore("weight_hi"))
            s_wlo = setup.enter_context(nc.semaphore("weight_lo"))
            at = [0, KC * DC, KC * DC + 2 * D, 0]

            def staged(j):
                n, width = jobs[j][3], jobs[j][5]
                a = stage[:, at[j]:at[j] + n]
                return a if width is None else a.rearrange("p (c n) -> p c n", n=width)

            x_tiles = x.rearrange("b (t p) d -> p (b t) d", p=P)
            with nc.Block() as block:
                @block.sync
                def _(sp):
                    sp.dma_start(X[:, 0:TT], x_tiles[:, 0:TT]).then_inc(s_x[0], 16)
                    sp.dma_start(tab[:], tables).then_inc(s_small, 16)
                    for j, job in enumerate(jobs):
                        if j == len(jobs) - 1:
                            sp.wait_ge(s_wlo, len(jobs) - 1)
                        sp.dma_start(staged(j), job[0]).then_inc(s_load[j], 16)
                    sp.dma_start(X[:, TT:], x_tiles[:, TT:]).then_inc(s_x[1], 16)

                @block.gpsimd
                def _(pool):
                    pool.memset(half[:], -0.5)
                    pool.memset(log_scale[:], P_SCALE_LOG)
                    pool.memset(ones_bf[:], 1.0)
                    pool.memset(csw[:], 0.0)
                    pool.memset(den_col[:], V_SCALE)

                @block.scalar
                def _(act):
                    act.dma_start(bc_sb[:], bc.rearrange("(p a) -> p a", a=1)).then_inc(s_small, 16)
                    for r in range(4):
                        act.dma_start(bqk_sb[r * DH:(r + 1) * DH, :], bqk).then_inc(s_small, 16)
                    for dst, src in ((bv_sb, bv), (bo_sb, bo)):
                        act.dma_start(dst[:], src.rearrange("(a n) -> a n", a=1).to_broadcast([P, D])).then_inc(s_small, 16)
                    act.dma_start(skip_sb[:], skip).then_inc(s_small, 16)
                    for j, job in enumerate(jobs):
                        act.wait_ge(s_load[j], 16)
                        nc.scalar.activation(job[1][:], staged(j), ACT.Copy, scale=job[4]).then_inc(s_whi, 1)

                @block.vector
                def _(dve):
                    for j, job in enumerate(jobs):
                        dve.wait_ge(s_whi, j + 1)
                        nc.vector.scalar_tensor_tensor(out=job[2][:], in0=staged(j), scalar=job[4], in1=job[1][:],
                                                       op0=ALU.mult, op1=ALU.subtract).then_inc(s_wlo, 1)
                        if j == 1:
                            dve.wait_ge(s_wlo, 2)
                            for r in range(4):
                                for one, four in ((wqk_hi, w4_hi), (wqk_lo, w4_lo)):
                                    nc.vector.tensor_copy(four[:, :, r, :], one[:].rearrange("p (n d) -> p n d", d=DH))
                    dve.wait_ge(s_small, 16 * 9)
                    nc.vector.tensor_copy(ident_bf[:], ident)
                    nc.vector.tensor_scalar(bqk_sb[:], bqk_sb[:], QK_SCALE, None, ALU.mult)
                    nc.vector.tensor_scalar(bv_sb[:], bv_sb[:], V_SCALE, None, ALU.mult)

        ctxn = sb("ctx_natural", [P, 2, TT, D], F32)
        stats = sb("stats", [P, TT, 6], F32)
        mv = sb("mean_var", [P, TT, 2], F32)
        ve = sb("var_plus_eps", [P, TT], F32)
        rstd = sb("rstd", [P, TT], F32)
        xn = sb("xn", [P, TT, D], F32)
        xT_hi, xT_lo = (sb(f"xT_{s}", [P, KC, S], F16) for s in ("hi", "lo"))
        c32 = sb("c32", [P, S], F32)
        c_hi, c_lo = (sb(f"c_{s}", [P, 2, S], F16) for s in ("hi", "lo"))
        v32 = sb("v32", [P, TT, D], F32)
        v_hi, v_lo = (sb(f"v_{s}", [P, 2, TT, D], F16) for s in ("hi", "lo"))
        QR, PR = 4, 4
        qk_hi = sb("qk_hi", [P, 2, 2, S], F16)
        qk32 = sb("qk32", [P, 2, 2, S], F32)
        qk = sb("qk", [P, QR, 2, S], F16)
        nmax = sb("minus_max", [P, 2, TT], F32)
        diag = sb("minus_max_diag", [P, 2, TT, P], BF16)
        p32 = sb("p32", [P, 2, TT, S], F32)
        p_hi, p_lo = (sb(f"p_{s}", [P, PR, TT, S], F16) for s in ("hi", "lo"))
        rden = sb("rden", [P, TT * NH], F32)
        o_n = sb("o_n", [P, TT, D], F32)
        oT_hi, oT_lo = (sb(f"oT_{s}", [P, KC, P], F16) for s in ("hi", "lo"))
        skt = sb("skip_term", [P, D], F32)
        xbo = sb("x_plus_bo", [P, TT, D], F32)

        pS, pST0, pST1, pO0, pO1, pH, pDen, pM = (
            ps(n) for n in ("p_scores", "p_scores_t0", "p_scores_t1", "p_o0", "p_o1", "p_qk", "p_den", "p_misc"))
        pST, pO = (pST0, pST1), (pO0, pO1)
        pSv = pS[:].rearrange("p (t k) -> p t k", t=TT)
        pSTv = [a[:].rearrange("p (t q) -> p t q", t=TT) for a in pST]
        pHv = pH[:].rearrange("p (a t) -> p a t", a=2)
        pMv = pM[:].rearrange("p (c t) -> p c t", c=KC)
        pDenv = pDen[:, 0:TT * NH].rearrange("p (t h) -> p t h", t=TT)

        s_stat = [sem(f"variance_{n}") for n in (1, 2)]
        s_rstd = [sem(f"rstd_ready_{n}") for n in (1, 2)]
        s_xn = sem("normed")
        s_pro = sem("prologue_product")
        s_epi = sem("epilogue_product")
        s_phi = sem("prologue_hi_half")
        s_xT = sem("xT_ready")
        s_rot = sem("c_rotated")
        s_c = sem("c_ready")
        s_v32 = sem("v32_ready")
        s_v = sem("v_ready")
        s_qk_mm = sem("qk_product")
        s_qk_act = sem("qk32_ready")
        s_qk_hi = sem("qk_hi_ready")
        s_qk = sem("qk_ready")
        s_s = sem("scores")
        s_nmax = sem("minus_max_ready")
        s_dg = sem("maxima_ready")
        s_st = sem("scores_t")
        s_e = sem("exp_done")
        s_ph = sem("p_hi_ready")
        s_pl = sem("p_lo_ready")
        s_pv = sem("weighted_done")
        s_on = sem("o_normed")
        s_ehi = sem("oT_hi_half")
        s_oT = sem("oT_ready")
        s_xbo = sem("bias_added")
        s_x1 = sem("x1_ready")
        s_vn = sem("v_normed")
        s_vT = sem("vT_written")
        s_x2 = sem("skip_added")
        s_pstep = sem("prologue_step")
        s_estep = sem("epilogue_step")
        s_passed = sem("wait_passed")
        s_cT = sem("ctx_t_loaded")

        pro = [("xT", 0), ("xT", 1), ("c", 0), ("v", 0), ("v", 1)]
        epi = [("oT", 0), ("wo", 0), ("oT", 1), ("wo", 1), ("vT", 0), ("sk", 0), ("vT", 1), ("sk", 1)]

        def pro_at(b, key):
            return b * len(pro) + pro.index(key) + 1

        def epi_at(b, key):
            return b * len(epi) + epi.index(key) + 1

        QK0, QKA0, DG0, ST0, E0, PL0, PV0, ON0, X10, X20 = 2, 1, 1, 4, 2, 2, 4, 2, 2, 4
        PSTEPS, ESTEPS = 5, 7
        LAG_S, LAG_ST, LAG_PV = 2, 3, 4

        def over_batches(engine, prologue, body):
            prologue(0, 0)
            body(0, 0, True, False, True, 0)
            with engine.Fori(0, B // 2 - 1) as i:
                body(i * 2 + 1, 1, True, True, True, i + 1)
                body(i * 2 + 2, 0, True, True, True, i + 1)
            body(B - 1, 1, True, True, False, B // 2)
            body(B, 0, False, True, False, B // 2)

        def is_first(b):
            return isinstance(b, int) and b == 0

        def head_at(b, parity, step, lag, heads, before):
            if step >= lag:
                return (b, parity, step - lag) if heads else None
            return (b - 1, 1 - parity, step - lag + NH) if before else None

        with nc.Block() as block:
            @block.sync
            def _(sp):
                def load(b, parity):
                    sp.dma_start(ctxn[:, parity], ctx_in[bass.ds(b, 1)].rearrange("a (t p) d -> p (a t) d", p=P)
                                 ).then_inc(s_ctxn[parity], 16)

                load(0, 0)
                load(1, 1)
                sp.dma_start(cT[:], ctx_t.rearrange("(c p) b s -> p c b s", p=P)).then_inc(s_cT, 16)
                with sp.Fori(0, B // 2 - 1) as i:
                    for r in range(2):
                        sp.wait_ge(s_x2, (i * 2 + r + 1) * TT + X20)
                        load(i * 2 + r + 2, r)
                sp.wait_ge(s_cT, 16)

            @block.gpsimd
            def _(pool):
                pool.sem_inc(s_pl, PL0)

                def power(n, b):
                    pool.wait_ge(s_stat[n], b + 1)
                    nc.gpsimd.tensor_tensor(rstd[:], ve[:], half[:], ALU.pow).then_inc(s_rstd[n], 1)

                def v_low(b, parity, t):
                    pool.wait_ge(s_phi, pro_at(b, ("v", t)))
                    nc.gpsimd.tensor_tensor(v_lo[:, parity, t, :], v32[:, t, :], v_hi[:, parity, t, :],
                                            ALU.subtract).then_inc(s_v, 1)

                def prologue(b, parity):
                    power(0, b)
                    for t in range(TT):
                        v_low(b, parity, t)

                def body(b, parity, heads, before, after, turn):
                    for step in range(NH):
                        if step == 0 and after:
                            power(0, b + 1)
                        at_ = head_at(b, parity, step, LAG_ST, heads, before)
                        if at_:
                            n = at_[0] * NH + at_[2]
                            r = at_[2]
                            pool.wait_ge(s_ph, n + 1)
                            nc.gpsimd.tensor_tensor(p_lo[:, r % PR], p32[:, r % 2], p_hi[:, r % PR],
                                                    ALU.subtract).then_inc(s_pl, 1)
                        if step in (1, 2) and before:
                            pool.wait_ge(s_x1, (b - 1) * TT + X10)
                            pool.sem_inc(s_passed, 1)
                            t = step - 1
                            nc.gpsimd.tensor_tensor(
                                xbo[:, t, :], X[:, bass.ds((b - 1) * TT + t, 1), :].rearrange("p a d -> p (a d)"),
                                bo_sb[:], ALU.add).then_inc(s_xbo, 1)
                        if step in (7, 8) and after:
                            v_low(b + 1, 1 - parity, step - 7)
                        if step == 10 and before:
                            power(1, b - 1)

                over_batches(pool, prologue, body)

            @block.tensor
            def _(pe):
                pe.sem_inc(s_st, ST0)
                pe.sem_inc(s_pv, PV0)

                def transposes(src, done):
                    for c in range(KC):
                        last = nc.tensor.transpose(pMv[:, c, :], src[:, c * P:(c + 1) * P], ident)
                    last.then_inc(done, 1)

                def to_xT(b, t):
                    if t == 0 and not is_first(b):
                        pe.wait_ge(s_v32, b * TT)
                        pe.wait_ge(s_x2, (b - 2) * TT + X20)
                    pe.wait_ge(s_xn, b * TT + t + 1)
                    if t:
                        pe.wait_ge(s_xT, b * TT + t)
                    transposes(xn[:, t, :], s_pro)

                def to_c(b):
                    pe.wait_ge(s_xT, b * TT + TT)
                    n = 0
                    for c in range(KC):
                        for w, m in ((wc_hi, xT_hi), (wc_hi, xT_lo), (wc_lo, xT_hi)):
                            last = nc.tensor.matmul(pM[:, 0:S], w[:, c, :], m[:, c, :], start=(n == 0), stop=(n == 3 * KC - 1))
                            n += 1
                    last.then_inc(s_pro, 1)

                def to_v(b, parity, t):
                    pe.wait_ge(s_c, b + 1)
                    if t:
                        pe.wait_ge(s_v32, b * TT + t)
                    for k, (w, m) in enumerate(((c_hi, wv_hi), (c_hi, wv_lo), (c_lo, wv_hi))):
                        last = nc.tensor.matmul(pM[:], w[:, parity, t * P:(t + 1) * P], m[:], start=(k == 0), stop=(k == 2))
                    last.then_inc(s_pro, 1)

                def prologue(b, parity):
                    for t in range(TT):
                        to_xT(b, t)
                    to_c(b)
                    for t in range(TT):
                        to_v(b, parity, t)

                def project(b, parity, h):
                    if h == 0:
                        pe.wait_ge(s_c, b + 1)
                    pe.wait_ge(s_qk_act, b * NH + h + QKA0)
                    for a in range(2):
                        for k, (w, m) in enumerate(((w4_hi, c_hi), (w4_hi, c_lo), (w4_lo, c_hi))):
                            last = nc.tensor.matmul(pHv[:, a, :], w[:, a * NH + h].rearrange("p r d -> p (r d)"), m[:, parity],
                                                    start=(k == 0), stop=(k == 2))
                    last.then_inc(s_qk_mm, 1)

                def scores(b, parity, h):
                    pe.wait_ge(s_qk, b * NH + h + 1 + QK0)
                    pe.wait_ge(s_dg, b * NH + h + DG0)
                    r = h % QR
                    for t in range(TT):
                        last = nc.tensor.matmul(pSv[:, t, :], qk[:, r, 0, t * P:(t + 1) * P], qk[:, r, 1, :],
                                                start=True, stop=True)
                    last.then_inc(s_s, 1)

                def scores_t(b, parity, h):
                    pe.wait_ge(s_dg, b * NH + h + 1 + DG0)
                    pe.wait_ge(s_e, b * NH + h - 1 + E0)
                    r = h % QR
                    for t in range(TT):
                        part = pSTv[h % 2][:, t, :]
                        nc.tensor.matmul(part, qk[:, r, 1, t * P:(t + 1) * P], qk[:, r, 0, :], start=True, stop=False)
                        last = nc.tensor.matmul(part, ones_bf[:], diag[:, h % 2].rearrange("p t q -> p (t q)"),
                                                start=False, stop=True)
                    last.then_inc(s_st, 1)

                def weighted(b, parity, h):
                    if h == 0:
                        pe.wait_ge(s_v, b * TT + TT)
                        pe.wait_ge(s_on, b * TT + ON0)
                    pe.wait_ge(s_pl, b * NH + h + 1 + PL0)
                    r = h % PR
                    for t in range(TT):
                        o_ = pO[t][:, h * DH:(h + 1) * DH]
                        n = 0
                        for c in range(TT):
                            ph, pl = (a[:, r, c, t * P:(t + 1) * P] for a in (p_hi, p_lo))
                            vh, vl = (a[:, parity, c, h * DH:(h + 1) * DH] for a in (v_hi, v_lo))
                            for w, v_ in ((ph, vh), (ph, vl), (pl, vh)):
                                nc.tensor.matmul(o_, w, v_, start=(n == 0), stop=(n == 3 * TT - 1))
                                n += 1
                        n = 0
                        for c in range(TT):
                            for a in (p_hi, p_lo):
                                last = nc.tensor.matmul(pDenv[:, t, h:h + 1], a[:, r, c, t * P:(t + 1) * P], den_col[:],
                                                        start=(n == 0), stop=(n == 2 * TT - 1))
                                n += 1
                    last.then_inc(s_pv, 1)

                def to_oT(b, t, after):
                    if t == 0:
                        pe.wait_ge(s_v32, (b + 2) * TT + TT if after else B * TT)
                        pe.wait_ge(s_x2, b * TT + X20)
                    else:
                        pe.wait_ge(s_x1, b * TT + t + X10)
                    pe.wait_ge(s_on, b * TT + t + 1 + ON0)
                    transposes(o_n[:, t, :], s_epi)

                def to_wo(b, t):
                    pe.wait_ge(s_oT, b * TT + t + 1)
                    n = 0
                    for c in range(KC):
                        for w, m in ((oT_hi, wo_hi), (oT_hi, wo_lo), (oT_lo, wo_hi)):
                            last = nc.tensor.matmul(pM[:], w[:, c, :], m[:, c, :], start=(n == 0), stop=(n == 3 * KC - 1))
                            n += 1
                    last.then_inc(s_epi, 1)

                def to_vT(b, t):
                    pe.wait_ge(s_vn, b * TT + t + 1)
                    pe.wait_ge(s_x1, b * TT + TT + X10)
                    if t:
                        pe.wait_ge(s_x2, b * TT + t + X20)
                    transposes(xn[:, t, :], s_epi)

                def to_skip(b, t):
                    pe.wait_ge(s_vT, b * TT + t + 1)
                    nc.tensor.matmul(pM[:], group, o_n[:, t, :], start=True, stop=True).then_inc(s_epi, 1)

                def body(b, parity, heads, before, after, turn):
                    for step in range(NH):
                        for lag, stage_ in ((LAG_ST, scores_t), (0, project), (LAG_S, scores), (LAG_PV, weighted)):
                            at_ = head_at(b, parity, step, lag, heads, before)
                            if at_:
                                stage_(*at_)
                        if after:
                            if step < TT:
                                to_xT(b + 1, step)
                            if step == 2:
                                to_c(b + 1)
                            if step in (4, 5):
                                to_v(b + 1, 1 - parity, step - 4)
                        if before:
                            if step in (6, 8):
                                to_oT(b - 1, (step - 6) // 2, after)
                            if step in (7, 9):
                                to_wo(b - 1, (step - 7) // 2)
                            if step in (11, 13):
                                to_vT(b - 1, (step - 11) // 2)
                            if step in (12, 14):
                                to_skip(b - 1, (step - 12) // 2)

                over_batches(pe, prologue, body)

            @block.scalar
            def _(act):
                act.sem_inc(s_qk_act, QKA0)
                act.sem_inc(s_e, E0)

                def xT_high(b, t):
                    act.wait_ge(s_pro, pro_at(b, ("xT", t)))
                    nc.scalar.activation(xT_hi[:, :, t * P:(t + 1) * P], pMv, ACT.Copy, scale=X_SCALE).then_inc(s_phi, 1)

                def c_high(b, parity):
                    act.wait_ge(s_rot, b + 1)
                    nc.scalar.activation(c_hi[:, parity], c32[:], ACT.Copy, scale=C_SCALE).then_inc(s_phi, 1)

                def v_high(b, parity, t):
                    act.wait_ge(s_v32, b * TT + t + 1)
                    if not is_first(b):
                        act.wait_ge(s_pv, (b - 1) * NH + PV0)
                    nc.scalar.activation(v_hi[:, parity, t, :], v32[:, t, :], ACT.Copy).then_inc(s_phi, 1)

                def prologue(b, parity):
                    for t in range(TT):
                        xT_high(b, t)
                    c_high(b, parity)
                    for t in range(TT):
                        v_high(b, parity, t)

                def evacuate(b, parity, h):
                    n = b * NH + h
                    act.wait_ge(s_qk_mm, n + 1)
                    act.wait_ge(s_qk, n - 1 + QK0)
                    for a in range(2):
                        last = nc.scalar.activation(qk32[:, h % 2, a, :], pHv[:, a, :], ACT.Identity,
                                                    bias=bqk_sb[:, a * NH + h:a * NH + h + 1],
                                                    scale=QK_SCALE / (C_SCALE * WD_SCALE))
                    last.then_inc(s_qk_act, 1)

                def qk_high(b, parity, h):
                    n = b * NH + h
                    act.wait_ge(s_qk_act, n + 1 + QKA0)
                    nc.scalar.activation(qk_hi[:, h % 2], qk32[:, h % 2], ACT.Copy).then_inc(s_qk_hi, 1)

                def exponentials(b, parity, h):
                    n = b * NH + h
                    act.wait_ge(s_st, n + 1 + ST0)
                    act.wait_ge(s_pl, n - 1 + PL0)
                    nc.scalar.activation(p32[:, h % 2].rearrange("p t q -> p (t q)"), pST[h % 2][:], ACT.Exp,
                                         bias=log_scale[:, 0:1], scale=SOFTMAX_SCALE / QK_SCALE ** 2).then_inc(s_e, 1)

                def p_high(b, parity, h):
                    n = b * NH + h
                    act.wait_ge(s_pv, n - 3 + PV0)
                    act.wait_ge(s_e, n + 1 + E0)
                    nc.scalar.activation(p_hi[:, h % PR], p32[:, h % 2], ACT.Copy).then_inc(s_ph, 1)

                def extras(b, parity, before, after, step):
                    if after:
                        if step in (1, 2):
                            xT_high(b + 1, step - 1)
                        if step == 4:
                            c_high(b + 1, 1 - parity)
                        if step in (6, 7):
                            v_high(b + 1, 1 - parity, step - 6)
                    if before:
                        if step in (7, 9):
                            act.wait_ge(s_epi, epi_at(b - 1, ("oT", (step - 7) // 2)))
                            nc.scalar.activation(oT_hi[:], pMv, ACT.Copy, scale=O_SCALE).then_inc(s_ehi, 1)
                        if step in (12, 14):
                            t = (step - 12) // 2
                            act.wait_ge(s_epi, epi_at(b - 1, ("vT", t)))
                            nc.scalar.activation(
                                vT[:, :, bass.ds(b - 1, 1), t * P:(t + 1) * P].rearrange("p c a s -> p c (a s)"), pMv,
                                ACT.Copy).then_inc(s_vT, 1)

                def body(b, parity, heads, before, after, turn):
                    for step in range(NH):
                        extras(b, parity, before, after, step)
                        at_ = head_at(b, parity, step, LAG_ST, heads, before)
                        if at_:
                            exponentials(*at_)
                        if heads:
                            evacuate(b, parity, step)
                        if at_:
                            p_high(*at_)
                        if heads:
                            qk_high(b, parity, step)

                over_batches(act, prologue, body)

            @block.vector
            def _(dve):
                for s_, n in ((s_qk, QK0), (s_dg, DG0), (s_on, ON0), (s_x1, X10), (s_x2, X20)):
                    dve.sem_inc(s_, n)

                def writer(s_, base, total):
                    count = [0]

                    def written(instruction):
                        count[0] += 1
                        assert count[0] <= total
                        instruction.then_inc(s_, 1)
                        dve.wait_ge(s_, base + count[0])

                    return written

                def tile_of(b, t):
                    return X[:, bass.ds(b * TT + t, 1), :].rearrange("p a d -> p (a d)")

                def moments(b, n, written):
                    for t in range(TT):
                        last = nc.vector.bn_stats(stats[:, t, :], tile_of(b, t))
                    written(last)
                    dve.sem_inc(s_passed, 1)
                    for t in range(TT):
                        last = nc.vector.bn_aggr(mv[:, t, :], stats[:, t, :])
                    written(last)
                    nc.vector.tensor_scalar(ve[:], mv[:, :, 1], EPS, None, ALU.add).then_inc(s_stat[n], 1)

                def normed(b, t):
                    return nc.vector.tensor_scalar(xn[:, t, :], tile_of(b, t), mv[:, t, 0:1], rstd[:, t:t + 1],
                                                   ALU.subtract, ALU.mult)

                def first_norm(b, written):
                    moments(b, 0, written)
                    dve.wait_ge(s_rstd[0], b + 1)
                    for t in range(TT):
                        normed(b, t).then_inc(s_xn, 1)

                def xT_low(b, t):
                    dve.wait_ge(s_phi, pro_at(b, ("xT", t)))
                    nc.vector.scalar_tensor_tensor(out=xT_lo[:, :, t * P:(t + 1) * P], in0=pMv, scalar=X_SCALE,
                                                   in1=xT_hi[:, :, t * P:(t + 1) * P],
                                                   op0=ALU.mult, op1=ALU.subtract).then_inc(s_xT, 1)

                def rotate(b, written):
                    dve.wait_ge(s_pro, pro_at(b, ("c", 0)))
                    written(nc.vector.tensor_scalar(c32[:], pM[:, 0:S], 1.0 / (X_SCALE * WC_SCALE), bc_sb[:, 0:1],
                                                    ALU.mult, ALU.add))
                    nc.vector.tensor_copy(csw[0:DH, :], c32[DH:2 * DH, :])
                    written(nc.vector.tensor_copy(csw[DH:2 * DH, :], c32[0:DH, :]))
                    nc.vector.tensor_tensor(c32[:], c32[:], tab[:, T_COS:T_COS + S], ALU.mult)
                    written(nc.vector.tensor_tensor(csw[:], csw[:], tab[:, T_SIN:T_SIN + S], ALU.mult))
                    nc.vector.tensor_tensor(c32[:], c32[:], csw[:], ALU.add).then_inc(s_rot, 1)

                def c_low(b, parity):
                    dve.wait_ge(s_phi, pro_at(b, ("c", 0)))
                    nc.vector.scalar_tensor_tensor(out=c_lo[:, parity], in0=c32[:], scalar=C_SCALE, in1=c_hi[:, parity],
                                                   op0=ALU.mult, op1=ALU.subtract).then_inc(s_c, 1)

                def v_full(b, t):
                    dve.wait_ge(s_pro, pro_at(b, ("v", t)))
                    if not is_first(b):
                        dve.wait_ge(s_v, b * TT)
                    nc.vector.scalar_tensor_tensor(out=v32[:, t, :], in0=pM[:], scalar=V_SCALE / (C_SCALE * WD_SCALE),
                                                   in1=bv_sb[:], op0=ALU.mult, op1=ALU.add).then_inc(s_v32, 1)

                def prologue(b, parity):
                    dve.wait_ge(s_x[0], 16)
                    written = writer(s_pstep, b * PSTEPS, PSTEPS)
                    first_norm(b, written)
                    for t in range(TT):
                        xT_low(b, t)
                    rotate(b, written)
                    c_low(b, parity)
                    for t in range(TT):
                        v_full(b, t)

                def halves_of(b, parity, h):
                    n = b * NH + h
                    dve.wait_ge(s_qk_hi, n + 1)
                    dve.wait_ge(s_st, n - 3 + ST0)
                    for a, mask in ((0, qmask), (1, kmask)):
                        last = nc.vector.scalar_tensor_tensor(out=qk[:, h % QR, a, :], in0=qk_hi[:, h % 2, a, :], scalar=mask,
                                                              in1=qk32[:, h % 2, a, :], op0=ALU.mult, op1=ALU.add)
                    last.then_inc(s_qk, 1)

                def maxima(b, parity, h):
                    n = b * NH + h
                    dve.wait_ge(s_s, n + 1)
                    nc.vector.tensor_reduce(nmax[:, h % 2, :], pSv, AX_X, ALU.max, negate=True).then_inc(s_nmax, 1)
                    dve.wait_ge(s_nmax, n + 1)
                    dve.wait_ge(s_st, n - 1 + ST0)
                    for t in range(TT):
                        last = nc.vector.tensor_scalar(diag[:, h % 2, t, :], ident_bf[:], nmax[:, h % 2, t:t + 1], None,
                                                       ALU.mult)
                    last.then_inc(s_dg, 1)

                def divide(b, written):
                    dve.wait_ge(s_pv, b * NH + NH + PV0)
                    written(nc.vector.reciprocal(rden[:], pDen[:, 0:TT * NH]))
                    for t in range(TT):
                        nc.vector.tensor_tensor(
                            o_n[:, t, :].rearrange("p (h d) -> p h d", d=DH), pO[t][:].rearrange("p (h d) -> p h d", d=DH),
                            rden[:, t * NH:(t + 1) * NH].unsqueeze(2).to_broadcast([P, NH, DH]), ALU.mult).then_inc(s_on, 1)

                def oT_low(b, t):
                    dve.wait_ge(s_ehi, b * TT + t + 1)
                    nc.vector.scalar_tensor_tensor(out=oT_lo[:], in0=pMv, scalar=O_SCALE, in1=oT_hi[:],
                                                   op0=ALU.mult, op1=ALU.subtract).then_inc(s_oT, 1)

                def add_attention(b, t):
                    dve.wait_ge(s_xbo, b * TT + t + 1)
                    dve.wait_ge(s_epi, epi_at(b, ("wo", t)))
                    nc.vector.scalar_tensor_tensor(out=tile_of(b, t), in0=pM[:], scalar=1.0 / (O_SCALE * WO_SCALE),
                                                   in1=xbo[:, t, :], op0=ALU.mult, op1=ALU.add).then_inc(s_x1, 1)

                def second_norm(b, parity, written):
                    dve.wait_ge(s_rstd[1], b + 1)
                    for t in range(TT):
                        written(normed(b, t))
                        nc.vector.scalar_tensor_tensor(out=o_n[:, t, :], in0=xn[:, t, :], scalar=skip_sb[:, t:t + 1],
                                                       in1=ctxn[:, parity, t, :], op0=ALU.mult, op1=ALU.mult).then_inc(s_vn, 1)

                def add_skip(b, parity, t, written):
                    dve.wait_ge(s_epi, epi_at(b, ("sk", t)))
                    written(nc.vector.tensor_tensor(skt[:], pM[:], ctxn[:, parity, t, :], ALU.mult))
                    nc.vector.tensor_tensor(tile_of(b, t), tile_of(b, t), skt[:], ALU.add).then_inc(s_x2, 1)

                def body(b, parity, heads, before, after, turn):
                    pwritten = writer(s_pstep, (b + 1) * PSTEPS, PSTEPS)
                    ewritten = writer(s_estep, (b - 1) * ESTEPS, ESTEPS)
                    for step in range(NH):
                        if step == LAG_PV and before:
                            divide(b - 1, ewritten)
                        if after:
                            if step == 0:
                                if is_first(b):
                                    dve.wait_ge(s_x[1], 16)
                                first_norm(b + 1, pwritten)
                            if step in (1, 2):
                                xT_low(b + 1, step - 1)
                            if step == 3:
                                rotate(b + 1, pwritten)
                            if step == 4:
                                c_low(b + 1, 1 - parity)
                            if step in (5, 6):
                                v_full(b + 1, step - 5)
                        if before:
                            if step in (7, 9):
                                oT_low(b - 1, (step - 7) // 2)
                            if step in (8, 10):
                                add_attention(b - 1, (step - 8) // 2)
                            if step == 10:
                                dve.wait_ge(s_x1, (b - 1) * TT + TT + X10)
                                dve.sem_inc(s_passed, 1)
                                moments(b - 1, 1, ewritten)
                            if step == 11:
                                dve.wait_ge(s_ctxn[1 - parity], turn * 16)
                                second_norm(b - 1, 1 - parity, ewritten)
                            if step in (13, 15):
                                add_skip(b - 1, 1 - parity, (step - 13) // 2, ewritten)
                        at_ = head_at(b, parity, step, LAG_S, heads, before)
                        if at_:
                            maxima(*at_)
                        if heads:
                            halves_of(b, parity, step)

                over_batches(dve, prologue, body)


def mixing(nc, X, vT, cT, toeplitz):
    PAIRS = B * XH * XH
    CB = KC * B
    with ExitStack() as st:
        def sb(name, shape, dt):
            return st.enter_context(nc.sbuf_tensor(name, shape, dt))

        def sem(name):
            return st.enter_context(nc.semaphore(name))

        t32 = sb("toeplitz32", [P, 2, D], F32)
        t_hi, t_lo = (sb(f"toeplitz_{s}", [P, 2, D], F16) for s in ("hi", "lo"))
        kv32 = sb("pairs32", [P, 2, KC, PAIRS], F32)
        kv_hi, kv_lo = (sb(f"pairs_{s}", [P, 2, KC, PAIRS], F16) for s in ("hi", "lo"))
        z = sb("weighted_pairs", [P, 2, KC, PAIRS], F32)
        half1 = sb("sum_of_2", [P, CB, 4 * XH], F32)
        half2 = sb("sum_of_4", [P, CB, 2 * XH], F32)
        vT_cb = vT[:].rearrange("p c b s -> p (c b) s")
        cT_cb = cT[:].rearrange("p c b s -> p (c b) s")

        s_t32 = [sem(f"toeplitz_loaded_{r}") for r in range(2)]
        s_thi = sem("toeplitz_hi_ready")
        s_tlo = sem("toeplitz_lo_ready")
        s_kv = sem("pairs_ready")
        s_kvhi = sem("pairs_hi_ready")
        s_kvlo = sem("pairs_lo_ready")
        s_y = sem("convolved")
        s_z = sem("weighted_pairs_ready")
        s_sum = sem("summed")
        s_pool = sem("partial_sum")
        TLO0, KVLO0, Y0, Z0, SUM0 = 2, 2, 2 * KC, 2 * KC, 2

        with ExitStack() as banks:
            pY = [[banks.enter_context(nc.psum_tensor(f"p_conv{r}{c}", [P, PAIRS], F32)) for c in range(KC)]
                  for r in range(2)]
            with nc.Block() as block:
                @block.sync
                def _(sp):
                    with sp.Fori(0, XG // 2) as i:
                        for r in range(2):
                            g = i * 2 + r
                            sp.wait_ge(s_tlo, g - 1 + TLO0)
                            sp.dma_start(t32[:, r, :], toeplitz[bass.ds(g, 1)].rearrange("a p n -> p (a n)")
                                         ).then_inc(s_t32[r], 16)

                @block.tensor
                def _(pe):
                    pe.sem_inc(s_y, Y0)
                    with pe.Fori(0, XG // 2) as i:
                        for r in range(2):
                            g = i * 2 + r
                            pe.wait_ge(s_kvlo, g + 1 + KVLO0)
                            for c in range(KC):
                                pe.wait_ge(s_z, (g - 2) * KC + c + 1 + Z0)
                                n = 0
                                for m in range(c + 1):
                                    block_ = slice((c - m) * P, (c - m + 1) * P)
                                    for w, v_ in ((t_hi, kv_hi), (t_hi, kv_lo), (t_lo, kv_hi)):
                                        last = nc.tensor.matmul(pY[r][c][:], w[:, r, block_], v_[:, r, m, :],
                                                                start=(n == 0), stop=(n == 3 * c + 2))
                                        n += 1
                                last.then_inc(s_y, 1)

                @block.scalar
                def _(act):
                    with act.Fori(0, XG // 2) as i:
                        for r in range(2):
                            g = i * 2 + r
                            act.wait_ge(s_t32[r], (i + 1) * 16)
                            act.wait_ge(s_y, (g - 1) * KC + Y0)
                            nc.scalar.activation(t_hi[:, r, :], t32[:, r, :], ACT.Copy, scale=T_SCALE).then_inc(s_thi, 1)
                            act.wait_ge(s_kv, g + 1)
                            nc.scalar.activation(kv_hi[:, r], kv32[:, r], ACT.Copy, scale=KV_SCALE).then_inc(s_kvhi, 1)

                @block.gpsimd
                def _(pool):
                    pool.sem_inc(s_sum, SUM0)
                    with pool.Fori(0, XG // 2) as i:
                        for r in range(2):
                            g = i * 2 + r
                            zz = z[:, r].rearrange("p c (b n) -> p (c b) n", b=B)
                            pool.wait_ge(s_z, (g + 1) * KC + Z0)
                            nc.gpsimd.tensor_tensor(half1[:], zz[:, :, 0:4 * XH], zz[:, :, 4 * XH:8 * XH],
                                                    ALU.add).then_inc(s_pool, 1)
                            pool.wait_ge(s_pool, g * 2 + 1)
                            nc.gpsimd.tensor_tensor(half2[:], half1[:, :, 0:2 * XH], half1[:, :, 2 * XH:4 * XH],
                                                    ALU.add).then_inc(s_pool, 1)
                            pool.wait_ge(s_pool, g * 2 + 2)
                            nc.gpsimd.tensor_tensor(vT_cb[:, :, bass.ds(g * XH, XH)], half2[:, :, 0:XH],
                                                    half2[:, :, XH:2 * XH], ALU.add).then_inc(s_sum, 1)

                @block.vector
                def _(dve):
                    dve.sem_inc(s_tlo, TLO0)
                    dve.sem_inc(s_kvlo, KVLO0)
                    dve.sem_inc(s_z, Z0)

                    def pairs(g, r):
                        dve.wait_ge(s_kvlo, g - 1 + KVLO0)
                        v_, c_ = (a[:, :, bass.ds(g * XH, XH)] for a in (vT_cb, cT_cb))
                        nc.vector.tensor_tensor(kv32[:, r].rearrange("p c (b i j) -> p (c b) i j", i=XH, j=XH),
                                                v_.unsqueeze(3).to_broadcast([P, CB, XH, XH]),
                                                c_.unsqueeze(2).to_broadcast([P, CB, XH, XH]), ALU.mult).then_inc(s_kv, 1)

                    def low_halves(g, r):
                        dve.wait_ge(s_thi, g + 1)
                        nc.vector.scalar_tensor_tensor(out=t_lo[:, r, :], in0=t32[:, r, :], scalar=T_SCALE, in1=t_hi[:, r, :],
                                                       op0=ALU.mult, op1=ALU.subtract).then_inc(s_tlo, 1)
                        dve.wait_ge(s_kvhi, g + 1)
                        nc.vector.scalar_tensor_tensor(out=kv_lo[:, r], in0=kv32[:, r], scalar=KV_SCALE, in1=kv_hi[:, r],
                                                       op0=ALU.mult, op1=ALU.subtract).then_inc(s_kvlo, 1)

                    def weigh(g, r):
                        dve.wait_ge(s_sum, g - 1 + SUM0)
                        for c in range(KC):
                            dve.wait_ge(s_y, g * KC + c + 1 + Y0)
                            nc.vector.tensor_tensor(
                                z[:, r, c].rearrange("p (b i j) -> p b i j", i=XH, j=XH),
                                pY[r][c][:].rearrange("p (b i j) -> p b i j", i=XH, j=XH),
                                cT[:, c, :, bass.ds(g * XH, XH)].unsqueeze(3).to_broadcast([P, B, XH, XH]),
                                ALU.mult).then_inc(s_z, 1)

                    pairs(0, 0)
                    pairs(1, 1)
                    low_halves(0, 0)
                    with dve.Fori(0, XG // 2 - 1) as i:
                        for r in range(2):
                            pairs(i * 2 + r + 2, r)
                            low_halves(i * 2 + r + 1, (r + 1) % 2)
                            weigh(i * 2 + r, r)
                    low_halves(XG - 1, 1)
                    weigh(XG - 2, 0)
                    weigh(XG - 1, 1)

        s_back = sem("transposed_back")
        s_added = sem("mixing_added")
        with ExitStack() as banks:
            pT = [banks.enter_context(nc.psum_tensor(f"p_back{r}", [P, KC, P], F32)) for r in range(4)]
            ident = sb("ident_back", [P, P], F32)
            with nc.Block() as block:
                tiles = [(b, t) for b in range(B) for t in range(TT)]

                @block.sync
                def _(sp):
                    pass

                @block.gpsimd
                def _(pool):
                    pool.memset(ident[:], 0.0).then_inc(s_pool, 1)
                    pool.wait_ge(s_pool, 2 * XG + 1)
                    nc.gpsimd.affine_select(out=ident[:], in_=ident[:], compare_op=ALU.not_equal, fill=1.0, base=0,
                                            pattern=[[-1, P]], channel_multiplier=1).then_inc(s_pool, 1)

                @block.tensor
                def _(pe):
                    pe.wait_ge(s_pool, 2 * XG + 2)
                    for n, (b, t) in enumerate(tiles):
                        if n >= len(pT):
                            pe.wait_ge(s_added, n - len(pT) + 1)
                        for c in range(KC):
                            last = nc.tensor.transpose(pT[n % len(pT)][:, c, :], vT[:, c, b, t * P:(t + 1) * P], ident[:])
                        last.then_inc(s_back, 1)

                @block.vector
                def _(dve):
                    for n in range(len(tiles)):
                        dve.wait_ge(s_back, n + 1)
                        row = X[:, n, :]
                        nc.vector.scalar_tensor_tensor(out=row, in0=pT[n % len(pT)][:].rearrange("p c l -> p (c l)"),
                                                       scalar=1.0 / (T_SCALE * KV_SCALE), in1=row,
                                                       op0=ALU.mult, op1=ALU.add).then_inc(s_added, 1)


def feed_forward(nc, X, tab, packed, scales, out):
    UNITS = MLP // (2 * P)
    GU = 2
    GROUPS = UNITS // GU
    THIRDS = 3 * GU
    HC = 2 * GU
    TB = 4
    TW = B * S // TB
    BT = TW // P
    TILES = B * TT
    SLOTS = TB * HC
    KS = P // 16
    W_FACTOR = 2.0 ** 14 * W_SCALE
    GU_OUT = 1.0 / (X_SCALE * W_SCALE)
    ROOT, CUBIC = 0.7978845608028654, 0.044715
    with ExitStack() as st:
        def sb(name, shape, dt):
            return st.enter_context(nc.sbuf_tensor(name, shape, dt))

        def sem(name):
            return st.enter_context(nc.semaphore(name))

        ident = tab[:, T_ID:T_ID + P]
        xT_hi, xT_lo = (sb(f"ff_xT_{s}", [P, 2, 2, B * S], F16) for s in ("hi", "lo"))
        w_hi, w_lo = (sb(f"ff_w_{s}", [P, 2, GU, 3, 2, D], F16) for s in ("hi", "lo"))
        codes = sb("codes", [P, GU, 3, D], I32)
        scale = sb("code_scales", [P, GU, 3, D], F32)
        mag = sb("magnitude_bits", [P, 2, D], U16)
        sign = sb("sign_bits", [P, 2, D], U16)
        w32 = sb("weights32", [P, 2, 2, D], F32)
        s_load = [sem(f"unit_loaded_{r}") for r in range(GU)]
        s_w32 = sem("weights32_ready")
        s_whi = sem("w_hi_ready")
        s_wlo = sem("w_lo_ready")
        s_down = sem("down_done")
        s_step = sem("ff_dve_step")
        W320, DOWN0 = THIRDS, SLOTS

        def load(sp, g):
            for c in range(GU):
                sp.wait_ge(s_w32, (g - 1) * THIRDS + (c + 1) * 3 + W320)
                unit = bass.ds(g * GU + c, 1)
                sp.dma_start(codes[:, c].rearrange("p c n -> p (c n)"),
                             packed[unit].rearrange("a p c n -> p (a c n)")).then_inc(s_load[c], 16)
                sp.dma_start(scale[:, c].rearrange("p c n -> p (c n)"),
                             scales[unit].rearrange("a k c n -> k (a c n)").unsqueeze(1).to_broadcast([KS, P // KS, 3 * D])
                             ).then_inc(s_load[c], 16)

        def decode(dve, written, g, c):
            unit, third = c // 3, c % 3
            if third == 0:
                dve.wait_ge(s_load[unit], (g + 1) * 32)
            code = codes[:, unit, third].bitcast(U16).rearrange("p (n w) -> p n w", w=2)[:, :, 0]
            for e, nibble in enumerate((0, 4)):
                nc.vector.tensor_scalar(mag[:, e], code, 9 - nibble, 0x0E00, ALU.logical_shift_left, ALU.bitwise_and)
                last = nc.vector.tensor_scalar(sign[:, e], code, 12 - nibble, 0x8000, ALU.logical_shift_left, ALU.bitwise_and)
            written(last)
            written(nc.vector.tensor_tensor(mag[:], mag[:], sign[:], ALU.bitwise_or))
            nc.vector.tensor_tensor(w32[:, c % 2], mag[:].bitcast(F16), scale[:, unit, third].unsqueeze(1).to_broadcast([P, 2, D]),
                                    ALU.mult).then_inc(s_w32, 1)

        def decoded_hi(act, g, r, c):
            act.wait_ge(s_w32, g * THIRDS + c + 1 + W320)
            act.wait_ge(s_down, (g - 1) * SLOTS + DOWN0)
            nc.scalar.activation(w_hi[:, r, c // 3, c % 3], w32[:, c % 2], ACT.Copy, scale=W_FACTOR).then_inc(s_whi, 1)

        def decoded_lo(dve, g, r, c):
            dve.wait_ge(s_whi, g * THIRDS + c + 1)
            nc.vector.scalar_tensor_tensor(out=w_lo[:, r, c // 3, c % 3], in0=w32[:, c % 2], scalar=W_FACTOR,
                                           in1=w_hi[:, r, c // 3, c % 3], op0=ALU.mult, op1=ALU.subtract).then_inc(s_wlo, 1)

        with ExitStack() as pre:
            stats = pre.enter_context(nc.sbuf_tensor("ff_stats", [P, TILES, 6], F32))
            mv = pre.enter_context(nc.sbuf_tensor("ff_mean_var", [P, TILES, 2], F32))
            ve = pre.enter_context(nc.sbuf_tensor("ff_var_plus_eps", [P, TILES], F32))
            rstd = pre.enter_context(nc.sbuf_tensor("ff_rstd", [P, TILES], F32))
            half = pre.enter_context(nc.sbuf_tensor("ff_minus_half", [P, TILES], F32))
            RX = 4
            xn = pre.enter_context(nc.sbuf_tensor("ff_xn", [P, RX, D], F32))
            pT = [pre.enter_context(nc.psum_tensor(f"ff_p_xT{r}", [P, 2, 2, P], F32)) for r in range(RX)]
            s_stat = pre.enter_context(nc.semaphore("ff_variance"))
            s_rstd = pre.enter_context(nc.semaphore("ff_rstd_ready"))
            s_xn = pre.enter_context(nc.semaphore("ff_normed"))
            s_tr = pre.enter_context(nc.semaphore("ff_transposed"))
            s_xhi = pre.enter_context(nc.semaphore("ff_xT_hi_ready"))
            s_xlo = pre.enter_context(nc.semaphore("ff_xT_lo_ready"))
            s_first = pre.enter_context(nc.semaphore("ff_dve_first_steps"))
            with nc.Block() as block:
                @block.sync
                def _(sp):
                    load(sp, 0)

                @block.gpsimd
                def _(pool):
                    pool.memset(half[:], -0.5).then_inc(s_rstd, 1)
                    pool.wait_ge(s_rstd, 1)
                    pool.wait_ge(s_stat, 1)
                    nc.gpsimd.tensor_tensor(rstd[:], ve[:], half[:], ALU.pow).then_inc(s_rstd, 1)

                @block.tensor
                def _(pe):
                    pe.sem_inc(s_down, DOWN0)
                    for n in range(TILES):
                        pe.wait_ge(s_xn, n + 1)
                        if n >= RX:
                            pe.wait_ge(s_xlo, n - RX + 1)
                        for q in range(2):
                            for e in range(2):
                                last = nc.tensor.transpose(pT[n % RX][:, q, e, :],
                                                           xn[:, n % RX, q * 2 * P:(q + 1) * 2 * P].rearrange(
                                                               "p (j e) -> p j e", e=2)[:, :, e], ident)
                        last.then_inc(s_tr, 1)

                @block.scalar
                def _(act):
                    for n in range(TILES):
                        act.wait_ge(s_tr, n + 1)
                        nc.scalar.activation(xT_hi[:, :, :, n * P:(n + 1) * P].rearrange("p q e t -> p (q e) t"),
                                             pT[n % RX][:].rearrange("p q e t -> p (q e) t"), ACT.Copy,
                                             scale=X_SCALE).then_inc(s_xhi, 1)
                    for c in range(THIRDS):
                        decoded_hi(act, 0, 0, c)

                @block.vector
                def _(dve):
                    dve.sem_inc(s_w32, W320)
                    firsts = [0]

                    def written(instruction):
                        firsts[0] += 1
                        instruction.then_inc(s_first, 1)
                        dve.wait_ge(s_first, firsts[0])

                    for n in range(TILES):
                        last = nc.vector.bn_stats(stats[:, n, :], X[:, n, :])
                    written(last)
                    for n in range(TILES):
                        last = nc.vector.bn_aggr(mv[:, n, :], stats[:, n, :])
                    written(last)
                    nc.vector.tensor_scalar(ve[:], mv[:, :, 1], EPS, None, ALU.add).then_inc(s_stat, 1)
                    dve.wait_ge(s_rstd, 2)

                    def normed(n):
                        if n >= RX:
                            dve.wait_ge(s_tr, n - RX + 1)
                        nc.vector.tensor_scalar(xn[:, n % RX, :], X[:, n, :], mv[:, n, 0:1], rstd[:, n:n + 1],
                                                ALU.subtract, ALU.mult).then_inc(s_xn, 1)

                    def low(n):
                        dve.wait_ge(s_xhi, n + 1)
                        tiles_ = (slice(None), slice(None), slice(None), slice(n * P, (n + 1) * P))
                        nc.vector.scalar_tensor_tensor(out=xT_lo[tiles_].rearrange("p q e t -> p (q e) t"),
                                                       in0=pT[n % RX][:].rearrange("p q e t -> p (q e) t"), scalar=X_SCALE,
                                                       in1=xT_hi[tiles_].rearrange("p q e t -> p (q e) t"),
                                                       op0=ALU.mult, op1=ALU.subtract).then_inc(s_xlo, 1)

                    for n in range(RX - 1):
                        normed(n)
                    for n in range(TILES):
                        if n + RX - 1 < TILES:
                            normed(n + RX - 1)
                        low(n)
                    for c in range(THIRDS):
                        decode(dve, written, 0, c)
                        decoded_lo(dve, 0, 0, c)

        cube = sb("ff_cubic", [P, 2, TW], F32)
        arg = sb("ff_tanh_arg", [P, 2, TW], F32)
        th = sb("ff_tanh", [P, 2, TW], F32)
        gated = sb("ff_gated", [P, 2, TW], F32)
        hidden = sb("ff_hidden", [P, 2, TW], F32)
        h_hi, h_lo = (sb(f"ff_hidden_{s}", [P, 2, TW], F16) for s in ("hi", "lo"))
        pG = [st.enter_context(nc.psum_tensor(f"ff_p_gate{r}", [P, TW], F32)) for r in range(2)]
        pU = [st.enter_context(nc.psum_tensor(f"ff_p_up{r}", [P, TW], F32)) for r in range(2)]
        pD = [st.enter_context(nc.psum_tensor(f"ff_p_down{r}", [P, D], F32)) for r in range(BT)]
        s_gate = sem("gate_done")
        s_up = sem("up_done")
        s_sq = sem("square_ready")
        s_arg = sem("tanh_arg_ready")
        s_th = sem("tanh_ready")
        s_h = sem("hidden_ready")
        s_hhi = sem("hidden_hi_ready")
        s_hlo = sem("hidden_lo_ready")
        s_acc = sem("down_added")
        s_out = sem("stored")
        H0, ARG0, ACC0 = 2, 2, 1
        DECODE_AT = {k: c for c, k in enumerate([k for k in range(SLOTS) if k % HC != 0][:THIRDS])}
        STEPS = 2 * SLOTS + 2 * THIRDS

        def over_groups(engine, body):
            with engine.Fori(0, GROUPS // 2 - 1) as i:
                for r in range(2):
                    body(i * 2 + r, r, False)
            for r in range(2):
                body(GROUPS - 2 + r, r, r == 1)

        with nc.Block() as block:
            @block.sync
            def _(sp):
                def body(g, r, last):
                    if not last:
                        load(sp, g + 1)

                over_groups(sp, body)
                for tb in range(TB):
                    sp.wait_ge(s_acc, ((GROUPS - 1) * TB + tb + 1) * BT + ACC0)
                    sp.dma_start(out.rearrange("b (t p) d -> p (b t) d", p=P)[:, tb * BT:(tb + 1) * BT, :],
                                 X[:, tb * BT:(tb + 1) * BT, :]).then_inc(s_out, 16)
                sp.wait_ge(s_out, 16 * TB)

            @block.tensor
            def _(pe):
                def gate_up(g, r, k):
                    n = g * SLOTS + k
                    tb, hc = k // HC, k % HC
                    tokens = slice(tb * TW, (tb + 1) * TW)
                    pe.wait_ge(s_h, n - 1 + H0)
                    if k == 0:
                        pe.wait_ge(s_wlo, (g + 1) * THIRDS)
                    for third, bank, done in ((0, pG, s_gate), (1, pU, s_up)):
                        m = 0
                        for q in range(2):
                            for e in range(2):
                                cols = slice(q * 2 * P + hc % 2 * P, q * 2 * P + hc % 2 * P + P)
                                for w, x_ in ((w_hi, xT_hi), (w_hi, xT_lo), (w_lo, xT_hi)):
                                    last = nc.tensor.matmul(bank[k % 2][:], w[:, r, hc // 2, third, e, cols], x_[:, q, e, tokens],
                                                            start=(m == 0), stop=(m == 11))
                                    m += 1
                        last.then_inc(done, 1)

                def down(g, r, k):
                    n = g * SLOTS + k
                    tb, hc = k // HC, k % HC
                    pe.wait_ge(s_hlo, n + 1)
                    if hc == 0:
                        pe.wait_ge(s_acc, (g * TB + tb) * BT + ACC0)
                    for t in range(BT):
                        tile = slice(t * P, (t + 1) * P)
                        for m, (h_, w) in enumerate(((h_hi, w_hi), (h_hi, w_lo), (h_lo, w_hi))):
                            last = nc.tensor.matmul(pD[t][:], h_[:, k % 2, tile], w[:, r, hc // 2, 2, hc % 2, :],
                                                    start=(hc == 0 and m == 0), stop=(hc == HC - 1 and m == 2))
                    last.then_inc(s_down, 1)

                gate_up(0, 0, 0)

                def body(g, r, last):
                    for k in range(SLOTS):
                        if k + 1 < SLOTS:
                            gate_up(g, r, k + 1)
                        elif not last:
                            gate_up(g + 1, 1 - r, 0)
                        down(g, r, k)

                over_groups(pe, body)

            @block.scalar
            def _(act):
                def body(g, r, last):
                    for k in range(SLOTS):
                        n = g * SLOTS + k
                        s_ = k % 2
                        act.wait_ge(s_gate, n + 1)
                        act.wait_ge(s_arg, n - 1 + ARG0)
                        nc.scalar.activation(cube[:, s_], pG[s_][:], ACT.Square, scale=GU_OUT).then_inc(s_sq, 1)
                        if k in DECODE_AT and not last:
                            decoded_hi(act, g + 1, 1 - r, DECODE_AT[k])
                        act.wait_ge(s_arg, n + 1 + ARG0)
                        act.wait_ge(s_h, n - 1 + H0)
                        nc.scalar.activation(th[:, s_], arg[:, s_], ACT.Tanh).then_inc(s_th, 1)
                        act.wait_ge(s_h, n + 1 + H0)
                        act.wait_ge(s_down, n - 1 + DOWN0)
                        nc.scalar.activation(h_hi[:, s_], hidden[:, s_], ACT.Copy).then_inc(s_hhi, 1)

                over_groups(act, body)

            @block.vector
            def _(dve):
                for s_, n in ((s_h, H0), (s_arg, ARG0), (s_acc, ACC0)):
                    dve.sem_inc(s_, n)

                def add_block(g, tb):
                    dve.wait_ge(s_down, g * SLOTS + (tb + 1) * HC + DOWN0)
                    for t in range(BT):
                        row = X[:, tb * BT + t, :]
                        nc.vector.scalar_tensor_tensor(out=row, in0=pD[t][:], scalar=1.0 / (W_SCALE * HIDDEN_SCALE), in1=row,
                                                       op0=ALU.mult, op1=ALU.add).then_inc(s_acc, 1)

                def body(g, r, last):
                    steps = [0]

                    def written(instruction):
                        steps[0] += 1
                        instruction.then_inc(s_step, 1)
                        dve.wait_ge(s_step, g * STEPS + steps[0])

                    for k in range(SLOTS):
                        n = g * SLOTS + k
                        s_ = k % 2
                        dve.wait_ge(s_sq, n + 1)
                        written(nc.vector.tensor_scalar(cube[:, s_], cube[:, s_], CUBIC * ROOT, ROOT, ALU.mult, ALU.add))
                        nc.vector.scalar_tensor_tensor(out=arg[:, s_], in0=pG[s_][:], scalar=GU_OUT, in1=cube[:, s_],
                                                       op0=ALU.mult, op1=ALU.mult).then_inc(s_arg, 1)
                        if k in DECODE_AT and not last:
                            decode(dve, written, g + 1, DECODE_AT[k])
                        dve.wait_ge(s_th, n + 1)
                        written(nc.vector.scalar_tensor_tensor(out=gated[:, s_], in0=th[:, s_], scalar=1.0, in1=pG[s_][:],
                                                               op0=ALU.add, op1=ALU.mult))
                        dve.wait_ge(s_up, n + 1)
                        nc.vector.scalar_tensor_tensor(out=hidden[:, s_], in0=pU[s_][:], scalar=0.5 * GU_OUT ** 2 * HIDDEN_SCALE,
                                                       in1=gated[:, s_], op0=ALU.mult, op1=ALU.mult).then_inc(s_h, 1)
                        if k in DECODE_AT and not last:
                            decoded_lo(dve, g + 1, 1 - r, DECODE_AT[k])
                        dve.wait_ge(s_hhi, n + 1)
                        nc.vector.tensor_tensor(h_lo[:, s_], hidden[:, s_], h_hi[:, s_], ALU.subtract).then_inc(s_hlo, 1)
                        if k and k % HC == 0:
                            add_block(g, k // HC - 1)
                    add_block(g, TB - 1)

                over_groups(dve, body)


def kernel(x, fside_S2_0, ctx_2048, L0_attn_W_c, L0_attn_b_c, L0_attn_W_d, L0_attn_b_d, L0_attn_W_o, L0_attn_b_o,
           L0_xattn_k, L0_ffn_gate_W_packed, L0_ffn_gate_scales, L0_ffn_up_W_packed, L0_ffn_up_scales,
           L0_ffn_down_W_packed, L0_ffn_down_scales):
    import numpy as np
    import concourse.bacc as bacc
    from concourse.bass_utils import run_bass_kernel_spmd

    rot = 2 * DH
    freq = (1.0 / 10000.0 ** (np.arange(0, rot, 2, dtype=np.float32) / np.float32(rot))).astype(np.float32)
    ang = (np.arange(S, dtype=np.float32)[None, :] * freq[:, None]).astype(np.float32)
    tables = np.zeros((P, T_COLS), np.float32)
    tables[:, T_COS:T_COS + S] = 1.0
    tables[0:DH, T_COS:T_COS + S] = np.cos(ang)
    tables[DH:rot, T_COS:T_COS + S] = np.cos(ang)
    tables[0:DH, T_SIN:T_SIN + S] = -np.sin(ang)
    tables[DH:rot, T_SIN:T_SIN + S] = np.sin(ang)
    tables[:, T_ID:T_ID + P] = np.eye(P)
    tables[:, T_GROUP:T_GROUP + P] = np.kron(np.eye(P // XH), np.ones((XH, XH)))
    tables[:, T_QMASK] = -(np.arange(P) // DH // 2)
    tables[:, T_KMASK] = -(np.arange(P) // DH % 2)

    def units(gate, up, down, per):
        g, u = (np.asarray(a).reshape(MLP // (2 * P), P, 2, 2, per).transpose(0, 4, 3, 2, 1) for a in (gate, up))
        d = np.asarray(down).T.reshape(MLP // (2 * P), per, D)
        g, u = (a.reshape(MLP // (2 * P), per, 2 * 2 * P) for a in (g, u))
        return np.ascontiguousarray(np.stack([g, u, d], axis=2))

    k = np.asarray(L0_xattn_k)
    padded = np.concatenate([np.zeros((XG, P - 1), k.dtype), k], axis=1)
    at = np.arange(D)[None, :] - np.arange(P)[:, None] + P - 1
    arrays = {
        "x": x, "ctx_natural_in": ctx_2048,
        "ctx_t": np.ascontiguousarray(np.asarray(ctx_2048).transpose(2, 0, 1)),
        "tables": tables,
        "wc": L0_attn_W_c, "bc": L0_attn_b_c, "wd": L0_attn_W_d,
        "bqk": np.ascontiguousarray(np.asarray(L0_attn_b_d)[:2 * D].reshape(2 * NH, DH).T),
        "bv": np.asarray(L0_attn_b_d)[2 * D:], "wo": L0_attn_W_o, "bo": L0_attn_b_o,
        "skip": np.asarray(fside_S2_0).reshape(TT, P).T,
        "toeplitz": np.ascontiguousarray(padded[:, at]),
        "packed": units(L0_ffn_gate_W_packed, L0_ffn_up_W_packed, L0_ffn_down_W_packed, P),
        "scales": units(L0_ffn_gate_scales, L0_ffn_up_scales, L0_ffn_down_scales, XH),
    }
    nc = bacc.Bacc("TRN2", target_bir_lowering=False, num_devices=1)
    arrays = {n: np.ascontiguousarray(a) for n, a in arrays.items()}
    args = [nc.dram_tensor(n, a.shape, mybir.dt.from_np(a.dtype), kind="ExternalInput").ap() for n, a in arrays.items()]
    out = nc.dram_tensor("out", (B, S, D), F32, kind="ExternalOutput").ap()
    program(nc, *args, out)
    r = run_bass_kernel_spmd(nc, [arrays], core_ids=[0])
    return r.results[0]["out"]
```

```python
from contextlib import ExitStack

import concourse.bass as bass
from concourse import mybir

P = 128
F32 = mybir.dt.float32
F16 = mybir.dt.float16
BF16 = mybir.dt.bfloat16
I32 = mybir.dt.int32
U16 = mybir.dt.uint16
ALU = mybir.AluOpType
ACT = mybir.ActivationFunctionType
AX_X = mybir.AxisListType.X

B, S, D = 8, 256, 512
DC = 128
NH, DH = 16, 32
KC = D // P
TT = S // P
XH = 8
XG = S // XH
MLP = 4096
EPS = 1e-5

X_SCALE = 2.0 ** 11
WC_SCALE = 2.0 ** 8
C_SCALE = 2.0 ** 4
WD_SCALE = 2.0 ** 8
QK_SCALE = 2.0 ** 2
V_SCALE = 2.0 ** 4
P_SCALE_LOG = 8 * 0.6931471805599453
O_SCALE = 2.0 ** 4
WO_SCALE = 2.0 ** 10
T_SCALE = 2.0 ** 10
KV_SCALE = 2.0 ** 4
W_SCALE = 2.0 ** 8
HIDDEN_SCALE = 2.0 ** -2
SOFTMAX_SCALE = float(DH) ** -0.5

UNITS = MLP // (2 * P)
GU = 2
THIRDS = 3 * GU
FIRST_THIRDS = 2
KS = P // 16
W320 = THIRDS

T_COS, T_SIN, T_ID, T_GROUP, T_QMASK, T_KMASK = 0, S, 2 * S, 2 * S + P, 2 * S + 2 * P, 2 * S + 2 * P + 1
T_COLS = T_KMASK + 1


def program(nc, x, ctx_in, ctx_t, tables, wc, bc, wd, bqk, bv, wo, bo, skip, toeplitz,
            packed, scales, out):
    with ExitStack() as top:
        def sb(name, shape, dt, stack=top):
            return stack.enter_context(nc.sbuf_tensor(name, shape, dt))

        X = sb("residual", [P, B * TT, D], F32)
        tab = sb("tables_sb", [P, T_COLS], F32)
        with ExitStack() as mid:
            vT = sb("norm_t", [P, KC, B, S], F32, mid)
            cT = sb("ctx_transposed", [P, KC, B, S], F32, mid)
            attention(nc, X, vT, cT, tab, x, ctx_in, ctx_t, tables, wc, bc, wd, bqk, bv, wo, bo, skip)
            weights = Decoder(nc, mid, packed, scales)
            norm = Norm(nc, mid)
            mixing(nc, X, vT, cT, tab, weights, norm, toeplitz)
            feed_forward(nc, X, vT, cT, tab, weights, norm, out)


def attention(nc, X, vT, cT, tab, x, ctx_in, ctx_t, tables, wc, bc, wd, bqk, bv, wo, bo, skip):
    with ExitStack() as st:
        def sb(name, shape, dt):
            return st.enter_context(nc.sbuf_tensor(name, shape, dt))

        def ps(name):
            return st.enter_context(nc.psum_tensor(name, [P, D], F32))

        def sem(name):
            return st.enter_context(nc.semaphore(name))

        ident = tab[:, T_ID:T_ID + P]
        group = tab[:, T_GROUP:T_GROUP + P]
        qmask = tab[:, T_QMASK:T_QMASK + 1]
        kmask = tab[:, T_KMASK:T_KMASK + 1]

        wc_hi, wc_lo = (sb(f"wc_{s}", [P, KC, DC], F16) for s in ("hi", "lo"))
        wv_hi, wv_lo = (sb(f"wv_{s}", [P, D], F16) for s in ("hi", "lo"))
        w4_hi, w4_lo = (sb(f"w4_{s}", [P, 2 * NH, 4, DH], F16) for s in ("hi", "lo"))
        wo_hi, wo_lo = (sb(f"wo_{s}", [P, KC, D], F16) for s in ("hi", "lo"))
        bc_sb = sb("bc_sb", [P, 1], F32)
        bqk_sb = sb("bqk_sb", [P, 2 * NH], F32)
        bv_sb = sb("bv_sb", [P, D], F32)
        bo_sb = sb("bo_sb", [P, D], F32)
        skip_sb = sb("skip_sb", [P, TT], F32)
        half = sb("minus_half", [P, TT], F32)
        ident_bf = sb("ident_bf", [P, P], BF16)
        ones_bf = sb("ones_bf", [P, P], BF16)
        den_col = sb("den_col", [P, 1], F16)
        log_scale = sb("log_scale", [P, 1], F32)
        csw = sb("c_swapped", [P, S], F32)
        s_ctxn = [sem(f"ctx_loaded_{r}") for r in range(2)]

        wo32 = vT[:, 0].rearrange("p b s -> p (b s)").rearrange("p (c n) -> p c n", c=KC)
        s_wo, s_wo_hi = sem("wo_loaded"), sem("wo_hi_ready")

        s_x = [sem("x_first_loaded"), sem("x_rest_loaded")]
        with ExitStack() as setup:
            stage = setup.enter_context(nc.sbuf_tensor("weights_stage", [P, 4 * D], F32))
            wqk_hi, wqk_lo = (setup.enter_context(nc.sbuf_tensor(f"wqk_{s}", [P, 2 * D], F16)) for s in ("hi", "lo"))
            jobs = [(wc.rearrange("(c p) n -> p c n", p=P), wc_hi, wc_lo, KC * DC, WC_SCALE, DC),
                    (wd[:, 0:2 * D], wqk_hi, wqk_lo, 2 * D, WD_SCALE, None),
                    (wd[:, 2 * D:3 * D], wv_hi, wv_lo, D, WD_SCALE, None)]
            s_load = [setup.enter_context(nc.semaphore(f"weight_loaded_{i}")) for i in range(len(jobs))]
            s_small = setup.enter_context(nc.semaphore("small_loaded"))
            s_whi = setup.enter_context(nc.semaphore("weight_hi"))
            s_wlo = setup.enter_context(nc.semaphore("weight_lo"))
            at = [0, KC * DC, KC * DC + 2 * D]

            def staged(j):
                n, width = jobs[j][3], jobs[j][5]
                a = stage[:, at[j]:at[j] + n]
                return a if width is None else a.rearrange("p (c n) -> p c n", n=width)

            x_tiles = x.rearrange("b (t p) d -> p (b t) d", p=P)
            with nc.Block() as block:
                @block.sync
                def _(sp):
                    sp.dma_start(X[:, 0:TT], x_tiles[:, 0:TT]).then_inc(s_x[0], 16)
                    sp.dma_start(tab[:], tables).then_inc(s_small, 16)
                    for j, job in enumerate(jobs):
                        sp.dma_start(staged(j), job[0]).then_inc(s_load[j], 16)
                    sp.dma_start(wo32, wo.rearrange("(c p) n -> p c n", p=P)).then_inc(s_wo, 16)
                    sp.wait_ge(s_small, 16 * 9)
                    sp.dma_start(X[:, TT:], x_tiles[:, TT:]).then_inc(s_x[1], 16)

                @block.gpsimd
                def _(pool):
                    pool.memset(half[:], -0.5)
                    pool.memset(log_scale[:], P_SCALE_LOG)
                    pool.memset(ones_bf[:], 1.0)
                    pool.memset(csw[:], 0.0)
                    pool.memset(den_col[:], V_SCALE)

                @block.scalar
                def _(act):
                    act.dma_start(bc_sb[:], bc.rearrange("(p a) -> p a", a=1)).then_inc(s_small, 16)
                    for r in range(4):
                        act.dma_start(bqk_sb[r * DH:(r + 1) * DH, :], bqk).then_inc(s_small, 16)
                    for dst, src in ((bv_sb, bv), (bo_sb, bo)):
                        act.dma_start(dst[:], src.rearrange("(a n) -> a n", a=1).to_broadcast([P, D])).then_inc(s_small, 16)
                    act.dma_start(skip_sb[:], skip).then_inc(s_small, 16)
                    for j, job in enumerate(jobs):
                        act.wait_ge(s_load[j], 16)
                        nc.scalar.activation(job[1][:], staged(j), ACT.Copy, scale=job[4]).then_inc(s_whi, 1)

                @block.vector
                def _(dve):
                    for j, job in enumerate(jobs):
                        dve.wait_ge(s_whi, j + 1)
                        nc.vector.scalar_tensor_tensor(out=job[2][:], in0=staged(j), scalar=job[4], in1=job[1][:],
                                                       op0=ALU.mult, op1=ALU.subtract).then_inc(s_wlo, 1)
                        if j == 1:
                            dve.wait_ge(s_wlo, 2)
                            for r in range(4):
                                for one, four in ((wqk_hi, w4_hi), (wqk_lo, w4_lo)):
                                    nc.vector.tensor_copy(four[:, :, r, :], one[:].rearrange("p (n d) -> p n d", d=DH))
                    dve.wait_ge(s_small, 16 * 9)
                    nc.vector.tensor_copy(ident_bf[:], ident)
                    nc.vector.tensor_scalar(bqk_sb[:], bqk_sb[:], QK_SCALE, None, ALU.mult)
                    nc.vector.tensor_scalar(bv_sb[:], bv_sb[:], V_SCALE, None, ALU.mult)

        ctxn = sb("ctx_natural", [P, 2, TT, D], F32)
        stats = sb("stats", [P, TT, 6], F32)
        mv = sb("mean_var", [P, TT, 2], F32)
        ve = sb("var_plus_eps", [P, TT], F32)
        rstd = sb("rstd", [P, TT], F32)
        xn = sb("xn", [P, TT, D], F32)
        xT_hi, xT_lo = (sb(f"xT_{s}", [P, KC, S], F16) for s in ("hi", "lo"))
        c32 = sb("c32", [P, S], F32)
        c_hi, c_lo = (sb(f"c_{s}", [P, 2, S], F16) for s in ("hi", "lo"))
        v32 = sb("v32", [P, TT, D], F32)
        v_hi, v_lo = (sb(f"v_{s}", [P, 2, TT, D], F16) for s in ("hi", "lo"))
        QR, PR = 4, 4
        qk_hi = sb("qk_hi", [P, 2, 2, S], F16)
        qk32 = sb("qk32", [P, 2, 2, S], F32)
        qk = sb("qk", [P, QR, 2, S], F16)
        nmax = sb("minus_max", [P, 2, TT], F32)
        diag = sb("minus_max_diag", [P, 2, TT, P], BF16)
        p32 = sb("p32", [P, 2, TT, S], F32)
        p_hi, p_lo = (sb(f"p_{s}", [P, PR, TT, S], F16) for s in ("hi", "lo"))
        rden = sb("rden", [P, TT * NH], F32)
        o_n = sb("o_n", [P, TT, D], F32)
        oT_hi, oT_lo = (sb(f"oT_{s}", [P, KC, P], F16) for s in ("hi", "lo"))
        skt = sb("skip_term", [P, D], F32)
        xbo = sb("x_plus_bo", [P, TT, D], F32)

        pS, pST0, pST1, pO0, pO1, pH, pDen, pM = (
            ps(n) for n in ("p_scores", "p_scores_t0", "p_scores_t1", "p_o0", "p_o1", "p_qk", "p_den", "p_misc"))
        pST, pO = (pST0, pST1), (pO0, pO1)
        pSv = pS[:].rearrange("p (t k) -> p t k", t=TT)
        pSTv = [a[:].rearrange("p (t q) -> p t q", t=TT) for a in pST]
        pHv = pH[:].rearrange("p (a t) -> p a t", a=2)
        pMv = pM[:].rearrange("p (c t) -> p c t", c=KC)
        pDenv = pDen[:, 0:TT * NH].rearrange("p (t h) -> p t h", t=TT)

        s_stat = [sem(f"variance_{n}") for n in (1, 2)]
        s_rstd = [sem(f"rstd_ready_{n}") for n in (1, 2)]
        s_xn = sem("normed")
        s_pro = sem("prologue_product")
        s_epi = sem("epilogue_product")
        s_phi = sem("prologue_hi_half")
        s_xT = sem("xT_ready")
        s_rot = sem("c_rotated")
        s_c = sem("c_ready")
        s_v32 = sem("v32_ready")
        s_v = sem("v_ready")
        s_qk_mm = sem("qk_product")
        s_qk_act = sem("qk32_ready")
        s_qk_hi = sem("qk_hi_ready")
        s_qk = sem("qk_ready")
        s_s = sem("scores")
        s_nmax = sem("minus_max_ready")
        s_dg = sem("maxima_ready")
        s_st = sem("scores_t")
        s_e = sem("exp_done")
        s_ph = sem("p_hi_ready")
        s_pl = sem("p_lo_ready")
        s_pv = sem("weighted_done")
        s_on = sem("o_normed")
        s_ehi = sem("oT_hi_half")
        s_oT = sem("oT_ready")
        s_xbo = sem("bias_added")
        s_x1 = sem("x1_ready")
        s_vn = sem("v_normed")
        s_vT = sem("vT_written")
        s_x2 = sem("skip_added")
        s_pstep = sem("prologue_step")
        s_estep = sem("epilogue_step")
        s_passed = sem("wait_passed")
        s_cT = sem("ctx_t_loaded")

        pro = [("xT", 0), ("xT", 1), ("c", 0), ("v", 0), ("v", 1)]
        epi = [("oT", 0), ("wo", 0), ("oT", 1), ("wo", 1), ("vT", 0), ("sk", 0), ("vT", 1), ("sk", 1)]

        def pro_at(b, key):
            return b * len(pro) + pro.index(key) + 1

        def epi_at(b, key):
            return b * len(epi) + epi.index(key) + 1

        QK0, QKA0, DG0, ST0, E0, PL0, PV0, ON0, X10, X20 = 2, 1, 1, 4, 2, 2, 4, 2, 2, 4
        PSTEPS, ESTEPS = 5, 7
        LAG_Q, LAG_S, LAG_ST, LAG_PV = 1, 2, 4, 5

        def over_batches(engine, prologue, body):
            prologue(0, 0)
            body(0, 0, True, False, True, 0)
            with engine.Fori(0, B // 2 - 1) as i:
                body(i * 2 + 1, 1, True, True, True, i + 1)
                body(i * 2 + 2, 0, True, True, True, i + 1)
            body(B - 1, 1, True, True, False, B // 2)
            body(B, 0, False, True, False, B // 2)

        def is_first(b):
            return isinstance(b, int) and b == 0

        def head_at(b, parity, step, lag, heads, before):
            if step >= lag:
                return (b, parity, step - lag) if heads else None
            return (b - 1, 1 - parity, step - lag + NH) if before else None

        with nc.Block() as block:
            @block.sync
            def _(sp):
                def load(b, parity):
                    sp.dma_start(ctxn[:, parity], ctx_in[bass.ds(b, 1)].rearrange("a (t p) d -> p (a t) d", p=P)
                                 ).then_inc(s_ctxn[parity], 16)

                load(0, 0)
                load(1, 1)
                sp.dma_start(cT[:], ctx_t.rearrange("(c p) b s -> p c b s", p=P)).then_inc(s_cT, 16)
                with sp.Fori(0, B // 2 - 1) as i:
                    for r in range(2):
                        sp.wait_ge(s_x2, (i * 2 + r + 1) * TT + X20)
                        load(i * 2 + r + 2, r)
                sp.wait_ge(s_cT, 16)

            @block.gpsimd
            def _(pool):
                pool.sem_inc(s_pl, PL0)

                def power(n, b):
                    pool.wait_ge(s_stat[n], b + 1)
                    nc.gpsimd.tensor_tensor(rstd[:], ve[:], half[:], ALU.pow).then_inc(s_rstd[n], 1)

                def v_low(b, parity, t):
                    pool.wait_ge(s_phi, pro_at(b, ("v", t)))
                    nc.gpsimd.tensor_tensor(v_lo[:, parity, t, :], v32[:, t, :], v_hi[:, parity, t, :],
                                            ALU.subtract).then_inc(s_v, 1)

                def prologue(b, parity):
                    power(0, b)
                    for t in range(TT):
                        v_low(b, parity, t)

                def body(b, parity, heads, before, after, turn):
                    for step in range(NH):
                        if step == 0 and after:
                            power(0, b + 1)
                        at_ = head_at(b, parity, step, LAG_ST, heads, before)
                        if at_:
                            n = at_[0] * NH + at_[2]
                            r = at_[2]
                            pool.wait_ge(s_ph, n + 1)
                            nc.gpsimd.tensor_tensor(p_lo[:, r % PR], p32[:, r % 2], p_hi[:, r % PR],
                                                    ALU.subtract).then_inc(s_pl, 1)
                        if step in (1, 2) and before:
                            pool.wait_ge(s_x1, (b - 1) * TT + X10)
                            pool.sem_inc(s_passed, 1)
                            t = step - 1
                            nc.gpsimd.tensor_tensor(
                                xbo[:, t, :], X[:, bass.ds((b - 1) * TT + t, 1), :].rearrange("p a d -> p (a d)"),
                                bo_sb[:], ALU.add).then_inc(s_xbo, 1)
                        if step in (7, 8) and after:
                            v_low(b + 1, 1 - parity, step - 7)
                        if step == 10 and before:
                            power(1, b - 1)

                over_batches(pool, prologue, body)

            @block.tensor
            def _(pe):
                pe.sem_inc(s_st, ST0)
                pe.sem_inc(s_pv, PV0)

                def transposes(src, done):
                    for c in range(KC):
                        last = nc.tensor.transpose(pMv[:, c, :], src[:, c * P:(c + 1) * P], ident)
                    last.then_inc(done, 1)

                def to_xT(b, t):
                    if t == 0 and not is_first(b):
                        pe.wait_ge(s_v32, b * TT)
                        pe.wait_ge(s_x2, (b - 2) * TT + X20)
                    pe.wait_ge(s_xn, b * TT + t + 1)
                    if t:
                        pe.wait_ge(s_xT, b * TT + t)
                    transposes(xn[:, t, :], s_pro)

                def to_c(b):
                    pe.wait_ge(s_xT, b * TT + TT)
                    n = 0
                    for c in range(KC):
                        for w, m in ((wc_hi, xT_hi), (wc_hi, xT_lo), (wc_lo, xT_hi)):
                            last = nc.tensor.matmul(pM[:, 0:S], w[:, c, :], m[:, c, :], start=(n == 0), stop=(n == 3 * KC - 1))
                            n += 1
                    last.then_inc(s_pro, 1)

                def to_v(b, parity, t):
                    pe.wait_ge(s_c, b + 1)
                    if t:
                        pe.wait_ge(s_v32, b * TT + t)
                    for k, (w, m) in enumerate(((c_hi, wv_hi), (c_hi, wv_lo), (c_lo, wv_hi))):
                        last = nc.tensor.matmul(pM[:], w[:, parity, t * P:(t + 1) * P], m[:], start=(k == 0), stop=(k == 2))
                    last.then_inc(s_pro, 1)

                def prologue(b, parity):
                    for t in range(TT):
                        to_xT(b, t)
                    to_c(b)
                    for t in range(TT):
                        to_v(b, parity, t)

                def project(b, parity, h):
                    if h == 0:
                        pe.wait_ge(s_c, b + 1)
                    pe.wait_ge(s_qk_act, b * NH + h + QKA0)
                    for a in range(2):
                        for k, (w, m) in enumerate(((w4_hi, c_hi), (w4_hi, c_lo), (w4_lo, c_hi))):
                            last = nc.tensor.matmul(pHv[:, a, :], w[:, a * NH + h].rearrange("p r d -> p (r d)"), m[:, parity],
                                                    start=(k == 0), stop=(k == 2))
                    last.then_inc(s_qk_mm, 1)

                def scores(b, parity, h):
                    pe.wait_ge(s_qk, b * NH + h + 1 + QK0)
                    pe.wait_ge(s_dg, b * NH + h + DG0)
                    r = h % QR
                    for t in range(TT):
                        last = nc.tensor.matmul(pSv[:, t, :], qk[:, r, 0, t * P:(t + 1) * P], qk[:, r, 1, :],
                                                start=True, stop=True)
                    last.then_inc(s_s, 1)

                def scores_t(b, parity, h):
                    pe.wait_ge(s_dg, b * NH + h + 1 + DG0)
                    pe.wait_ge(s_e, b * NH + h - 1 + E0)
                    r = h % QR
                    for t in range(TT):
                        part = pSTv[h % 2][:, t, :]
                        nc.tensor.matmul(part, qk[:, r, 1, t * P:(t + 1) * P], qk[:, r, 0, :], start=True, stop=False)
                        last = nc.tensor.matmul(part, ones_bf[:], diag[:, h % 2].rearrange("p t q -> p (t q)"),
                                                start=False, stop=True)
                    last.then_inc(s_st, 1)

                def weighted(b, parity, h):
                    if h == 0:
                        pe.wait_ge(s_v, b * TT + TT)
                        pe.wait_ge(s_on, b * TT + ON0)
                    pe.wait_ge(s_pl, b * NH + h + 1 + PL0)
                    r = h % PR
                    for t in range(TT):
                        o_ = pO[t][:, h * DH:(h + 1) * DH]
                        n = 0
                        for c in range(TT):
                            ph, pl = (a[:, r, c, t * P:(t + 1) * P] for a in (p_hi, p_lo))
                            vh, vl = (a[:, parity, c, h * DH:(h + 1) * DH] for a in (v_hi, v_lo))
                            for w, v_ in ((ph, vh), (ph, vl), (pl, vh)):
                                nc.tensor.matmul(o_, w, v_, start=(n == 0), stop=(n == 3 * TT - 1))
                                n += 1
                        n = 0
                        for c in range(TT):
                            for a in (p_hi, p_lo):
                                last = nc.tensor.matmul(pDenv[:, t, h:h + 1], a[:, r, c, t * P:(t + 1) * P], den_col[:],
                                                        start=(n == 0), stop=(n == 2 * TT - 1))
                                n += 1
                    last.then_inc(s_pv, 1)

                def to_oT(b, t, after):
                    if t == 0:
                        pe.wait_ge(s_v32, (b + 2) * TT + TT if after else B * TT)
                        pe.wait_ge(s_x2, b * TT + X20)
                    else:
                        pe.wait_ge(s_x1, b * TT + t + X10)
                    pe.wait_ge(s_on, b * TT + t + 1 + ON0)
                    transposes(o_n[:, t, :], s_epi)

                def to_wo(b, t):
                    pe.wait_ge(s_oT, b * TT + t + 1)
                    n = 0
                    for c in range(KC):
                        for w, m in ((oT_hi, wo_hi), (oT_hi, wo_lo), (oT_lo, wo_hi)):
                            last = nc.tensor.matmul(pM[:], w[:, c, :], m[:, c, :], start=(n == 0), stop=(n == 3 * KC - 1))
                            n += 1
                    last.then_inc(s_epi, 1)

                def to_vT(b, t):
                    pe.wait_ge(s_vn, b * TT + t + 1)
                    pe.wait_ge(s_x1, b * TT + TT + X10)
                    if t:
                        pe.wait_ge(s_x2, b * TT + t + X20)
                    transposes(xn[:, t, :], s_epi)

                def to_skip(b, t):
                    pe.wait_ge(s_vT, b * TT + t + 1)
                    nc.tensor.matmul(pM[:], group, o_n[:, t, :], start=True, stop=True).then_inc(s_epi, 1)

                def body(b, parity, heads, before, after, turn):
                    for step in range(NH):
                        for lag, stage_ in ((LAG_ST, scores_t), (0, project), (LAG_S, scores), (LAG_PV, weighted)):
                            at_ = head_at(b, parity, step, lag, heads, before)
                            if at_:
                                stage_(*at_)
                        if after:
                            if step in (1, 2):
                                to_xT(b + 1, step - 1)
                            if step == 3:
                                to_c(b + 1)
                            if step in (4, 5):
                                to_v(b + 1, 1 - parity, step - 4)
                        if before:
                            if step in (6, 8):
                                to_oT(b - 1, (step - 6) // 2, after)
                            if step in (7, 9):
                                to_wo(b - 1, (step - 7) // 2)
                            if step in (11, 13):
                                to_vT(b - 1, (step - 11) // 2)
                            if step in (12, 14):
                                to_skip(b - 1, (step - 12) // 2)

                over_batches(pe, prologue, body)

            @block.scalar
            def _(act):
                act.sem_inc(s_qk_act, QKA0)
                act.sem_inc(s_e, E0)

                def xT_high(b, t):
                    act.wait_ge(s_pro, pro_at(b, ("xT", t)))
                    nc.scalar.activation(xT_hi[:, :, t * P:(t + 1) * P], pMv, ACT.Copy, scale=X_SCALE).then_inc(s_phi, 1)

                def c_high(b, parity):
                    act.wait_ge(s_rot, b + 1)
                    nc.scalar.activation(c_hi[:, parity], c32[:], ACT.Copy, scale=C_SCALE).then_inc(s_phi, 1)

                def v_high(b, parity, t):
                    act.wait_ge(s_v32, b * TT + t + 1)
                    if not is_first(b):
                        act.wait_ge(s_pv, (b - 1) * NH + PV0)
                    nc.scalar.activation(v_hi[:, parity, t, :], v32[:, t, :], ACT.Copy).then_inc(s_phi, 1)

                def prologue(b, parity):
                    for t in range(TT):
                        xT_high(b, t)
                    act.wait_ge(s_wo, 16)
                    nc.scalar.activation(wo_hi[:], wo32, ACT.Copy, scale=WO_SCALE).then_inc(s_wo_hi, 1)
                    c_high(b, parity)
                    for t in range(TT):
                        v_high(b, parity, t)

                def evacuate(b, parity, h):
                    n = b * NH + h
                    act.wait_ge(s_qk_mm, n + 1)
                    act.wait_ge(s_qk, n - 1 + QK0)
                    for a in range(2):
                        last = nc.scalar.activation(qk32[:, h % 2, a, :], pHv[:, a, :], ACT.Identity,
                                                    bias=bqk_sb[:, a * NH + h:a * NH + h + 1],
                                                    scale=QK_SCALE / (C_SCALE * WD_SCALE))
                    last.then_inc(s_qk_act, 1)

                def qk_high(b, parity, h):
                    n = b * NH + h
                    act.wait_ge(s_qk_act, n + 1 + QKA0)
                    nc.scalar.activation(qk_hi[:, h % 2], qk32[:, h % 2], ACT.Copy).then_inc(s_qk_hi, 1)

                def exponentials(b, parity, h):
                    n = b * NH + h
                    act.wait_ge(s_st, n + 1 + ST0)
                    act.wait_ge(s_pl, n - 1 + PL0)
                    nc.scalar.activation(p32[:, h % 2].rearrange("p t q -> p (t q)"), pST[h % 2][:], ACT.Exp,
                                         bias=log_scale[:, 0:1], scale=SOFTMAX_SCALE / QK_SCALE ** 2).then_inc(s_e, 1)

                def p_high(b, parity, h):
                    n = b * NH + h
                    act.wait_ge(s_pv, n - 3 + PV0)
                    act.wait_ge(s_e, n + 1 + E0)
                    nc.scalar.activation(p_hi[:, h % PR], p32[:, h % 2], ACT.Copy).then_inc(s_ph, 1)

                def extras(b, parity, before, after, step):
                    if after:
                        if step in (2, 3):
                            xT_high(b + 1, step - 2)
                    if before:
                        if step in (7, 9):
                            act.wait_ge(s_epi, epi_at(b - 1, ("oT", (step - 7) // 2)))
                            nc.scalar.activation(oT_hi[:], pMv, ACT.Copy, scale=O_SCALE).then_inc(s_ehi, 1)
                        if step in (12, 14):
                            t = (step - 12) // 2
                            act.wait_ge(s_epi, epi_at(b - 1, ("vT", t)))
                            nc.scalar.activation(
                                vT[:, :, bass.ds(b - 1, 1), t * P:(t + 1) * P].rearrange("p c a s -> p c (a s)"), pMv,
                                ACT.Copy, scale=KV_SCALE).then_inc(s_vT, 1)

                def body(b, parity, heads, before, after, turn):
                    for step in range(NH):
                        extras(b, parity, before, after, step)
                        at_ = head_at(b, parity, step, LAG_ST, heads, before)
                        if at_:
                            exponentials(*at_)
                        if after and step == 4:
                            c_high(b + 1, 1 - parity)
                        if after and step in (6, 7):
                            v_high(b + 1, 1 - parity, step - 6)
                        if heads:
                            evacuate(b, parity, step)
                        if at_:
                            p_high(*at_)
                        if heads:
                            qk_high(b, parity, step)

                over_batches(act, prologue, body)

            @block.vector
            def _(dve):
                for s_, n in ((s_qk, QK0), (s_dg, DG0), (s_on, ON0), (s_x1, X10), (s_x2, X20)):
                    dve.sem_inc(s_, n)

                def writer(s_, base, total):
                    count = [0]

                    def written(instruction):
                        count[0] += 1
                        assert count[0] <= total
                        instruction.then_inc(s_, 1)
                        dve.wait_ge(s_, base + count[0])

                    return written

                def tile_of(b, t):
                    return X[:, bass.ds(b * TT + t, 1), :].rearrange("p a d -> p (a d)")

                def moments(b, n, written):
                    for t in range(TT):
                        last = nc.vector.bn_stats(stats[:, t, :], tile_of(b, t))
                    written(last)
                    dve.sem_inc(s_passed, 1)
                    for t in range(TT):
                        last = nc.vector.bn_aggr(mv[:, t, :], stats[:, t, :])
                    written(last)
                    nc.vector.tensor_scalar(ve[:], mv[:, :, 1], EPS, None, ALU.add).then_inc(s_stat[n], 1)

                def normed(b, t):
                    return nc.vector.tensor_scalar(xn[:, t, :], tile_of(b, t), mv[:, t, 0:1], rstd[:, t:t + 1],
                                                   ALU.subtract, ALU.mult)

                def first_normed(b):
                    dve.wait_ge(s_rstd[0], b + 1)
                    for t in range(TT):
                        normed(b, t).then_inc(s_xn, 1)

                def xT_low(b, t):
                    dve.wait_ge(s_phi, pro_at(b, ("xT", t)))
                    nc.vector.scalar_tensor_tensor(out=xT_lo[:, :, t * P:(t + 1) * P], in0=pMv, scalar=X_SCALE,
                                                   in1=xT_hi[:, :, t * P:(t + 1) * P],
                                                   op0=ALU.mult, op1=ALU.subtract).then_inc(s_xT, 1)

                def rotate(b, written):
                    dve.wait_ge(s_pro, pro_at(b, ("c", 0)))
                    written(nc.vector.tensor_scalar(c32[:], pM[:, 0:S], 1.0 / (X_SCALE * WC_SCALE), bc_sb[:, 0:1],
                                                    ALU.mult, ALU.add))
                    nc.vector.tensor_copy(csw[0:DH, :], c32[DH:2 * DH, :])
                    written(nc.vector.tensor_copy(csw[DH:2 * DH, :], c32[0:DH, :]))
                    nc.vector.tensor_tensor(c32[:], c32[:], tab[:, T_COS:T_COS + S], ALU.mult)
                    written(nc.vector.tensor_tensor(csw[:], csw[:], tab[:, T_SIN:T_SIN + S], ALU.mult))
                    nc.vector.tensor_tensor(c32[:], c32[:], csw[:], ALU.add).then_inc(s_rot, 1)

                def c_low(b, parity):
                    dve.wait_ge(s_phi, pro_at(b, ("c", 0)))
                    nc.vector.scalar_tensor_tensor(out=c_lo[:, parity], in0=c32[:], scalar=C_SCALE, in1=c_hi[:, parity],
                                                   op0=ALU.mult, op1=ALU.subtract).then_inc(s_c, 1)

                def v_full(b, t):
                    dve.wait_ge(s_pro, pro_at(b, ("v", t)))
                    if not is_first(b):
                        dve.wait_ge(s_v, b * TT)
                    nc.vector.scalar_tensor_tensor(out=v32[:, t, :], in0=pM[:], scalar=V_SCALE / (C_SCALE * WD_SCALE),
                                                   in1=bv_sb[:], op0=ALU.mult, op1=ALU.add).then_inc(s_v32, 1)

                def prologue(b, parity):
                    dve.wait_ge(s_x[0], 16)
                    written = writer(s_pstep, b * PSTEPS, PSTEPS)
                    moments(b, 0, written)
                    first_normed(b)
                    for t in range(TT):
                        xT_low(b, t)
                    dve.wait_ge(s_wo_hi, 1)
                    nc.vector.scalar_tensor_tensor(out=wo_lo[:], in0=wo32, scalar=WO_SCALE, in1=wo_hi[:],
                                                   op0=ALU.mult, op1=ALU.subtract)
                    rotate(b, written)
                    c_low(b, parity)
                    for t in range(TT):
                        v_full(b, t)

                def halves_of(b, parity, h):
                    n = b * NH + h
                    dve.wait_ge(s_qk_hi, n + 1)
                    dve.wait_ge(s_st, n - 3 + ST0)
                    for a, mask in ((0, qmask), (1, kmask)):
                        last = nc.vector.scalar_tensor_tensor(out=qk[:, h % QR, a, :], in0=qk_hi[:, h % 2, a, :], scalar=mask,
                                                              in1=qk32[:, h % 2, a, :], op0=ALU.mult, op1=ALU.add)
                    last.then_inc(s_qk, 1)

                def maxima(b, parity, h):
                    n = b * NH + h
                    dve.wait_ge(s_s, n + 1)
                    nc.vector.tensor_reduce(nmax[:, h % 2, :], pSv, AX_X, ALU.max, negate=True).then_inc(s_nmax, 1)
                    dve.wait_ge(s_nmax, n + 1)
                    dve.wait_ge(s_st, n - 1 + ST0)
                    for t in range(TT):
                        last = nc.vector.tensor_scalar(diag[:, h % 2, t, :], ident_bf[:], nmax[:, h % 2, t:t + 1], None,
                                                       ALU.mult)
                    last.then_inc(s_dg, 1)

                def divide(b, written):
                    dve.wait_ge(s_pv, b * NH + NH + PV0)
                    written(nc.vector.reciprocal(rden[:], pDen[:, 0:TT * NH]))
                    for t in range(TT):
                        nc.vector.tensor_tensor(
                            o_n[:, t, :].rearrange("p (h d) -> p h d", d=DH), pO[t][:].rearrange("p (h d) -> p h d", d=DH),
                            rden[:, t * NH:(t + 1) * NH].unsqueeze(2).to_broadcast([P, NH, DH]), ALU.mult).then_inc(s_on, 1)

                def oT_low(b, t):
                    dve.wait_ge(s_ehi, b * TT + t + 1)
                    nc.vector.scalar_tensor_tensor(out=oT_lo[:], in0=pMv, scalar=O_SCALE, in1=oT_hi[:],
                                                   op0=ALU.mult, op1=ALU.subtract).then_inc(s_oT, 1)

                def add_attention(b, t):
                    dve.wait_ge(s_xbo, b * TT + t + 1)
                    dve.wait_ge(s_epi, epi_at(b, ("wo", t)))
                    nc.vector.scalar_tensor_tensor(out=tile_of(b, t), in0=pM[:], scalar=1.0 / (O_SCALE * WO_SCALE),
                                                   in1=xbo[:, t, :], op0=ALU.mult, op1=ALU.add).then_inc(s_x1, 1)

                def second_norm(b, parity, t, written):
                    dve.wait_ge(s_rstd[1], b + 1)
                    written(normed(b, t))
                    nc.vector.scalar_tensor_tensor(out=o_n[:, t, :], in0=xn[:, t, :], scalar=skip_sb[:, t:t + 1],
                                                   in1=ctxn[:, parity, t, :], op0=ALU.mult, op1=ALU.mult).then_inc(s_vn, 1)

                def add_skip(b, parity, t, written):
                    dve.wait_ge(s_epi, epi_at(b, ("sk", t)))
                    written(nc.vector.tensor_tensor(skt[:], pM[:], ctxn[:, parity, t, :], ALU.mult))
                    nc.vector.tensor_tensor(tile_of(b, t), tile_of(b, t), skt[:], ALU.add).then_inc(s_x2, 1)

                def body(b, parity, heads, before, after, turn):
                    pwritten = writer(s_pstep, (b + 1) * PSTEPS, PSTEPS)
                    ewritten = writer(s_estep, (b - 1) * ESTEPS, ESTEPS)
                    for step in range(NH):
                        if step == LAG_PV and before:
                            divide(b - 1, ewritten)
                        if after:
                            if step == 0:
                                if is_first(b):
                                    dve.wait_ge(s_x[1], 16)
                                moments(b + 1, 0, pwritten)
                            if step == 1:
                                first_normed(b + 1)
                            if step in (2, 3):
                                xT_low(b + 1, step - 2)
                            if step == 4:
                                rotate(b + 1, pwritten)
                            if step in (5, 6):
                                v_full(b + 1, step - 5)
                        if before:
                            if step in (7, 9):
                                oT_low(b - 1, (step - 7) // 2)
                            if step in (8, 10):
                                add_attention(b - 1, (step - 8) // 2)
                            if step == 10:
                                dve.wait_ge(s_x1, (b - 1) * TT + TT + X10)
                                dve.sem_inc(s_passed, 1)
                                moments(b - 1, 1, ewritten)
                            if step in (11, 12):
                                dve.wait_ge(s_ctxn[1 - parity], turn * 16)
                                second_norm(b - 1, 1 - parity, step - 11, ewritten)
                            if step in (13, 15):
                                add_skip(b - 1, 1 - parity, (step - 13) // 2, ewritten)
                        at_ = head_at(b, parity, step, LAG_S, heads, before)
                        if at_:
                            maxima(*at_)
                        if after and step == 4:
                            c_low(b + 1, 1 - parity)
                        at_ = head_at(b, parity, step, LAG_Q, heads, before)
                        if at_:
                            halves_of(*at_)

                over_batches(dve, prologue, body)


class Decoder:

    def __init__(self, nc, st, packed, scales):
        def sb(name, shape, dt):
            return st.enter_context(nc.sbuf_tensor(name, shape, dt))

        self.nc, self.packed, self.scales = nc, packed, scales
        self.codes = sb("codes", [P, GU, 3, D], I32)
        self.scale = sb("code_scales", [P, GU, 3, D], F32)
        self.mag = sb("magnitude_bits", [P, 2, D], U16)
        self.sign = sb("sign_bits", [P, 2, D], U16)
        self.w32 = sb("weights32", [P, 2, 2, D], F32)
        self.s_load = [st.enter_context(nc.semaphore(f"unit_loaded_{r}")) for r in range(GU)]
        self.s_w32 = st.enter_context(nc.semaphore("weights32_ready"))

    def load(self, sp, g):
        for c in range(GU):
            sp.wait_ge(self.s_w32, (g - 1) * THIRDS + (c + 1) * 3 + W320)
            unit = bass.ds(g * GU + c, 1)
            sp.dma_start(self.codes[:, c].rearrange("p c n -> p (c n)"),
                         self.packed[unit].rearrange("a p c n -> p (a c n)")).then_inc(self.s_load[c], 16)
            sp.dma_start(self.scale[:, c].rearrange("p c n -> p (c n)"),
                         self.scales[unit].rearrange("a k c n -> k (a c n)").unsqueeze(1).to_broadcast([KS, P // KS, 3 * D])
                         ).then_inc(self.s_load[c], 16)

    def bits(self, dve, g, c):
        unit, third = c // 3, c % 3
        if third == 0:
            dve.wait_ge(self.s_load[unit], (g + 1) * 32)
        dve.wait_ge(self.s_w32, g * THIRDS + c + W320)
        code = self.codes[:, unit, third].bitcast(U16).rearrange("p (n w) -> p n w", w=2)[:, :, 0]
        for e, nibble in enumerate((0, 4)):
            self.nc.vector.tensor_scalar(self.mag[:, e], code, 9 - nibble, 0x0E00, ALU.logical_shift_left, ALU.bitwise_and)
            last = self.nc.vector.tensor_scalar(self.sign[:, e], code, 12 - nibble, 0x8000, ALU.logical_shift_left,
                                                ALU.bitwise_and)
        return last

    def values(self):
        return self.nc.vector.tensor_tensor(self.mag[:], self.mag[:], self.sign[:], ALU.bitwise_or)

    def scaled(self, c):
        unit, third = c // 3, c % 3
        self.nc.vector.tensor_tensor(self.w32[:, c % 2], self.mag[:].bitcast(F16),
                                     self.scale[:, unit, third].unsqueeze(1).to_broadcast([P, 2, D]),
                                     ALU.mult).then_inc(self.s_w32, 1)


class Norm:
    QUARTER = B * TT // 4

    def __init__(self, nc, st):
        def sb(name, *shape):
            return st.enter_context(nc.sbuf_tensor(name, [P, *shape], F32))

        self.nc = nc
        tiles = B * TT
        self.stats = sb("ff_stats", tiles, 6)
        self.mv = sb("ff_mean_var", tiles, 2)
        self.ve = sb("ff_var_plus_eps", tiles)
        self.rstd = sb("ff_rstd", tiles)
        self.shift = sb("ff_minus_mean_rstd", tiles)
        self.half = sb("ff_minus_half", tiles)
        self.xn = sb("ff_xn", self.QUARTER, D)
        self.s_var = st.enter_context(nc.semaphore("ff_variance"))
        self.s_rstd = st.enter_context(nc.semaphore("ff_rstd_ready"))
        self.s_shift = st.enter_context(nc.semaphore("ff_shift_ready"))
        self.s_xn = st.enter_context(nc.semaphore("ff_normed"))

    def moments(self, X, n):
        return self.nc.vector.bn_stats(self.stats[:, n, :], X[:, n, :])

    def means(self, tiles):
        for n in tiles:
            last = self.nc.vector.bn_aggr(self.mv[:, n, :], self.stats[:, n, :])
        return last

    def tiles(self, q):
        return slice(q * self.QUARTER, (q + 1) * self.QUARTER)

    def variances(self, q):
        at = self.tiles(q)
        self.nc.vector.tensor_scalar(self.ve[:, at], self.mv[:, at, 1], EPS, None, ALU.add).then_inc(self.s_var, 1)

    def reciprocals(self, pool, q):
        at = self.tiles(q)
        pool.wait_ge(self.s_var, q + 1)
        self.nc.gpsimd.tensor_tensor(self.rstd[:, at], self.ve[:, at], self.half[:, at], ALU.pow).then_inc(self.s_rstd, 1)

    def shifts(self, dve, q):
        at = self.tiles(q)
        dve.wait_ge(self.s_rstd, q + 2)
        self.nc.vector.scalar_tensor_tensor(out=self.shift[:, at], in0=self.mv[:, at, 0], scalar=-1.0, in1=self.rstd[:, at],
                                            op0=ALU.mult, op1=ALU.mult).then_inc(self.s_shift, 1)

    def normed(self, X, n):
        self.nc.scalar.activation(self.xn[:, n % self.QUARTER, :], X[:, n, :], ACT.Identity,
                                  bias=self.shift[:, n:n + 1], scale=self.rstd[:, n:n + 1]).then_inc(self.s_xn, 1)


def mixing(nc, X, vT, cT, tab, weights, norm, toeplitz):
    PAIRS = B * XH * XH
    CB = KC * B
    POOL_PAIRS = PAIRS // 2
    with ExitStack() as st:
        def sb(name, shape, dt):
            return st.enter_context(nc.sbuf_tensor(name, shape, dt))

        def sem(name):
            return st.enter_context(nc.semaphore(name))

        t32 = sb("toeplitz32", [P, 2, D], F32)
        t_hi, t_lo = (sb(f"toeplitz_{s}", [P, 2, D], F16) for s in ("hi", "lo"))
        kv32 = sb("pairs32", [P, 2, KC, PAIRS], F32)
        kv_hi, kv_lo = (sb(f"pairs_{s}", [P, 2, KC, PAIRS], F16) for s in ("hi", "lo"))
        z = sb("weighted_pairs", [P, 2, KC, PAIRS], F32)
        half1 = sb("sum_of_2", [P, CB, 4 * XH], F32)
        half2 = sb("sum_of_4", [P, CB, 2 * XH], F32)
        vT_cb = vT[:].rearrange("p c b s -> p (c b) s")
        cT_cb = cT[:].rearrange("p c b s -> p (c b) s")

        s_t32 = [sem(f"toeplitz_loaded_{r}") for r in range(2)]
        s_thi = sem("toeplitz_hi_ready")
        s_tscaled = sem("toeplitz_scaled")
        s_tlo = sem("toeplitz_lo_ready")
        s_kv = sem("pairs_ready")
        s_kvhi = sem("pairs_hi_ready")
        s_kvlo = sem("pairs_lo_ready")
        s_kvlo_rest = sem("pairs_lo_rest")
        s_y = sem("convolved")
        s_z = sem("weighted_pairs_ready")
        s_sum = sem("summed")
        s_first = sem("first_thirds_step")
        s_pool = sem("partial_sum")
        TLO0, KVLO0, Y0, Z0, SUM0 = 2, 2, 2 * KC, 2 * KC, 2

        with ExitStack() as banks:
            pY = [[banks.enter_context(nc.psum_tensor(f"p_conv{r}{c}", [P, PAIRS], F32)) for c in range(KC)]
                  for r in range(2)]
            with nc.Block() as block:
                @block.sync
                def _(sp):
                    def load(g, r):
                        sp.wait_ge(s_tlo, g - 1 + TLO0)
                        sp.dma_start(t32[:, r, :], toeplitz[bass.ds(g, 1)].rearrange("a p n -> p (a n)")
                                     ).then_inc(s_t32[r], 16)

                    load(0, 0)
                    load(1, 1)
                    weights.load(sp, 0)
                    with sp.Fori(1, XG // 2) as i:
                        for r in range(2):
                            load(i * 2 + r, r)

                @block.tensor
                def _(pe):
                    pe.sem_inc(s_y, Y0)
                    with pe.Fori(0, XG // 2) as i:
                        for r in range(2):
                            g = i * 2 + r
                            pe.wait_ge(s_tlo, g + 1 + TLO0)
                            pe.wait_ge(s_kvlo, g + 1 + KVLO0)
                            pe.wait_ge(s_kvlo_rest, g + 1 + KVLO0)
                            for c in range(KC):
                                pe.wait_ge(s_z, (g - 2) * KC + c + 1 + Z0)
                                n = 0
                                for m in range(c + 1):
                                    block_ = slice((c - m) * P, (c - m + 1) * P)
                                    for w, v_ in ((t_hi, kv_hi), (t_hi, kv_lo), (t_lo, kv_hi)):
                                        last = nc.tensor.matmul(pY[r][c][:], w[:, r, block_], v_[:, r, m, :],
                                                                start=(n == 0), stop=(n == 3 * c + 2))
                                        n += 1
                                last.then_inc(s_y, 1)

                @block.scalar
                def _(act):
                    with act.Fori(0, XG // 2) as i:
                        for r in range(2):
                            g = i * 2 + r
                            act.wait_ge(s_t32[r], (i + 1) * 16)
                            nc.scalar.activation(t32[:, r, :], t32[:, r, :], ACT.Copy, scale=T_SCALE).then_inc(s_tscaled, 1)
                            act.wait_ge(s_y, (g - 1) * KC + Y0)
                            act.wait_ge(s_tscaled, g + 1)
                            nc.scalar.activation(t_hi[:, r, :], t32[:, r, :], ACT.Copy).then_inc(s_thi, 1)
                            act.wait_ge(s_kv, g + 1)
                            nc.scalar.activation(kv_hi[:, r], kv32[:, r], ACT.Copy).then_inc(s_kvhi, 1)

                @block.gpsimd
                def _(pool):
                    for s_, n in ((s_sum, SUM0), (s_tlo, TLO0), (s_kvlo_rest, KVLO0)):
                        pool.sem_inc(s_, n)

                    def low_halves(g, r):
                        pool.wait_ge(s_thi, g + 1)
                        nc.gpsimd.tensor_tensor(t_lo[:, r, :], t32[:, r, :], t_hi[:, r, :], ALU.subtract).then_inc(s_tlo, 1)
                        pool.wait_ge(s_kvhi, g + 1)
                        rest = (slice(None), r, KC - 1, slice(PAIRS - POOL_PAIRS, PAIRS))
                        nc.gpsimd.tensor_tensor(kv_lo[rest], kv32[rest], kv_hi[rest], ALU.subtract).then_inc(s_kvlo_rest, 1)

                    def sums(g, r):
                        zz = z[:, r].rearrange("p c (b n) -> p (c b) n", b=B)
                        pool.wait_ge(s_z, (g + 1) * KC + Z0)
                        nc.gpsimd.tensor_tensor(half1[:], zz[:, :, 0:4 * XH], zz[:, :, 4 * XH:8 * XH],
                                                ALU.add).then_inc(s_pool, 1)
                        pool.wait_ge(s_pool, g * 2 + 1)
                        nc.gpsimd.tensor_tensor(half2[:], half1[:, :, 0:2 * XH], half1[:, :, 2 * XH:4 * XH],
                                                ALU.add).then_inc(s_pool, 1)
                        pool.wait_ge(s_pool, g * 2 + 2)
                        nc.gpsimd.tensor_tensor(vT_cb[:, :, bass.ds(g * XH, XH)], half2[:, :, 0:XH],
                                                half2[:, :, XH:2 * XH], ALU.add).then_inc(s_sum, 1)

                    low_halves(0, 0)
                    low_halves(1, 1)
                    with pool.Fori(0, XG // 2 - 1) as i:
                        for r in range(2):
                            low_halves(i * 2 + r + 2, r)
                            sums(i * 2 + r, r)
                    sums(XG - 2, 0)
                    sums(XG - 1, 1)

                @block.vector
                def _(dve):
                    dve.sem_inc(weights.s_w32, W320)
                    dve.sem_inc(s_kvlo, KVLO0)
                    dve.sem_inc(s_z, Z0)

                    def pairs(g, r):
                        dve.wait_ge(s_kvlo, g - 1 + KVLO0)
                        dve.wait_ge(s_kvlo_rest, g - 1 + KVLO0)
                        v_, c_ = (a[:, :, bass.ds(g * XH, XH)] for a in (vT_cb, cT_cb))
                        nc.vector.tensor_tensor(kv32[:, r].rearrange("p c (b i j) -> p (c b) i j", i=XH, j=XH),
                                                v_.unsqueeze(3).to_broadcast([P, CB, XH, XH]),
                                                c_.unsqueeze(2).to_broadcast([P, CB, XH, XH]), ALU.mult).then_inc(s_kv, 1)

                    def low_halves(g, r):
                        dve.wait_ge(s_kvhi, g + 1)
                        lo, full, hi = (a[:, r].rearrange("p c n -> p (c n)")[:, 0:KC * PAIRS - POOL_PAIRS]
                                        for a in (kv_lo, kv32, kv_hi))
                        nc.vector.tensor_tensor(lo, full, hi, ALU.subtract).then_inc(s_kvlo, 1)

                    def weigh(g, r):
                        dve.wait_ge(s_sum, g - 1 + SUM0)
                        for c in range(KC):
                            dve.wait_ge(s_y, g * KC + c + 1 + Y0)
                            nc.vector.tensor_tensor(
                                z[:, r, c].rearrange("p (b i j) -> p b i j", i=XH, j=XH),
                                pY[r][c][:].rearrange("p (b i j) -> p b i j", i=XH, j=XH),
                                cT[:, c, :, bass.ds(g * XH, XH)].unsqueeze(3).to_broadcast([P, B, XH, XH]),
                                ALU.mult).then_inc(s_z, 1)

                    pairs(0, 0)
                    pairs(1, 1)
                    low_halves(0, 0)
                    with dve.Fori(0, XG // 2 - 1) as i:
                        for r in range(2):
                            pairs(i * 2 + r + 2, r)
                            low_halves(i * 2 + r + 1, (r + 1) % 2)
                            weigh(i * 2 + r, r)
                    low_halves(XG - 1, 1)
                    weigh(XG - 2, 0)
                    written = counted(dve, s_first, 0)
                    for c in range(FIRST_THIRDS):
                        written(weights.bits(dve, 0, c))
                        written(weights.values())
                        weights.scaled(c)
                        if c == 0:
                            weigh(XG - 1, 1)

        s_back = sem("transposed_back")
        s_added = sem("mixing_added")
        s_step = sem("back_dve_step")
        Q = norm.QUARTER
        with ExitStack() as banks:
            pT = [banks.enter_context(nc.psum_tensor(f"p_back{r}", [P, KC, P], F32)) for r in range(4)]
            ident = tab[:, T_ID:T_ID + P]
            with nc.Block() as block:
                tiles = [(b, t) for b in range(B) for t in range(TT)]

                @block.gpsimd
                def _(pool):
                    pool.memset(norm.half[:], -0.5).then_inc(norm.s_rstd, 1)
                    pool.wait_ge(norm.s_rstd, 1)
                    for q in range(2):
                        norm.reciprocals(pool, q)

                @block.tensor
                def _(pe):
                    for n, (b, t) in enumerate(tiles):
                        if n >= len(pT):
                            pe.wait_ge(s_added, n - len(pT) + 1)
                        for c in range(KC):
                            last = nc.tensor.transpose(pT[n % len(pT)][:, c, :], vT[:, c, b, t * P:(t + 1) * P], ident)
                        last.then_inc(s_back, 1)

                @block.scalar
                def _(act):
                    act.wait_ge(norm.s_shift, 1)
                    for n in range(norm.QUARTER):
                        norm.normed(X, n)

                @block.vector
                def _(dve):
                    written = counted(dve, s_step, 0)
                    for n in range(len(tiles)):
                        dve.wait_ge(s_back, n + 1)
                        row = X[:, n, :]
                        nc.vector.scalar_tensor_tensor(out=row, in0=pT[n % len(pT)][:].rearrange("p c l -> p (c l)"),
                                                       scalar=1.0 / (T_SCALE * KV_SCALE), in1=row,
                                                       op0=ALU.mult, op1=ALU.add).then_inc(s_added, 1)
                        if 1 <= n <= 2 * Q:
                            dve.wait_ge(s_added, n)
                            moments = norm.moments(X, n - 1)
                            if n % Q == 0:
                                written(moments)
                                written(norm.means(range(n - Q, n)))
                                norm.variances(n // Q - 1)
                        if n == 2 * Q - 1:
                            norm.shifts(dve, 0)
                        if n == 3 * Q:
                            norm.shifts(dve, 1)


def counted(engine, semaphore, done):
    def written(instruction):
        written.count += 1
        instruction.then_inc(semaphore, 1)
        engine.wait_ge(semaphore, done + written.count)

    written.count = 0
    return written


def feed_forward(nc, X, vT, cT, tab, weights, norm, out):
    GROUPS = UNITS // GU
    HC = 2 * GU
    TB = 4
    TW = B * S // TB
    BT = TW // P
    SLOTS = TB * HC
    W_FACTOR = 2.0 ** 14 * W_SCALE
    GU_OUT = 1.0 / (X_SCALE * W_SCALE)
    ROOT, CUBIC = 0.7978845608028654, 0.044715
    with ExitStack() as st:
        def sb(name, shape, dt):
            return st.enter_context(nc.sbuf_tensor(name, shape, dt))

        def sem(name):
            return st.enter_context(nc.semaphore(name))

        ident = tab[:, T_ID:T_ID + P]
        xT_hi, xT_lo = (cT[:, 2 * a:2 * a + 2].rearrange("p c b s -> p (c b s)").bitcast(F16).rearrange(
            "p (q e t) -> p q e t", q=2, e=2) for a in range(2))
        W_SIZE = 2 * GU * 3 * 2 * D
        w_hi = vT[:].rearrange("p c b s -> p (c b s)").bitcast(F16)[:, 0:W_SIZE].rearrange(
            "p (r u c e n) -> p r u c e n", r=2, u=GU, c=3, e=2)
        w_lo = sb("ff_w_lo", [P, 2, GU, 3, 2, D], F16)
        w32, s_w32 = weights.w32, weights.s_w32
        s_whi = sem("w_hi_ready")
        s_wlo = sem("w_lo_ready")
        s_tr = sem("ff_transposed")
        s_xhi = sem("ff_xT_hi_ready")
        s_xlo = sem("ff_xT_lo_ready")
        s_down = sem("down_done")
        s_step = sem("ff_dve_step")
        DOWN0 = SLOTS

        def decoded_hi(act, g, r, c):
            act.wait_ge(s_w32, g * THIRDS + c + 1 + W320)
            act.wait_ge(s_down, (g - 1) * SLOTS + DOWN0)
            nc.scalar.activation(w_hi[:, r, c // 3, c % 3], w32[:, c % 2], ACT.Copy, scale=W_FACTOR).then_inc(s_whi, 1)

        def decoded_lo(dve, g, r, c):
            dve.wait_ge(s_whi, g * THIRDS + c + 1)
            nc.vector.scalar_tensor_tensor(out=w_lo[:, r, c // 3, c % 3], in0=w32[:, c % 2], scalar=W_FACTOR,
                                           in1=w_hi[:, r, c // 3, c % 3], op0=ALU.mult, op1=ALU.subtract).then_inc(s_wlo, 1)

        cube = sb("ff_cubic", [P, 2, TW], F32)
        arg = sb("ff_tanh_arg", [P, 2, TW], F32)
        th = sb("ff_tanh", [P, 2, TW], F32)
        gated = sb("ff_gated", [P, 2, TW], F32)
        hidden = sb("ff_hidden", [P, 2, TW], F32)
        h_hi, h_lo = (sb(f"ff_hidden_{s}", [P, 2, TW], F16) for s in ("hi", "lo"))
        pG = [st.enter_context(nc.psum_tensor(f"ff_p_gate{r}", [P, TW], F32)) for r in range(2)]
        pU = st.enter_context(nc.psum_tensor("ff_p_up", [P, TW], F32))
        pT = st.enter_context(nc.psum_tensor("ff_p_xT", [P, TW], F32))
        pD = [st.enter_context(nc.psum_tensor(f"ff_p_down{r}", [P, D], F32)) for r in range(BT)]
        s_gate = sem("gate_done")
        s_up = sem("up_done")
        s_sq = sem("square_ready")
        s_arg = sem("tanh_arg_ready")
        s_th = sem("tanh_ready")
        s_h = sem("hidden_ready")
        s_hhi = sem("hidden_hi_ready")
        s_hlo = sem("hidden_lo_ready")
        s_acc = sem("down_added")
        s_out = sem("stored")
        H0, ARG0, ACC0 = 2, 2, 1
        DECODE_AT = {k: c for c, k in enumerate([k for k in range(HC, SLOTS) if k % HC != 0][:THIRDS])}
        DECODE_IN_FIRST = {k: c for c, k in enumerate((5, 7, 8, 11, 13, 14))}
        assert HC == BT == TB == 4 and THIRDS == 6
        OWN_AT = {0: (3, 4), 1: (5,)}
        TILE_BEFORE_DOWN = {1: 5, 2: 7, 4: 8, 5: 10, 8: 12, 9: 14}
        TILE_AFTER_DOWN = {0: 4, 1: 6, 4: 9, 5: 11, 8: 13, 9: 15}
        STEPS = 2 * SLOTS + 2 * THIRDS

        def over_groups(engine, body):
            body(0, 0, True, False)
            with engine.Fori(0, (GROUPS - 2) // 2) as i:
                for r in (1, 0):
                    body(i * 2 + (2 - r), r, False, False)
            body(GROUPS - 1, 1, False, True)

        def tile_bank(n):
            bank = (pT, pU, *pG)[n] if n < BT else pT
            return bank[:].rearrange("p (q e t) -> p (q e) t", q=2, e=2)

        with nc.Block() as block:
            @block.sync
            def _(sp):
                def body(g, r, first, last):
                    if not last:
                        weights.load(sp, g + 1)

                over_groups(sp, body)
                for tb in range(TB):
                    sp.wait_ge(s_acc, ((GROUPS - 1) * TB + tb + 1) * BT + ACC0)
                    sp.dma_start(out.rearrange("b (t p) d -> p (b t) d", p=P)[:, tb * BT:(tb + 1) * BT, :],
                                 X[:, tb * BT:(tb + 1) * BT, :]).then_inc(s_out, 16)
                sp.wait_ge(s_out, 16 * TB)

            @block.gpsimd
            def _(pool):
                for q in range(2, TB):
                    norm.reciprocals(pool, q)

            @block.tensor
            def _(pe):
                pe.sem_inc(s_down, DOWN0)

                def transposes(n):
                    pe.wait_ge(norm.s_xn, n + 1)
                    if n > BT:
                        pe.wait_ge(s_xlo, n)
                    for q in range(2):
                        for e in range(2):
                            last = nc.tensor.transpose(tile_bank(n)[:, 2 * q + e, :],
                                                       norm.xn[:, n % BT, q * 2 * P:(q + 1) * 2 * P].rearrange(
                                                           "p (j e) -> p j e", e=2)[:, :, e], ident)
                    last.then_inc(s_tr, 1)

                def gate_up(g, r, k, first=False):
                    n = g * SLOTS + k
                    tb, hc = k // HC, k % HC
                    tokens = slice(tb * TW, (tb + 1) * TW)
                    if first:
                        if hc == 0:
                            pe.wait_ge(s_xlo, BT * (tb + 1))
                        if tb == 0 and hc % 2 == 0:
                            pe.wait_ge(s_wlo, 3 * (hc // 2) + 2)
                    elif k == 0:
                        pe.wait_ge(s_wlo, (g + 1) * THIRDS)
                    for third, bank, done in ((0, pG[k % 2], s_gate), (1, pU, s_up)):
                        pe.wait_ge(s_h, n - 1 + third + H0)
                        m = 0
                        for q in range(2):
                            for e in range(2):
                                cols = slice(q * 2 * P + hc % 2 * P, q * 2 * P + hc % 2 * P + P)
                                for w, x_ in ((w_hi, xT_hi), (w_hi, xT_lo), (w_lo, xT_hi)):
                                    last = nc.tensor.matmul(bank[:], w[:, r, hc // 2, third, e, cols], x_[:, q, e, tokens],
                                                            start=(m == 0), stop=(m == 11))
                                    m += 1
                        last.then_inc(done, 1)

                def down(g, r, k, first):
                    n = g * SLOTS + k
                    tb, hc = k // HC, k % HC
                    if first and tb == 0 and hc % 2 == 0:
                        pe.wait_ge(s_wlo, 3 * (hc // 2) + 3)
                    pe.wait_ge(s_hlo, n + 1)
                    if hc == 0:
                        pe.wait_ge(s_acc, (g * TB + tb) * BT + ACC0)
                    for t in range(BT):
                        tile = slice(t * P, (t + 1) * P)
                        for m, (h_, w) in enumerate(((h_hi, w_hi), (h_hi, w_lo), (h_lo, w_hi))):
                            last = nc.tensor.matmul(pD[t][:], h_[:, k % 2, tile], w[:, r, hc // 2, 2, hc % 2, :],
                                                    start=(hc == 0 and m == 0), stop=(hc == HC - 1 and m == 2))
                    last.then_inc(s_down, 1)

                for n in range(BT):
                    transposes(n)
                gate_up(0, 0, 0, True)

                def body(g, r, first, last):
                    for k in range(SLOTS):
                        if k + 1 < SLOTS:
                            gate_up(g, r, k + 1, first)
                        elif not last:
                            gate_up(g + 1, 1 - r, 0)
                        if first and k in TILE_BEFORE_DOWN:
                            transposes(TILE_BEFORE_DOWN[k])
                        down(g, r, k, first)
                        if first and k in TILE_AFTER_DOWN:
                            transposes(TILE_AFTER_DOWN[k])

                over_groups(pe, body)

            @block.scalar
            def _(act):
                def tile_high(n):
                    act.wait_ge(s_tr, n + 1)
                    nc.scalar.activation(xT_hi[:, :, :, n * P:(n + 1) * P].rearrange("p q e t -> p (q e) t"),
                                         tile_bank(n), ACT.Copy, scale=X_SCALE).then_inc(s_xhi, 1)

                def normed_block(q):
                    act.wait_ge(norm.s_shift, q + 1)
                    for n in range(BT * q, BT * (q + 1)):
                        act.wait_ge(s_tr, n - BT + 1)
                        norm.normed(X, n)

                for c in range(FIRST_THIRDS):
                    decoded_hi(act, 0, 0, c)
                for n in range(BT):
                    tile_high(n)
                normed_block(1)
                decoded_hi(act, 0, 0, FIRST_THIRDS)

                def body(g, r, first, last):
                    decode_at = DECODE_IN_FIRST if first else {} if last else DECODE_AT
                    for k in range(SLOTS):
                        n = g * SLOTS + k
                        s_ = k % 2
                        act.wait_ge(s_gate, n + 1)
                        act.wait_ge(s_arg, n - 1 + ARG0)
                        nc.scalar.activation(cube[:, s_], pG[s_][:], ACT.Square, scale=GU_OUT).then_inc(s_sq, 1)
                        if k - 1 in decode_at:
                            decoded_hi(act, g + 1, 1 - r, decode_at[k - 1])
                        act.wait_ge(s_arg, n + 1 + ARG0)
                        act.wait_ge(s_h, n - 1 + H0)
                        nc.scalar.activation(th[:, s_], arg[:, s_], ACT.Tanh).then_inc(s_th, 1)
                        act.wait_ge(s_h, n + 1 + H0)
                        act.wait_ge(s_down, n - 1 + DOWN0)
                        nc.scalar.activation(h_hi[:, s_], hidden[:, s_], ACT.Copy).then_inc(s_hhi, 1)
                        if not first:
                            continue
                        if k - 1 in TILE_BEFORE_DOWN:
                            tile_high(TILE_BEFORE_DOWN[k - 1])
                        for c in OWN_AT.get(k, ()):
                            decoded_hi(act, 0, 0, c)
                        if k - 1 in TILE_AFTER_DOWN:
                            tile_high(TILE_AFTER_DOWN[k - 1])
                        if k % HC == HC - 1 and k // HC + 2 < TB:
                            normed_block(k // HC + 2)

                over_groups(act, body)

            @block.vector
            def _(dve):
                for s_, n in ((s_h, H0), (s_arg, ARG0), (s_acc, ACC0)):
                    dve.sem_inc(s_, n)

                def add_block(g, tb):
                    dve.wait_ge(s_down, g * SLOTS + (tb + 1) * HC + DOWN0)
                    for t in range(BT):
                        row = X[:, tb * BT + t, :]
                        nc.vector.scalar_tensor_tensor(out=row, in0=pD[t][:], scalar=1.0 / (W_SCALE * HIDDEN_SCALE), in1=row,
                                                       op0=ALU.mult, op1=ALU.add).then_inc(s_acc, 1)

                def tile_low(n):
                    dve.wait_ge(s_xhi, n + 1)
                    to = (slice(None), slice(None), slice(None), slice(n * P, (n + 1) * P))
                    nc.vector.scalar_tensor_tensor(out=xT_lo[to].rearrange("p q e t -> p (q e) t"),
                                                   in0=tile_bank(n), scalar=X_SCALE,
                                                   in1=xT_hi[to].rearrange("p q e t -> p (q e) t"),
                                                   op0=ALU.mult, op1=ALU.subtract).then_inc(s_xlo, 1)

                def own_third(written, c):
                    written(weights.bits(dve, 0, c))
                    written(weights.values())
                    weights.scaled(c)

                def hidden_values(n, s_, written, third=None, previous=None):
                    dve.wait_ge(s_sq, n + 1)
                    written(nc.vector.tensor_scalar(cube[:, s_], cube[:, s_], CUBIC * ROOT, ROOT, ALU.mult, ALU.add))
                    nc.vector.scalar_tensor_tensor(out=arg[:, s_], in0=pG[s_][:], scalar=GU_OUT, in1=cube[:, s_],
                                                   op0=ALU.mult, op1=ALU.mult).then_inc(s_arg, 1)
                    if third:
                        written(weights.bits(dve, third[0], third[2]))
                    dve.wait_ge(s_th, n + 1)
                    written(nc.vector.scalar_tensor_tensor(out=gated[:, s_], in0=th[:, s_], scalar=1.0, in1=pG[s_][:],
                                                           op0=ALU.add, op1=ALU.mult))
                    dve.wait_ge(s_up, n + 1)
                    nc.vector.scalar_tensor_tensor(out=hidden[:, s_], in0=pU[:], scalar=0.5 * GU_OUT ** 2 * HIDDEN_SCALE,
                                                   in1=gated[:, s_], op0=ALU.mult, op1=ALU.mult).then_inc(s_h, 1)
                    if third:
                        written(weights.values())
                    dve.wait_ge(s_hhi, n + 1)
                    nc.vector.tensor_tensor(h_lo[:, s_], hidden[:, s_], h_hi[:, s_], ALU.subtract).then_inc(s_hlo, 1)
                    if third:
                        weights.scaled(third[2])
                    if previous:
                        decoded_lo(dve, *previous)

                for c in range(FIRST_THIRDS):
                    decoded_lo(dve, 0, 0, c)
                for n in range(BT):
                    tile_low(n)
                written = counted(dve, s_step, 0)
                own_third(written, FIRST_THIRDS)
                decoded_lo(dve, 0, 0, FIRST_THIRDS)

                def first_group(k):
                    if k - 1 in TILE_BEFORE_DOWN:
                        tile_low(TILE_BEFORE_DOWN[k - 1])
                    own = OWN_AT.get(k, ())
                    for c in own:
                        own_third(written, c)
                        if c > own[0]:
                            decoded_lo(dve, 0, 0, c - 1)
                    if own:
                        decoded_lo(dve, 0, 0, own[-1])
                    if k - 1 in TILE_AFTER_DOWN:
                        tile_low(TILE_AFTER_DOWN[k - 1])
                    q = k // HC + 2
                    if q < TB and k % HC == HC - 2:
                        block_ = range(BT * q, BT * (q + 1))
                        for n in block_:
                            last = norm.moments(X, n)
                        written(last)
                        written(norm.means(block_))
                        norm.variances(q)
                    if q < TB and k % HC == HC - 1:
                        norm.shifts(dve, q)

                hidden_values(0, 0, written)
                first_group(0)

                def body(g, r, first, last):
                    decode_at = DECODE_IN_FIRST if first else {} if last else DECODE_AT
                    step = written if first else counted(dve, s_step, (g - 1) * STEPS + written.count)
                    for k in range(1, SLOTS if last else SLOTS + 1):
                        third, previous = ((g + 1, 1 - r, decode_at[at]) if at in decode_at else None for at in (k, k - 1))
                        hidden_values(g * SLOTS + k, k % 2, step, third, previous)
                        if first and k < SLOTS:
                            first_group(k)
                        if k % HC == 0:
                            add_block(g, k // HC - 1)
                    if last:
                        add_block(g, TB - 1)

                over_groups(dve, body)


def kernel(x, fside_S2_0, ctx_2048, L0_attn_W_c, L0_attn_b_c, L0_attn_W_d, L0_attn_b_d, L0_attn_W_o, L0_attn_b_o,
           L0_xattn_k, L0_ffn_gate_W_packed, L0_ffn_gate_scales, L0_ffn_up_W_packed, L0_ffn_up_scales,
           L0_ffn_down_W_packed, L0_ffn_down_scales):
    import numpy as np
    import concourse.bacc as bacc
    from concourse.bass_utils import run_bass_kernel_spmd

    rot = 2 * DH
    freq = (1.0 / 10000.0 ** (np.arange(0, rot, 2, dtype=np.float32) / np.float32(rot))).astype(np.float32)
    ang = (np.arange(S, dtype=np.float32)[None, :] * freq[:, None]).astype(np.float32)
    tables = np.zeros((P, T_COLS), np.float32)
    tables[:, T_COS:T_COS + S] = 1.0
    tables[0:DH, T_COS:T_COS + S] = np.cos(ang)
    tables[DH:rot, T_COS:T_COS + S] = np.cos(ang)
    tables[0:DH, T_SIN:T_SIN + S] = -np.sin(ang)
    tables[DH:rot, T_SIN:T_SIN + S] = np.sin(ang)
    tables[:, T_ID:T_ID + P] = np.eye(P)
    tables[:, T_GROUP:T_GROUP + P] = np.kron(np.eye(P // XH), np.ones((XH, XH)))
    tables[:, T_QMASK] = -(np.arange(P) // DH // 2)
    tables[:, T_KMASK] = -(np.arange(P) // DH % 2)

    def units(gate, up, down, per):
        g, u = (np.asarray(a).reshape(MLP // (2 * P), P, 2, 2, per).transpose(0, 4, 3, 2, 1) for a in (gate, up))
        d = np.asarray(down).T.reshape(MLP // (2 * P), per, D)
        g, u = (a.reshape(MLP // (2 * P), per, 2 * 2 * P) for a in (g, u))
        return np.ascontiguousarray(np.stack([g, u, d], axis=2))

    k = np.asarray(L0_xattn_k)
    padded = np.concatenate([np.zeros((XG, P - 1), k.dtype), k], axis=1)
    at = np.arange(D)[None, :] - np.arange(P)[:, None] + P - 1
    arrays = {
        "x": x, "ctx_natural_in": ctx_2048,
        "ctx_t": np.ascontiguousarray(np.asarray(ctx_2048).transpose(2, 0, 1)),
        "tables": tables,
        "wc": L0_attn_W_c, "bc": L0_attn_b_c, "wd": L0_attn_W_d,
        "bqk": np.ascontiguousarray(np.asarray(L0_attn_b_d)[:2 * D].reshape(2 * NH, DH).T),
        "bv": np.asarray(L0_attn_b_d)[2 * D:], "wo": L0_attn_W_o, "bo": L0_attn_b_o,
        "skip": np.asarray(fside_S2_0).reshape(TT, P).T,
        "toeplitz": np.ascontiguousarray(padded[:, at]),
        "packed": units(L0_ffn_gate_W_packed, L0_ffn_up_W_packed, L0_ffn_down_W_packed, P),
        "scales": units(L0_ffn_gate_scales, L0_ffn_up_scales, L0_ffn_down_scales, XH),
    }
    nc = bacc.Bacc("TRN2", target_bir_lowering=False, num_devices=1)
    arrays = {n: np.ascontiguousarray(a) for n, a in arrays.items()}
    args = [nc.dram_tensor(n, a.shape, mybir.dt.from_np(a.dtype), kind="ExternalInput").ap() for n, a in arrays.items()]
    out = nc.dram_tensor("out", (B, S, D), F32, kind="ExternalOutput").ap()
    program(nc, *args, out)
    r = run_bass_kernel_spmd(nc, [arrays], core_ids=[0])
    return r.results[0]["out"]
```
